# Optimizing a Trainium2 kernel written in Bass

```python
import numpy as np
import jax
import jax.numpy as jnp

def _softmax(x, axis=-1):
    return jax.nn.softmax(x, axis=axis)

def _gelu(x):
    return jax.nn.gelu(x, approximate=True)

def _silu(x):
    return jax.nn.silu(x)

def _sigmoid(x):
    return jax.nn.sigmoid(x)

def _layernorm(x, axis=-1, eps=1e-05):
    m = jnp.mean(x, axis=axis, keepdims=True)
    v = jnp.var(x, axis=axis, keepdims=True)
    return (x - m) / jnp.sqrt(v + eps)

def _scatter_add(tgt, idx, src, axis=0):
    return tgt.at[idx].add(src)

def _segment_sum(src, seg, n):
    return jax.ops.segment_sum(src, seg, n)
kernel_name = 'mk_adaln_d1_jaxref_r8_caf71c'

def setup_inputs(seed: int=0):
    np.random.seed(seed)
    _w = jnp.asarray

    def _L0_attn_setup():
        import jax, jax.numpy as jnp
        import numpy as np
        DIM = 256
        HEADS = 16
        HEAD_DIM = DIM // HEADS
        CHUNK = 128
        B, N = (4, 256)

        def _rmsnorm(x, w, eps):
            return x * jax.lax.rsqrt(jnp.mean(x * x, axis=-1, keepdims=True) + eps) * w

        def _weight_quant(w):
            scale = 1.0 / jnp.clip(jnp.mean(jnp.abs(w)), 1e-05, None)
            q = jnp.clip(jnp.round(w * scale), -1.0, 1.0) / scale
            return w + jax.lax.stop_gradient(q - w)

        def _forward(x, qkv_w, qkv_norm_w, proj_w, proj_norm_w, norm_w, s):
            Bb, Nn, C = x.shape
            H, D, T = (HEADS, HEAD_DIM, CHUNK)
            nc = Nn // T
            eps = jnp.finfo(x.dtype).eps
            scale = D ** (-0.5)
            h = _rmsnorm(x, qkv_norm_w, eps)
            qkv = h @ _weight_quant(qkv_w).T
            qkv = qkv.reshape(Bb, Nn, 3, H, D)
            q, k, v = (qkv[:, :, 0], qkv[:, :, 1], qkv[:, :, 2])

            def chunks(t):
                return t.reshape(Bb, nc, T, H, D).transpose(1, 0, 3, 2, 4)
            qc, kc, vc = (chunks(q), chunks(k), chunks(v))
            tt = jnp.arange(T, dtype=x.dtype)
            lam_t = jnp.exp(-s[:, None] * tt)
            lam_rev = jnp.exp(-s[:, None] * (T - tt))
            diff = tt[:, None] - tt[None, :]
            mask = jnp.where(diff >= 0, jnp.exp(-s[:, None, None] * diff), 0.0)
            lam_T = jnp.exp(-s * T)[:, None, None]

            def step(S, qkv_c):
                qi, ki, vi = qkv_c
                scores = jnp.einsum('bhtd,bhsd,hts->bhts', qi, ki, mask)
                intra = jnp.einsum('bhts,bhsd->bhtd', scores, vi)
                cross = jnp.einsum('bhtd,ht,bhde->bhte', qi, lam_t, S)
                o = scale * (intra + cross)
                kv = jnp.einsum('bhtd,ht,bhte->bhde', ki, lam_rev, vi)
                return (lam_T * S + kv, o)
            S0 = jnp.zeros((Bb, H, D, D), x.dtype)
            _, outs = jax.lax.scan(step, S0, (qc, kc, vc))
            out = outs.transpose(1, 0, 3, 2, 4).reshape(Bb, Nn, C)
            out = _rmsnorm(out, norm_w, 1e-06)
            out = _rmsnorm(out, proj_norm_w, eps) @ _weight_quant(proj_w).T
            return out
        key = jax.random.key(seed)
        ks = jax.random.split(key, 3)
        x = jax.random.normal(ks[0], (B, N, DIM), jnp.float32)
        bound = float(1.0 / np.sqrt(DIM))
        qkv_w = jax.random.uniform(ks[1], (3 * DIM, DIM), jnp.float32, -bound, bound)
        proj_w = jax.random.uniform(ks[2], (DIM, DIM), jnp.float32, -bound, bound)
        return {'x': x, 'qkv_w': qkv_w, 'qkv_norm_w': jnp.ones((DIM,), jnp.float32), 'proj_w': proj_w, 'proj_norm_w': jnp.ones((DIM,), jnp.float32), 'norm_w': jnp.ones((DIM,), jnp.float32), 's': jnp.full((HEADS,), 0.02, jnp.float32)}
    _L0_attn_in = _L0_attn_setup()

    def _L0_ffn_setup():
        import jax, jax.numpy as jnp
        import numpy as np
        E, K, H, F = (64, 6, 256, 96)
        G, KG = (8, 4)
        SHARED_F = 96
        SCALE = 2.5
        T = 2 * 128
        CAP = 2 * (T * K // E)

        def _grouped_topk(logits, bias):
            scores = jax.nn.sigmoid(logits.astype(jnp.float32))
            scores_b = scores + bias[None, :]
            gs = scores_b.reshape(-1, G, E // G)
            group_scores = jnp.sum(jax.lax.top_k(gs, 2)[0], axis=-1)
            gidx = jax.lax.top_k(group_scores, KG)[1]
            rows = jnp.arange(group_scores.shape[0])[:, None]
            group_mask = jnp.zeros_like(group_scores).at[rows, gidx].set(1.0)
            score_mask = jnp.repeat(group_mask, E // G, axis=-1) > 0
            tmp = jnp.where(score_mask, scores_b, -jnp.inf)
            topk_ids = jax.lax.top_k(tmp, K)[1]
            topk_w = jnp.take_along_axis(scores, topk_ids, axis=-1)
            topk_w = topk_w / jnp.sum(topk_w, axis=-1, keepdims=True)
            return (topk_w * SCALE, topk_ids)

        def _routed_moe(x, topk_w, topk_ids, w_gate, w_up, w_down):
            Tn = x.shape[0]
            flat_e = topk_ids.reshape(-1)
            order = jnp.argsort(flat_e)
            se = flat_e[order]
            pos = jnp.arange(Tn * K) - jnp.searchsorted(se, se, side='left')
            tok = order // K
            valid = pos < CAP
            slot = jnp.where(valid, pos, CAP)
            buf = jnp.zeros((E, CAP + 1, H), x.dtype).at[se, slot].set(x[tok])[:, :CAP]
            h = jax.nn.silu(jnp.einsum('ech,ehf->ecf', buf, w_gate)) * jnp.einsum('ech,ehf->ecf', buf, w_up)
            out = jnp.einsum('ecf,efh->ech', h, w_down)
            gathered = out[se, jnp.minimum(pos, CAP - 1)] * valid.astype(x.dtype)[:, None]
            w = topk_w.reshape(-1)[order].astype(x.dtype)[:, None]
            return jax.ops.segment_sum(gathered * w, tok, num_segments=Tn)
        key = jax.random.key(seed)
        ks = jax.random.split(key, 9)
        s = 0.02
        return dict(hidden_states=jax.random.normal(ks[0], (2, 128, H), jnp.float32), gate_w=jax.random.normal(ks[1], (H, E), jnp.float32) * s, bias=jax.random.normal(ks[2], (E,), jnp.float32) * s, w_gate=jax.random.normal(ks[3], (E, H, F), jnp.float32) * s, w_up=jax.random.normal(ks[4], (E, H, F), jnp.float32) * s, w_down=jax.random.normal(ks[5], (E, F, H), jnp.float32) * s, ws_gate=jax.random.normal(ks[6], (H, SHARED_F), jnp.float32) * s, ws_up=jax.random.normal(ks[7], (H, SHARED_F), jnp.float32) * s, ws_down=jax.random.normal(ks[8], (SHARED_F, H), jnp.float32) * s)
    _L0_ffn_in = _L0_ffn_setup()
    _L0_c = _w((lambda *s: np.random.randn(*s).astype(np.float32) * 0.05)(8, 256))
    _L0_wmod = _w((lambda *s: np.random.randn(*s).astype(np.float32) * 0.05)(256, 6 * 256) * 256 ** (-0.5))
    _d = {'L0_attn_x': _L0_attn_in['x'], 'L0_attn_qkv_w': _L0_attn_in['qkv_w'], 'L0_attn_qkv_norm_w': _L0_attn_in['qkv_norm_w'], 'L0_attn_proj_w': _L0_attn_in['proj_w'], 'L0_attn_proj_norm_w': _L0_attn_in['proj_norm_w'], 'L0_attn_norm_w': _L0_attn_in['norm_w'], 'L0_attn_s': _L0_attn_in['s'], 'L0_ffn_gate_w': _L0_ffn_in['gate_w'], 'L0_ffn_bias': _L0_ffn_in['bias'], 'L0_ffn_w_gate': _L0_ffn_in['w_gate'], 'L0_ffn_w_up': _L0_ffn_in['w_up'], 'L0_ffn_w_down': _L0_ffn_in['w_down'], 'L0_ffn_ws_gate': _L0_ffn_in['ws_gate'], 'L0_ffn_ws_up': _L0_ffn_in['ws_up'], 'L0_ffn_ws_down': _L0_ffn_in['ws_down'], 'L0_c': _L0_c, 'L0_wmod': _L0_wmod}
    _x0 = _d['L0_attn_x']
    _d['L0_attn_x'] = jax.random.normal(jax.random.fold_in(jax.random.key(seed), 1), (8, 256, 256), dtype=_x0.dtype)
    del _x0
    return _d

def reference(L0_attn_x, L0_attn_qkv_w, L0_attn_qkv_norm_w, L0_attn_proj_w, L0_attn_proj_norm_w, L0_attn_norm_w, L0_attn_s, L0_ffn_gate_w, L0_ffn_bias, L0_ffn_w_gate, L0_ffn_w_up, L0_ffn_w_down, L0_ffn_ws_gate, L0_ffn_ws_up, L0_ffn_ws_down, L0_c, L0_wmod):

    def _L0_attn_ref(x, qkv_w, qkv_norm_w, proj_w, proj_norm_w, norm_w, s):
        import jax, jax.numpy as jnp
        import numpy as np
        DIM = 256
        HEADS = 16
        HEAD_DIM = DIM // HEADS
        CHUNK = 128
        B, N = (4, 256)

        def _rmsnorm(x, w, eps):
            return x * jax.lax.rsqrt(jnp.mean(x * x, axis=-1, keepdims=True) + eps) * w

        def _weight_quant(w):
            scale = 1.0 / jnp.clip(jnp.mean(jnp.abs(w)), 1e-05, None)
            q = jnp.clip(jnp.round(w * scale), -1.0, 1.0) / scale
            return w + jax.lax.stop_gradient(q - w)

        def _forward(x, qkv_w, qkv_norm_w, proj_w, proj_norm_w, norm_w, s):
            Bb, Nn, C = x.shape
            H, D, T = (HEADS, HEAD_DIM, CHUNK)
            nc = Nn // T
            eps = jnp.finfo(x.dtype).eps
            scale = D ** (-0.5)
            h = _rmsnorm(x, qkv_norm_w, eps)
            qkv = h @ _weight_quant(qkv_w).T
            qkv = qkv.reshape(Bb, Nn, 3, H, D)
            q, k, v = (qkv[:, :, 0], qkv[:, :, 1], qkv[:, :, 2])

            def chunks(t):
                return t.reshape(Bb, nc, T, H, D).transpose(1, 0, 3, 2, 4)
            qc, kc, vc = (chunks(q), chunks(k), chunks(v))
            tt = jnp.arange(T, dtype=x.dtype)
            lam_t = jnp.exp(-s[:, None] * tt)
            lam_rev = jnp.exp(-s[:, None] * (T - tt))
            diff = tt[:, None] - tt[None, :]
            mask = jnp.where(diff >= 0, jnp.exp(-s[:, None, None] * diff), 0.0)
            lam_T = jnp.exp(-s * T)[:, None, None]

            def step(S, qkv_c):
                qi, ki, vi = qkv_c
                scores = jnp.einsum('bhtd,bhsd,hts->bhts', qi, ki, mask)
                intra = jnp.einsum('bhts,bhsd->bhtd', scores, vi)
                cross = jnp.einsum('bhtd,ht,bhde->bhte', qi, lam_t, S)
                o = scale * (intra + cross)
                kv = jnp.einsum('bhtd,ht,bhte->bhde', ki, lam_rev, vi)
                return (lam_T * S + kv, o)
            S0 = jnp.zeros((Bb, H, D, D), x.dtype)
            _, outs = jax.lax.scan(step, S0, (qc, kc, vc))
            out = outs.transpose(1, 0, 3, 2, 4).reshape(Bb, Nn, C)
            out = _rmsnorm(out, norm_w, 1e-06)
            out = _rmsnorm(out, proj_norm_w, eps) @ _weight_quant(proj_w).T
            return out
        return _forward(x, qkv_w, qkv_norm_w, proj_w, proj_norm_w, norm_w, s)

    def _L0_ffn_ref(hidden_states, gate_w, bias, w_gate, w_up, w_down, ws_gate, ws_up, ws_down):
        import jax, jax.numpy as jnp
        import numpy as np
        E, K, H, F = (64, 6, 256, 96)
        G, KG = (8, 4)
        SHARED_F = 96
        SCALE = 2.5
        T = 2 * 128
        CAP = 2 * (T * K // E)

        def _grouped_topk(logits, bias):
            scores = jax.nn.sigmoid(logits.astype(jnp.float32))
            scores_b = scores + bias[None, :]
            gs = scores_b.reshape(-1, G, E // G)
            group_scores = jnp.sum(jax.lax.top_k(gs, 2)[0], axis=-1)
            gidx = jax.lax.top_k(group_scores, KG)[1]
            rows = jnp.arange(group_scores.shape[0])[:, None]
            group_mask = jnp.zeros_like(group_scores).at[rows, gidx].set(1.0)
            score_mask = jnp.repeat(group_mask, E // G, axis=-1) > 0
            tmp = jnp.where(score_mask, scores_b, -jnp.inf)
            topk_ids = jax.lax.top_k(tmp, K)[1]
            topk_w = jnp.take_along_axis(scores, topk_ids, axis=-1)
            topk_w = topk_w / jnp.sum(topk_w, axis=-1, keepdims=True)
            return (topk_w * SCALE, topk_ids)

        def _routed_moe(x, topk_w, topk_ids, w_gate, w_up, w_down):
            Tn = x.shape[0]
            flat_e = topk_ids.reshape(-1)
            order = jnp.argsort(flat_e)
            se = flat_e[order]
            pos = jnp.arange(Tn * K) - jnp.searchsorted(se, se, side='left')
            tok = order // K
            valid = pos < CAP
            slot = jnp.where(valid, pos, CAP)
            buf = jnp.zeros((E, CAP + 1, H), x.dtype).at[se, slot].set(x[tok])[:, :CAP]
            h = jax.nn.silu(jnp.einsum('ech,ehf->ecf', buf, w_gate)) * jnp.einsum('ech,ehf->ecf', buf, w_up)
            out = jnp.einsum('ecf,efh->ech', h, w_down)
            gathered = out[se, jnp.minimum(pos, CAP - 1)] * valid.astype(x.dtype)[:, None]
            w = topk_w.reshape(-1)[order].astype(x.dtype)[:, None]
            return jax.ops.segment_sum(gathered * w, tok, num_segments=Tn)
        orig_shape = hidden_states.shape
        x = hidden_states.reshape(-1, H)
        router_logits = x @ gate_w
        topk_w, topk_ids = _grouped_topk(router_logits, bias)
        y = _routed_moe(x, topk_w, topk_ids, w_gate, w_up, w_down)
        shared = jax.nn.silu(x @ ws_gate) * (x @ ws_up) @ ws_down
        return (y + shared).reshape(orig_shape)
    x = L0_attn_x
    mod = (_silu(L0_c) @ L0_wmod).reshape(L0_c.shape[0], 6, 1, -1)
    sa, ca, ga, sb, cb, gb = (mod[:, 0], mod[:, 1], mod[:, 2], mod[:, 3], mod[:, 4], mod[:, 5])
    ga = (2 * (ga >= 0) - 1) * jnp.maximum(jnp.abs(ga), 0.25)
    gb = (2 * (gb >= 0) - 1) * jnp.maximum(jnp.abs(gb), 0.25)
    h = _layernorm(x, axis=-1) * (1 + ca) + sa
    x = x + ga * _L0_attn_ref(h, L0_attn_qkv_w, L0_attn_qkv_norm_w, L0_attn_proj_w, L0_attn_proj_norm_w, L0_attn_norm_w, L0_attn_s)
    h = _layernorm(x, axis=-1) * (1 + cb) + sb
    x = x + gb * _L0_ffn_ref(h, L0_ffn_gate_w, L0_ffn_bias, L0_ffn_w_gate, L0_ffn_w_up, L0_ffn_w_down, L0_ffn_ws_gate, L0_ffn_ws_up, L0_ffn_ws_down)
    return x

_drawn_inputs = setup_inputs


def setup_inputs(seed=0):
    import zlib

    import numpy as np

    out = dict(_drawn_inputs(seed))
    spreads = {'L0_attn_qkv_norm_w': (1.0, 0.2),
     'L0_attn_proj_norm_w': (1.0, 0.6),
     'L0_attn_norm_w': (1.0, 0.6),
     'L0_attn_s': (0.019999999552965164, 0.6)}
    factors = {'L0_ffn_gate_w': 8.0,
     'L0_ffn_bias': 8.0,
     'L0_ffn_w_gate': 8.0,
     'L0_ffn_w_up': 8.0,
     'L0_ffn_w_down': 8.0,
     'L0_ffn_ws_gate': 8.0,
     'L0_ffn_ws_up': 8.0,
     'L0_ffn_ws_down': 8.0}
    for name, (base, spread) in spreads.items():
        noise = np.random.default_rng([zlib.crc32(name.encode()), seed]).standard_normal(out[name].shape)
        drawn = base * np.exp(spread * noise) if base else spread * noise
        out[name] = jnp.asarray(drawn.astype(out[name].dtype))
    for name, factor in factors.items():
        out[name] = (out[name] * factor).astype(out[name].dtype)
    return out
```

```python
from contextlib import ExitStack

import concourse.bass as bass
from concourse import mybir

ALU = mybir.AluOpType
ACT = mybir.ActivationFunctionType
F32 = mybir.dt.float32
BF16 = mybir.dt.bfloat16
U32 = mybir.dt.uint32
AX_X = mybir.AxisListType.X
RADD = bass.bass_isa.ReduceOp.add

P = 128
B, N, C = 8, 256, 256
HEADS, HD = 16, 16
T = 128
NT = N // T
KC = C // P
HPJ = HEADS // KC
E, TOPK, F = 64, 6, 96
G, KG = 8, 4
EG = E // G
CAP = 2 * (256 * TOPK // E)
SLOTS = 64
ROWS = E * SLOTS
ROWW = C + E
PAIRS = E // 2
RING = 10
NBUF = 2
EPS_F = 1.1920928955078125e-07
EPS_LN = 1e-5
EPS_O = 1e-6
ROUTE_SCALE = 2.5
MAGIC = 12582912.0
ROUTE_STEPS = 17
OUT = -1.0e30
PICK = -2.0e30


def spread(ap, at, n):
    dims = [list(d) for d in ap.ap]
    dims.insert(at, [0, n])
    return bass.AP(ap.tensor, ap.offset, dims)


def seen(eng, sem, count):
    if isinstance(count, int) and count <= 0:
        return
    eng.wait_ge(sem, count)


def adaln_attention_moe(nc, x, qkv_w, qkv_norm_w, proj_w, proj_norm_w, norm_w, s, gate_w, bias,
                        w_gate, w_up, w_down, ws_gate, ws_up, ws_down, c, wmod, out):
    with ExitStack() as ctx:
        def sb(name, shape, dt=F32):
            return ctx.enter_context(nc.sbuf_tensor(name, shape, dt))

        def sem(name):
            return ctx.enter_context(nc.semaphore(name))

        rows_dram = nc.dram_tensor("rows_dram", [ROWS, ROWW], F32, kind="Internal").ap()
        eout_dram = nc.dram_tensor("eout_dram", [ROWS, C], F32, kind="Internal").ap()
        mod_dram = nc.dram_tensor("mod_dram", [B, 4 * C], F32, kind="Internal").ap()

        ident = sb("ident", [P, P])
        upper = sb("upper", [P, P], BF16)
        ones_bf = sb("ones_bf", [P, P], BF16)
        half_exp = sb("half_exp", [P, 2, 2])
        diff = sb("diff", [P, T])
        t_left = sb("t_left", [P, 1])
        part_ix = sb("part_ix", [P, 1], U32)
        part_bit = sb("part_bit", [P, 1], U32)
        zero_row = sb("zero_row", [P, C])
        trow = sb("trow", [P, T])
        decay = sb("decay", [P, 4, KC, 2, T])
        s_row = sb("s_row", [P, HEADS])
        s_part = sb("s_part", [P, KC])
        neg_s = sb("neg_s", [P, HEADS])
        neg_s_part = sb("neg_s_part", [P, KC])
        lam_q = sb("lam_q", [P, KC, T])
        lam_rev = sb("lam_rev", [P, HEADS])
        even_odd = sb("even_odd", [P, 2])
        head_block = sb("head_block", [P, P])
        w_qkv = sb("w_qkv", [P, KC, 3 * C])
        w_proj = sb("w_proj", [P, KC, C])
        norm_cols = sb("norm_cols", [P, 3, KC])
        q_scale = sb("q_scale", [P, 2, KC])
        stat_w = sb("stat_w", [P, KC, 2])
        gate_sb = sb("gate_sb", [P, KC, E])
        ws_gu = sb("ws_gu", [P, KC, 2, F])
        ws_d = sb("ws_d", [F, C])
        bias_row = sb("bias_row", [P, E])
        row_base = sb("row_base", [P, E])
        mod_cols = sb("mod_cols", [P, 4, B])
        abs_sum = sb("abs_sum", [P, 2])
        abs_all = sb("abs_all", [P, 2])
        w_mean = sb("w_mean", [P, 2])
        w_inv = sb("w_inv", [P, 2])
        c_sb = sb("c_sb", [B, C])
        c_sig = sb("c_sig", [B, C])
        c_cols = sb("c_cols", [P, KC, B])
        mod_rows = sb("mod_rows", [B, 4 * C])
        sign_rows = sb("sign_rows", [B, 2, C])
        abs_rows = sb("abs_rows", [B, 2, C])

        xa = sb("xa", [P, NT, C])
        xres = sb("xres", [P, NT, C])
        mod_b = [sb(f"mod_b{i}", [P, 3, C]) for i in range(2)]
        gb_all = sb("gb_all", [P, B, C])
        mod_cur = [sb(f"mod_cur{i}", [P, 4]) for i in range(2)]
        bn1 = sb("bn1", [P, NT, 6])
        mv1 = sb("mv1", [P, NT, 2])
        ve1 = sb("ve1", [P, NT])
        rstd1 = sb("rstd1", [P, NT])
        z1 = sb("z1", [P, NT, C])
        hT = sb("hT", [P, KC, N])
        hsq = sb("hsq", [P, KC, N])
        rr_t = sb("rr_t", [P, NT])
        rr2 = sb("rr2", [P, NT])
        a16 = [sb(f"a16_{i}", [P, NT]) for i in range(2)]
        qT = sb("qT", [P, KC, N])
        k_eo = [sb(f"k_eo{i}", [P, KC, N]) for i in range(2)]
        v_eo = [sb(f"v_eo{i}", [P, NT, HEADS // 2, 2, HD]) for i in range(2)]
        v_full = sb("v_full", [P, C])
        k_lam = sb("k_lam", [P, C])
        q_lam = sb("q_lam", [P, KC, T])
        state = sb("state", [P, KC, P])
        scm = sb("scm", [P, 4, KC, 2, T])
        oT = sb("oT", [P, NT, KC, T])
        osq = sb("osq", [P, NT, KC, T])
        fin = sb("fin", [P, 5, NT])
        fac = sb("fac", [P, NT])
        attn = sb("attn", [P, NT, C])
        x2 = [sb(f"x2_{i}", [P, NT, C]) for i in range(2)]
        bn2 = sb("bn2", [P, NT, 6])
        mv2 = sb("mv2", [P, NT, 2])
        ve2 = sb("ve2", [P, NT])
        rstd2 = sb("rstd2", [P, NT])
        z2 = sb("z2", [P, NT, C])
        h2s = sb("h2s", [P, NT, C])
        h2row = [sb(f"h2row{i}", [P, NT, ROWW]) for i in range(2)]
        h2T = sb("h2T", [P, KC, N])
        pre = sb("pre", [P, B * NT, C])
        r_exp = sb("r_exp", [P, NT, E])
        r_den = sb("r_den", [P, NT, E])
        r_sig = sb("r_sig", [P, NT, E])
        r_sc = sb("r_sc", [P, NT, E])
        g_top = sb("g_top", [P, NT * G, 8])
        g_sum = sb("g_sum", [P, NT, 2 * G])
        g_best = sb("g_best", [P, NT, 8])
        g_rep = sb("g_rep", [P, NT, 2 * G])
        g_pick = sb("g_pick", [P, NT, G])
        g_pen = sb("g_pen", [P, NT, G])
        e_val = sb("e_val", [P, NT, E])
        e_best = sb("e_best", [P, NT, 8])
        e_rep = sb("e_rep", [P, NT, E])
        sel = sb("sel", [P, NT, E])
        sel_bf = sb("sel_bf", [P, NT, E], BF16)
        carry = sb("carry", [P, NT, E], BF16)
        w_raw = sb("w_raw", [P, NT, E])
        w_sum = sb("w_sum", [P, NT])
        w_rec = sb("w_rec", [P, NT])
        keep = sb("keep", [P, NT, E])
        row_key = sb("row_key", [P, NT, E])
        key = sb("key", [P, NT, E])
        key_top = sb("key_top", [P, NT, 8])
        slot_ix = [sb(f"slot_ix{i}", [P, NT, 8], U32) for i in range(2)]
        slot_all = sb("slot_all", [P, B * NT, 8], U32)
        s_exp = sb("s_exp", [F, N])
        s_gu = sb("s_gu", [F, N])
        s_h = sb("s_h", [F, N])
        sh_g = sb("sh_g", [P, NT, C])

        eg = sb("eg", [P, RING, 2, KC, F])
        eu = sb("eu", [P, RING, 2, KC, F])
        ed = sb("ed", [F, RING, 2, C])
        pad = sb("pad", [P, 1])
        pool_pad = sb("pool_pad", [P, 4])
        wcol = [sb(f"wcol{i}", [P, 1]) for i in range(NBUF)]
        xr = [h2row[0][:, 0], h2row[1][:, 0]]
        xt = [attn[:, i].rearrange("p (k r) -> p k r", k=KC) for i in range(NBUF)]
        e_exp = [s_exp[:, 0:P], s_exp[:, P:N]]
        e_gu = [s_gu[:, 0:P], s_gu[:, P:N]]
        e_h = [s_h[:, 0:P], s_h[:, P:N]]
        e_out = [oT[:, i].rearrange("p j t -> p (j t)") for i in range(NBUF)]
        qkv_raw = eg[:, 0:4].rearrange("p a b k f -> p (a b k f)")[:, 0:6 * C].rearrange("p (a c) -> p a c", a=6)
        proj_raw = eg[:, 4:6].rearrange("p a b k f -> p (a b k f)")[:, 0:2 * C].rearrange("p (a c) -> p a c", a=2)
        wmod_sb = eu[:, 0:8].rearrange("p a b k f -> p (a b k f)").rearrange("p (k n) -> p k n", k=2)
        zeros = scm[:, 0:2].rearrange("p r j q t -> p (r j q t)")
        gath = [g for g in (
            eg[:, 0:4].rearrange("p a b k f -> p (a b k f)").rearrange("p (j c) -> p j c", j=TOPK),
            eg[:, 4:8].rearrange("p a b k f -> p (a b k f)").rearrange("p (j c) -> p j c", j=TOPK))]
        ysum = [z1[:, i] for i in range(2)]
        ygb = [h2s[:, i] for i in range(2)]
        yout = [z2[:, i] for i in range(2)]

        ps_s = ctx.enter_context(nc.psum_tensor("ps_s", [P, 4, 512], F32))
        ps_o = ctx.enter_context(nc.psum_tensor("ps_o", [P, 512], F32))
        ps_a = ctx.enter_context(nc.psum_tensor("ps_a", [P, 512], F32))
        ps_b = ctx.enter_context(nc.psum_tensor("ps_b", [P, 512], F32))
        ps_c = ctx.enter_context(nc.psum_tensor("ps_c", [P, 512], F32))
        e_xt = [ps_a[:, 0:C], ps_b[:, 0:C]]
        e_gups = [ps_s[:, i, 0:2 * P] for i in range(NBUF)]
        e_dn = [ps_c[:, 0:C], ps_o[:, 0:C]]

        names = """
        prologue_step
        silu_step
        shared_step
        slot_step
        factor_step
        route
        ld_small ld_norms ld_c ld_wmod ld_qkvw ld_projw ld_gate ld_shared ld_xa ld_xres ld_modb0 ld_modb1 ld_gb
        ld_first pairs_landed ld_xr0 ld_xr1 st_mod st_zero st_rows0 st_rows1 st_eout0 st_eout1
        st_gath0 st_gath1 st_y0 st_y1
        c_zero c_fill c_shape c_neg c_decay0 c_decay c_lam   c_misc
        q_abs q_all     q_tern q_tp q_sc q_w
        m_exp   m_silu m_tp m_ct m_mm m_cols m_rows0    m_rows
        ln1_step ln1_ve ln1_rstd z1_ready xt_done mod_cur_ready hT_ready hsq_ready
        q_done q_taken k_done k_taken v_done v_taken kt_done rr_a rr2_ready a16_ready
        klam_ready qlam_ready kv_done state_ready
        sc0 sc1 mk0 mk1 pv0 pv1 o_taken
        os_done f1   f5 f_ready proj_done attn_ready x2_ready
        ln2_step ln2_ve ln2_rstd z2_ready h2_mul h2_ready h2t_done h2T_ready
        lg_done lg_exp r1               selbf_ready
           w_ready carry_ready
        gu_done sg_exp sg1   sh_ready dn_done sh_gated pre_ready
        pos_done    slots_ready
        xtp xt_taken wcol_ready gup ge_exp    gh_ready dnp e_evac
        y_ix y_settled y_zero y_sum y_gb y_out
        """.split() + [f"ld_slot{i}" for i in range(RING)]
        S = {n: sem(n) for n in names}

        block = ctx.enter_context(nc.Block())

        x_t = x.rearrange("b (i p) c -> b p i c", p=P)
        out_t = out.rearrange("b (i p) c -> (b i) p c", p=P)
        wg_v = w_gate.rearrange("(r e) (p k) f -> r p e k f", e=2, k=KC)
        wu_v = w_up.rearrange("(r e) (p k) f -> r p e k f", e=2, k=KC)
        wd_v = w_down.rearrange("(r e) f c -> r f e c", e=2)
        rows_v = rows_dram.rearrange("(r p) c -> r p c", p=P)
        eout_v = eout_dram.rearrange("(r p) c -> r p c", p=P)

        def token_steps(eng, step):
            for s in range(3):
                step(s, s % 2, s // 2, max(s - 1, 0) // 2)
            with eng.Fori(0, (B - 4) // 2) as i:
                step(2 * i + 3, 1, i + 1, i + 1)
                step(2 * i + 4, 0, i + 2, i + 1)
            step(B - 1, 1, (B - 1) // 2, (B - 2) // 2)
            step(B, 0, B // 2, (B - 1) // 2)
            step(B + 1, 1, (B + 1) // 2, B // 2)

        def pair_steps(eng, step):
            step(-1, 0, -1)
            step(0, 0, 0)
            with eng.Fori(0, (PAIRS - 2) // RING) as i:
                for m in range(1, 1 + RING):
                    step(RING * i + m, i, m)
            step(PAIRS - 1, 0, PAIRS - 1)
            step(PAIRS, 0, PAIRS)

        def turn(i, m, n):
            return RING // n * i + m // n

        def before(v, start):
            return isinstance(v, int) and v < start

        def at_end(v, end):
            return isinstance(v, int) and v >= end

        @block.sync
        def _(sp):
            sp.dma_start(c_sb[:], c).then_inc(S["ld_c"], 16)
            sp.dma_start(s_row[:], spread(s, 0, P)).then_inc(S["ld_small"], 16)
            for j in range(KC):
                for a in range(HPJ):
                    sp.dma_start(s_part[HD * a:HD * a + HD, j:j + 1], spread(s[HPJ * j + a:HPJ * j + a + 1], 0, HD)
                                 ).then_inc(S["ld_small"], 16)
            sp.dma_start(xa[:], x_t[0]).then_inc(S["ld_xa"], 16)
            sp.dma_start(gate_sb[:], gate_w.rearrange("(k p) e -> p k e", p=P)).then_inc(S["ld_gate"], 16)
            sp.dma_start(ws_gu[:, :, 0], ws_gate.rearrange("(k p) f -> p k f", p=P)).then_inc(S["ld_shared"], 16)
            sp.dma_start(ws_gu[:, :, 1], ws_up.rearrange("(k p) f -> p k f", p=P)).then_inc(S["ld_shared"], 16)
            sp.dma_start(ws_d[:], ws_down).then_inc(S["ld_shared"], 16)
            sp.wait_ge(S["c_zero"], 1)
            sp.dma_start(rows_dram.rearrange("(p r) c -> p (r c)", p=P).rearrange("p (a n) -> p a n", n=1024),
                         spread(zeros, 1, ROWS // P * ROWW // 1024)).then_inc(S["st_zero"], 16)
            sp.wait_ge(S["m_rows"], 1)
            sp.dma_start(mod_dram, mod_rows[:]).then_inc(S["st_mod"], 16)
            sp.wait_ge(S["st_mod"], 16)
            sp.dma_start(gb_all[:], spread(mod_dram[:, 3 * C:4 * C], 0, P)).then_inc(S["ld_gb"], 16)
            sp.wait_ge(S["q_tp"], 1)
            sp.wait_ge(S["m_mm"], 1)

            def load_pair(p):
                sp.dma_start(eg[:, p], wg_v[p]).then_inc(S["ld_first"], 16)
                sp.dma_start(eu[:, p], wu_v[p]).then_inc(S["ld_first"], 16)
                sp.dma_start(ed[:, p], wd_v[p]).then_inc(S["ld_first"], 16)

            def step(s, par, h, hp):
                if at_end(s, B):
                    return
                if not at_end(s, B - 1):
                    sp.wait_ge(S["z1_ready"], s + 1)
                    sp.dma_start(xa[:], x_t[s + 1]).then_inc(S["ld_xa"], 16)
                seen(sp, S["h2_ready"], s - 1)
                sp.dma_start(mod_b[par][:].rearrange("p a c -> p (a c)"),
                             spread(mod_dram[s, 0:3 * C], 0, P)).then_inc(S[f"ld_modb{par}"], 16)
                if before(s, 3):
                    for p in range(RING * s // 3, RING * (s + 1) // 3):
                        load_pair(p)
                seen(sp, S["x2_ready"], s)
                sp.dma_start(xres[:], x_t[s]).then_inc(S["ld_xres"], 16)

            token_steps(sp, step)

            for par in range(2):
                sp.wait_ge(S[f"st_rows{par}"], 16 * B // 2 * NT * TOPK)
            for q in range(NBUF):
                sp.dma_start(xr[q], rows_v[q]).then_inc(S[f"ld_xr{q}"], 16)

            def load_rows(q, buf):
                sp.wait_ge(S["xtp"], q - NBUF + 1)
                sp.wait_ge(S["wcol_ready"], q - NBUF + 1)
                sp.dma_start(xr[buf], rows_v[q]).then_inc(S[f"ld_xr{buf}"], 16)

            def store_rows(q, buf):
                sp.wait_ge(S["e_evac"], q + 1)
                sp.dma_start(eout_v[q], e_out[buf]).then_inc(S[f"st_eout{buf}"], 16)

            load_rows(NBUF, 0)
            TURNS = PAIRS // NBUF - 2
            with sp.Fori(0, TURNS) as i:
                for u in range(NBUF):
                    load_rows(NBUF * i + (u + NBUF + 1), (1 + u) % NBUF)
                    store_rows(NBUF * i + u, u)
            for q in range(NBUF * TURNS + NBUF + 1, PAIRS):
                load_rows(q, q % NBUF)
            for q in range(NBUF * TURNS, PAIRS):
                store_rows(q, q % NBUF)

            with sp.Fori(0, B) as b:
                for i in range(NT):
                    sp.wait_ge(S["y_out"], NT * b + (i + 1))
                    sp.dma_start(out_t[NT * b + i], yout[i]).then_inc(S[f"st_y{i}"], 16)
            for i in range(NT):
                sp.wait_ge(S[f"st_y{i}"], 16 * B + 16)

        @block.gpsimd
        def _(pool):
            g = nc.gpsimd
            last_row = g.to_reg(ROWS - 1)
            g.memset(zeros, 0.0).then_inc(S["c_zero"], 1)
            g.memset(ident[:], 0.0)
            g.memset(upper[:], 1.0)
            g.memset(head_block[:], 1.0)
            g.memset(half_exp[:, 0], -0.5)
            g.memset(half_exp[:, 1], 0.5)
            g.memset(zero_row[:], 0.0)
            for i in range(2):
                g.memset(v_eo[i][:], 0.0)
            g.memset(carry[:], 0.0)
            g.memset(stat_w[:], 1.0)
            g.iota(part_ix[:], pattern=[[0, 1]], base=0, channel_multiplier=1)
            g.iota(t_left[:], pattern=[[0, 1]], base=T, channel_multiplier=-1, allow_small_or_imprecise_dtypes=True)
            g.iota(trow[:], pattern=[[1, T]], base=0, channel_multiplier=0, allow_small_or_imprecise_dtypes=True)
            g.iota(row_base[:], pattern=[[-SLOTS, E]], base=ROWS, channel_multiplier=0,
                   allow_small_or_imprecise_dtypes=True)
            g.iota(diff[:], pattern=[[1, T]], base=0, channel_multiplier=-1,
                   allow_small_or_imprecise_dtypes=True).then_inc(S["c_fill"], 1)
            pool.wait_ge(S["c_fill"], 1)
            g.affine_select(out=ident[:], in_=ident[:], pattern=[[-1, P]], compare_op=ALU.not_equal, fill=1.0,
                            base=0, channel_multiplier=1)
            g.affine_select(out=upper[:], in_=upper[:], pattern=[[1, P]], compare_op=ALU.is_ge, fill=0.0,
                            base=-1, channel_multiplier=-1)
            hb = head_block[:].rearrange("p (g e) -> p g e", e=HD)
            g.affine_select(out=hb, in_=hb, pattern=[[-HD, HPJ], [0, HD]], compare_op=ALU.is_ge, fill=0.0,
                            base=0, channel_multiplier=1).then_inc(S["c_shape"], 1)
            pool.wait_ge(S["c_shape"], 1)
            g.affine_select(out=hb, in_=hb, pattern=[[HD, HPJ], [0, HD]], compare_op=ALU.is_ge, fill=0.0,
                            base=HD - 1, channel_multiplier=-1).then_inc(S["c_shape"], 1)
            pool.wait_ge(S["q_abs"], 1)
            g.partition_all_reduce(abs_all[:], abs_sum[:], P, RADD).then_inc(S["q_all"], 1)
            pool.wait_ge(S["c_decay0"], 1)
            dv = decay[:].rearrange("p r j q t -> p (r j q) t")
            g.affine_select(out=dv, in_=dv, pattern=[[0, HEADS], [1, T]], compare_op=ALU.is_ge, fill=0.0,
                            base=0, channel_multiplier=-1).then_inc(S["c_decay"], 1)

            def power(out_, in_, which, ready, done, n):
                pool.wait_ge(S[ready], n)
                g.tensor_tensor(out_, in_, half_exp[:, which], ALU.pow).then_inc(S[done], 1)

            def settle(at):
                return g.tensor_tensor(pool_pad[:, at:at + 1], half_exp[:, 0, 0:1], half_exp[:, 0, 0:1], ALU.add)

            def dispatch(b, par, tile):
                if tile == 0:
                    pool.wait_ge(S["slots_ready"], b + 1)
                    pool.wait_ge(S["w_ready"], b + 1)
                    pool.wait_ge(S["h2_ready"], b + 1)
                    settle(par)
                for j in range(TOPK):
                    g.indirect_dma_start(
                        out=rows_dram, out_offset=bass.IndirectOffsetOnAxis(ap=slot_ix[par][:, tile, j:j + 1], axis=0),
                        in_=h2row[par][:, tile, :], in_offset=None, bounds_check=last_row,
                        oob_is_err=False).then_inc(S[f"st_rows{par}"], 16)

            def step(s, par, h, hp):
                if not before(s, 1) and not at_end(s, B + 1):
                    power(fac[:], fin[:, 4], 1, "f5", "f_ready", s)
                if not at_end(s, B):
                    pool.wait_ge(S["q_taken"], s + 1)
                    seen(pool, S["pv1"], s)
                    g.tensor_tensor(q_lam[:], qT[:, :, T:2 * T], lam_q[:], ALU.mult).then_inc(S["qlam_ready"], 1)
                if not before(s, 3):
                    dispatch(s - 3, 1 - par, 0)
                    dispatch(s - 3, 1 - par, 1)
                if not at_end(s, B - 1):
                    power(rstd1[:], ve1[:], 0, "ln1_ve", "ln1_rstd", s + 2)
                if not before(s, 1) and not at_end(s, B + 1):
                    power(rstd2[:], ve2[:], 0, "ln2_ve", "ln2_rstd", s)
                    pool.wait_ge(S["z2_ready"], s)
                    pool.wait_ge(S[f"ld_modb{1 - par}"], 16 * (hp + 1))
                    g.tensor_tensor(h2s[:], z2[:], spread(mod_b[1 - par][:, 2], 1, NT), ALU.mult).then_inc(S["h2_mul"], 1)
                    pool.wait_ge(S["h2_mul"], s)
                    seen(pool, S["h2t_done"], s - 2)
                    seen(pool, S[f"st_rows{1 - par}"], 16 * NT * TOPK * hp)
                    g.tensor_tensor(h2row[1 - par][:, :, 0:C], h2s[:], spread(mod_b[1 - par][:, 1], 1, NT),
                                    ALU.add).then_inc(S["h2_ready"], 1)

            pool.wait_ge(S["ln1_ve"], 1)
            g.tensor_tensor(rstd1[:], ve1[:], half_exp[:, 0], ALU.pow).then_inc(S["ln1_rstd"], 1)
            pool.wait_ge(S["st_zero"], 16)
            pool.wait_ge(S["c_lam"], 1)
            token_steps(pool, step)
            for tile in range(NT):
                dispatch(B - 1, 1, tile)

            def load_pair(p, slot):
                pool.wait_ge(S["dnp"], p - RING + 1)
                g.dma_start(eg[:, slot], wg_v[p]).then_inc(S[f"ld_slot{slot}"], 16)
                g.dma_start(eu[:, slot], wu_v[p]).then_inc(S[f"ld_slot{slot}"], 16)
                g.dma_start(ed[:, slot], wd_v[p]).then_inc(S[f"ld_slot{slot}"], 16)

            def landed(slot, count):
                pool.wait_ge(S[f"ld_slot{slot}"], 48 * count)
                pool.sem_inc(S["pairs_landed"], 1)

            pool.wait_ge(S["ld_first"], 48 * RING)
            pool.sem_inc(S["pairs_landed"], RING)
            with pool.Fori(1, PAIRS // RING) as i:
                for slot in range(RING):
                    load_pair(RING * i + slot, slot)
                    if slot:
                        landed(slot - 1, i)
                landed(RING - 1, i)
            for p in range(PAIRS // RING * RING, PAIRS):
                load_pair(p, p % RING)
            for p in range(PAIRS // RING * RING, PAIRS):
                landed(p % RING, p // RING)

            for i in range(NBUF):
                pool.wait_ge(S[f"st_eout{i}"], 16 * (len(range(i, PAIRS, NBUF)) + 1))
            pool.sem_inc(S["y_settled"], 1)
            with pool.Fori(0, B) as b:
                for i in range(NT):
                    pool.wait_ge(S["y_settled"], NT * b + (i + 1))
                    pool.wait_ge(S["y_zero"], NT * b + (i + 1))
                    pool.wait_ge(S["y_ix"], NT * b + (i + 1))
                    settle(2).then_inc(S["y_settled"], 1)
                    for j in range(TOPK):
                        g.indirect_dma_start(
                            out=gath[i][:, j], out_offset=None, in_=eout_dram,
                            in_offset=bass.IndirectOffsetOnAxis(ap=slot_ix[i][:, 0, j:j + 1], axis=0),
                            bounds_check=last_row, oob_is_err=False).then_inc(S[f"st_gath{i}"], 16)

        @block.scalar
        def _(act):
            a = nc.scalar
            a.dma_start(qkv_raw, qkv_w.rearrange("(a p) c -> p a c", p=P)).then_inc(S["ld_qkvw"], 16)
            a.dma_start(proj_raw, proj_w.rearrange("(a p) c -> p a c", p=P)).then_inc(S["ld_projw"], 16)
            a.dma_start(wmod_sb, wmod.rearrange("(k p) n -> p k n", p=P)).then_inc(S["ld_wmod"], 16)
            for i, w in enumerate((qkv_norm_w, norm_w, proj_norm_w)):
                a.dma_start(norm_cols[:, i], w.rearrange("(k p) -> p k", p=P),
                            allow_slow_non_contiguous=True).then_inc(S["ld_norms"], 16)
            a.dma_start(bias_row[:], spread(bias, 0, P)).then_inc(S["ld_norms"], 16)

            def copy(out_, in_, scale=1.0):
                return a.activation(out_, in_, ACT.Copy, scale=scale)

            act.wait_ge(S["ld_c"], 16)
            a.activation(c_sig[:], c_sb[:], ACT.Exp, scale=-1.0).then_inc(S["m_exp"], 1)
            act.wait_ge(S["c_neg"], 1)
            for h in range(HEADS):
                last = a.activation(decay[:, h % 8 // 2, h // 8, h % 2], diff[:], ACT.Exp, scale=neg_s[:, h:h + 1])
            last.then_inc(S["c_decay0"], 1)
            for j in range(KC):
                a.activation(lam_q[:, j], trow[:], ACT.Exp, scale=neg_s_part[:, j:j + 1])
            a.activation(lam_rev[:], neg_s[:], ACT.Exp, scale=t_left[:, 0:1]).then_inc(S["c_lam"], 1)

            def norm1_out(b, par):
                act.wait_ge(S["xt_done"], b + 1)
                act.wait_ge(S["mod_cur_ready"], b + 1)
                seen(act, S["v_done"], b)
                seen(act, S["kt_done"], b)
                for j in range(KC):
                    last = a.activation(hT[:, j], ps_a[:, N * j:N * j + N], ACT.Identity,
                                        scale=mod_cur[par][:, 2 + j:3 + j], bias=mod_cur[par][:, j:j + 1])
                last.then_inc(S["hT_ready"], 1)
                for j in range(KC):
                    last = a.activation(hsq[:, j], ps_a[:, N * j:N * j + N], ACT.Square,
                                        scale=mod_cur[par][:, 2 + j:3 + j], bias=mod_cur[par][:, j:j + 1])
                last.then_inc(S["hsq_ready"], 1)

            def step(s, par, h, hp):
                has_prev = not before(s, 1) and not at_end(s, B + 1)
                cur = not at_end(s, B)
                if cur:
                    act.wait_ge(S["q_done"], s + 1)
                    seen(act, S["qlam_ready"], s)
                    copy(qT[:].rearrange("p j t -> p (j t)"), ps_a[:]).then_inc(S["q_taken"], 1)
                    act.wait_ge(S["k_done"], s + 1)
                    for i in range(2):
                        last = copy(k_eo[i][:].rearrange("p j t -> p (j t)"), ps_b[:], even_odd[:, i:i + 1])
                    last.then_inc(S["k_taken"], 1)
                    act.wait_ge(S["v_done"], s + 1)
                    act.wait_ge(S["rr2_ready"], s + 1)
                    copy(v_full[:], ps_c[:, 0:C], rr2[:, 0:1])
                    for tile in range(NT):
                        vv = ps_c[:, C * tile:C * tile + C].rearrange("p (a q d) -> p a q d", q=2, d=HD)
                        for i in range(2):
                            last = copy(v_eo[i][:, tile, :, i], vv[:, :, i], rr2[:, tile:tile + 1])
                    last.then_inc(S["v_taken"], 1)
                if has_prev:
                    act.wait_ge(S["h2t_done"], s)
                    copy(h2T[:].rearrange("p j t -> p (j t)"), ps_a[:]).then_inc(S["h2T_ready"], 1)
                if cur:
                    act.wait_ge(S["pv1"], s + 1)
                    copy(oT[:].rearrange("p i j t -> p (i j t)"), ps_o[:])
                    a.activation(osq[:].rearrange("p i j t -> p (i j t)"), ps_o[:], ACT.Square).then_inc(S["o_taken"], 1)
                if has_prev:
                    act.wait_ge(S["lg_done"], s)
                    seen(act, S["r1"], s - 1)
                    a.activation(r_exp[:].rearrange("p i e -> p (i e)"), ps_b[:, 0:NT * E], ACT.Exp,
                                 scale=-1.0).then_inc(S["lg_exp"], 1)
                if not at_end(s, B - 1):
                    norm1_out(s + 1, 1 - par)
                if has_prev:
                    act.wait_ge(S["gu_done"], s)
                    seen(act, S["sg1"], s - 1)
                    a.activation(s_exp[:], ps_c[0:F, 0:N], ACT.Tanh, scale=0.5).then_inc(S["sg_exp"], 1)

            norm1_out(0, 0)
            act.wait_ge(S["c_misc"], 1)
            act.wait_ge(S["c_fill"], 1)
            token_steps(act, step)

            def pair_step(q, i, m):
                if not before(q, 0) and not at_end(q, PAIRS):
                    act.wait_ge(S["gup"], q + 1)
                    a.activation(e_exp[m % NBUF], e_gups[m % NBUF][0:F, 0:P], ACT.Tanh,
                                 scale=0.5).then_inc(S["ge_exp"], 1)
                if not before(q, 1):
                    n = (m - 1) % NBUF
                    act.wait_ge(S["dnp"], q)
                    act.wait_ge(S["wcol_ready"], q)
                    seen(act, S[f"st_eout{n}"], 16 * (turn(i, m - 1, NBUF) + 1))
                    copy(e_out[n], e_dn[n], wcol[n][:, 0:1]).then_inc(S["e_evac"], 1)

            for n in range(NBUF):
                act.sem_inc(S[f"st_eout{n}"], 16)
            pair_steps(act, pair_step)

            def clear(i):
                copy(gath[i], spread(zero_row[:], 1, TOPK)).then_inc(S["y_zero"], 1)

            act.wait_ge(S["dnp"], PAIRS)
            for i in range(NT):
                clear(i)
            with act.Fori(0, B - 1) as b:
                for i in range(NT):
                    act.wait_ge(S["y_sum"], NT * b + (i + 1))
                    clear(i)

        @block.vector
        def _(dve):
            v = nc.vector
            dve.wait_ge(S["m_exp"], 1)
            v.tensor_scalar(c_sig[:], c_sig[:], 1.0, None, ALU.add).then_inc(S["prologue_step"], 1)
            dve.wait_ge(S["prologue_step"], 1)
            v.reciprocal(c_sig[:], c_sig[:]).then_inc(S["prologue_step"], 1)
            dve.wait_ge(S["prologue_step"], 2)
            v.tensor_tensor(c_sb[:], c_sb[:], c_sig[:], ALU.mult).then_inc(S["m_silu"], 1)
            dve.wait_ge(S["ld_qkvw"], 16)
            v.tensor_reduce(abs_sum[:, 0:1], qkv_raw, mybir.AxisListType.XY, ALU.add, apply_absolute_value=True)
            dve.wait_ge(S["ld_projw"], 16)
            v.tensor_reduce(abs_sum[:, 1:2], proj_raw, mybir.AxisListType.XY, ALU.add,
                            apply_absolute_value=True).then_inc(S["q_abs"], 1)
            dve.wait_ge(S["ld_small"], 16 * (1 + HEADS))
            dve.wait_ge(S["ld_norms"], 16 * 4)
            dve.wait_ge(S["c_fill"], 1)
            v.tensor_scalar(neg_s[:], s_row[:], -1.0, None, ALU.mult)
            v.tensor_scalar(neg_s_part[:], s_part[:], -1.0, None, ALU.mult)
            v.tensor_scalar(diff[:], diff[:], 0.0, None, ALU.max).then_inc(S["c_neg"], 1)
            v.memset(ones_bf[:], 1.0)
            v.tensor_scalar(part_bit[:], part_ix[:], HD, None, ALU.bitwise_and).then_inc(S["prologue_step"], 1)
            dve.wait_ge(S["prologue_step"], 3)
            v.tensor_scalar(even_odd[:, 1:2], part_bit[:], 1.0 / HD, None, ALU.mult)
            v.tensor_scalar(even_odd[:, 0:1], part_bit[:], -1.0 / HD, 1.0, ALU.mult, ALU.add)
            v.tensor_tensor(q_scale[:, 0], norm_cols[:, 1], norm_cols[:, 1], ALU.mult).then_inc(S["prologue_step"], 1)
            dve.wait_ge(S["prologue_step"], 4)
            v.tensor_scalar(stat_w[:, :, 1], q_scale[:, 0], EPS_F, None, ALU.add)
            v.tensor_tensor(q_scale[:, 1], norm_cols[:, 1], norm_cols[:, 2], ALU.mult).then_inc(S["c_misc"], 1)
            dve.wait_ge(S["q_all"], 1)
            v.tensor_scalar(w_mean[:, 0:1], abs_all[:, 0:1], 1.0 / (3 * C * C), 1e-5, ALU.mult, ALU.max)
            v.tensor_scalar(w_mean[:, 1:2], abs_all[:, 1:2], 1.0 / (C * C), 1e-5, ALU.mult,
                            ALU.max).then_inc(S["prologue_step"], 1)
            dve.wait_ge(S["prologue_step"], 5)
            v.reciprocal(w_inv[:], w_mean[:]).then_inc(S["prologue_step"], 1)
            dve.wait_ge(S["c_misc"], 1)
            v.tensor_scalar(q_scale[:, 0], norm_cols[:, 0], w_mean[:, 0:1], None, ALU.mult)
            v.tensor_scalar(q_scale[:, 1], q_scale[:, 1], w_mean[:, 1:2], None, ALU.mult).then_inc(S["q_sc"], 1)
            dve.wait_ge(S["prologue_step"], 6)
            v.tensor_scalar(qkv_raw, qkv_raw, w_inv[:, 0:1], MAGIC, ALU.mult, ALU.add)
            v.tensor_scalar(proj_raw, proj_raw, w_inv[:, 1:2], MAGIC, ALU.mult, ALU.add).then_inc(S["prologue_step"], 1)
            dve.wait_ge(S["prologue_step"], 7)
            v.tensor_scalar(qkv_raw, qkv_raw, MAGIC, 1.0, ALU.subtract, ALU.min)
            v.tensor_scalar(proj_raw, proj_raw, MAGIC, 1.0, ALU.subtract, ALU.min).then_inc(S["prologue_step"], 1)
            dve.wait_ge(S["prologue_step"], 8)
            v.tensor_scalar(qkv_raw, qkv_raw, -1.0, None, ALU.max)
            v.tensor_scalar(proj_raw, proj_raw, -1.0, None, ALU.max).then_inc(S["q_tern"], 1)
            dve.wait_ge(S["m_tp"], 1)
            v.tensor_copy(c_cols[:].rearrange("p k b -> p (k b)"), ps_o[:, 0:KC * B]).then_inc(S["m_ct"], 1)
            dve.wait_ge(S["m_mm"], 1)
            mc = mod_cols[:].rearrange("p m b -> p (m b)")
            v.tensor_copy(mc[:, 0:2 * B], ps_o[:, 64:64 + 2 * B])
            v.tensor_scalar(mc[:, 2 * B:4 * B], ps_o[:, 64 + 2 * B:64 + 4 * B], 1.0, None, ALU.add).then_inc(S["m_cols"], 1)
            v.tensor_copy(mod_rows[:, 0:2 * C], ps_b[0:B, :])
            v.tensor_copy(mod_rows[:, 2 * C:4 * C], ps_c[0:B, :]).then_inc(S["m_rows0"], 1)
            dve.wait_ge(S["m_rows0"], 1)
            gates = mod_rows[:].rearrange("p (m c) -> p m c", m=4)[:, 0:4:3]
            v.tensor_scalar(mod_rows[:, 2 * C:3 * C], mod_rows[:, 2 * C:3 * C], 1.0, None, ALU.add)
            v.tensor_scalar(sign_rows[:], gates, 0.0, 2.0, ALU.is_ge, ALU.mult).then_inc(S["prologue_step"], 1)
            v.scalar_tensor_tensor(out=abs_rows[:], in0=gates, scalar=-1.0, in1=gates, op0=ALU.mult,
                                   op1=ALU.max).then_inc(S["prologue_step"], 1)
            dve.wait_ge(S["prologue_step"], 9)
            v.tensor_scalar(sign_rows[:], sign_rows[:], 1.0, None, ALU.subtract).then_inc(S["prologue_step"], 1)
            dve.wait_ge(S["prologue_step"], 10)
            dve.wait_ge(S["prologue_step"], 11)
            v.scalar_tensor_tensor(out=gates, in0=abs_rows[:], scalar=0.25, in1=sign_rows[:], op0=ALU.max,
                                   op1=ALU.mult).then_inc(S["m_rows"], 1)
            dve.wait_ge(S["q_tp"], 1)
            dve.wait_ge(S["q_sc"], 1)
            for k in range(KC):
                v.tensor_scalar(w_qkv[:, k, 0:512], ps_s[:, k], q_scale[:, 0, k:k + 1], None, ALU.mult)
                v.tensor_scalar(w_qkv[:, k, 512:768], ps_s[:, 2, C * k:C * k + C], q_scale[:, 0, k:k + 1], None, ALU.mult)
                last = v.tensor_scalar(w_proj[:, k], ps_s[:, 3, C * k:C * k + C], q_scale[:, 1, k:k + 1], None, ALU.mult)
            last.then_inc(S["q_w"], 1)

            def settle():
                v.memset(pad[:], 0.0)

            def norm_stats(b, x_, bn, mv, ve, pre_):
                for i in range(NT):
                    last = v.bn_stats(bn[:, i], x_[:, i])
                last.then_inc(S[pre_ + "_step"], 1)
                dve.wait_ge(S[pre_ + "_step"], 2 * b + 1)
                settle()
                for i in range(NT):
                    last = v.bn_aggr(mv[:, i], bn[:, i])
                last.then_inc(S[pre_ + "_step"], 1)
                dve.wait_ge(S[pre_ + "_step"], 2 * b + 2)
                v.tensor_scalar(ve[:], mv[:, :, 1], EPS_LN, None, ALU.add).then_inc(S[pre_ + "_ve"], 1)

            def norm_apply(b, x_, mv, rstd, z, pre_, z_sem):
                dve.wait_ge(S[pre_ + "_rstd"], b + 1)
                for i in range(NT):
                    last = v.tensor_scalar(z[:, i], x_[:, i], mv[:, i, 0:1], rstd[:, i:i + 1], ALU.subtract, ALU.mult)
                last.then_inc(S[z_sem], 1)

            def norm1_stats(b):
                dve.wait_ge(S["ld_xa"], 16 * (b + 1))
                norm_stats(b, xa, bn1, mv1, ve1, "ln1")

            def norm1_apply(b, par):
                seen(dve, S["xt_done"], b)
                norm_apply(b, xa, mv1, rstd1, z1, "ln1", "z1_ready")
                seen(dve, S["hsq_ready"], b - 1)
                v.tensor_copy(mod_cur[par][:], mod_cols[:, :, b]).then_inc(S["mod_cur_ready"], 1)

            def rms(b, par):
                dve.wait_ge(S["kt_done"], b + 1)
                v.tensor_scalar(rr_t[:], ps_a[:, C:C + NT], 1.0 / C, EPS_F, ALU.mult, ALU.add).then_inc(S["rr_a"], 1)
                dve.wait_ge(S["rr_a"], b + 1)
                seen(dve, S["v_taken"], b)
                v.reciprocal(rr2[:], rr_t[:]).then_inc(S["rr2_ready"], 1)
                dve.wait_ge(S["kt_done"], b + 1)
                seen(dve, S["kv_done"], b)
                v.tensor_tensor(k_lam[:].rearrange("p (h d) -> p h d", d=HD),
                                ps_a[:, 0:C].rearrange("p (h d) -> p h d", d=HD), spread(lam_rev[:], 2, HD),
                                ALU.mult).then_inc(S["klam_ready"], 1)
                dve.wait_ge(S["rr2_ready"], b + 1)
                v.tensor_scalar(a16[par][:], rr2[:], 1.0 / HD, None, ALU.mult).then_inc(S["a16_ready"], 1)
            def state_block(b):
                dve.wait_ge(S["kv_done"], b + 1)
                seen(dve, S["pv1"], b)
                v.tensor_tensor(state[:], ps_b[:, 0:KC * P].rearrange("p (j m) -> p j m", j=KC),
                                spread(head_block[:], 1, KC), ALU.mult).then_inc(S["state_ready"], 1)

            def out_norms(b, par):
                dve.wait_ge(S["os_done"], b + 1)
                dve.wait_ge(S["a16_ready"], b + 1)
                v.scalar_tensor_tensor(out=fin[:, 1], in0=ps_o[:, 0:NT], scalar=1.0 / C, in1=a16[par][:],
                                       op0=ALU.mult, op1=ALU.mult).then_inc(S["f1"], 1)
                dve.wait_ge(S["f1"], b + 1)
                v.tensor_scalar(fin[:, 2], fin[:, 1], EPS_F * EPS_O, None, ALU.add).then_inc(S["factor_step"], 1)
                dve.wait_ge(S["factor_step"], 2 * b + 1)
                v.reciprocal(fin[:, 3], fin[:, 2]).then_inc(S["factor_step"], 1)
                dve.wait_ge(S["factor_step"], 2 * b + 2)
                v.tensor_tensor(fin[:, 4], fin[:, 3], a16[par][:], ALU.mult).then_inc(S["f5"], 1)

            def residual(b, par, hb):
                dve.wait_ge(S["f_ready"], b + 1)
                dve.wait_ge(S["proj_done"], b + 1)
                dve.wait_ge(S[f"ld_modb{par}"], 16 * (hb + 1))
                for i in range(NT):
                    last = v.scalar_tensor_tensor(out=attn[:, i], in0=ps_c[:, C * i:C * i + C], scalar=fac[:, i:i + 1],
                                                  in1=mod_b[par][:, 0], op0=ALU.mult, op1=ALU.mult)
                last.then_inc(S["attn_ready"], 1)
                dve.wait_ge(S["attn_ready"], b + 1)
                dve.wait_ge(S["ld_xres"], 16 * (b + 1))
                v.tensor_tensor(x2[par][:], attn[:], xres[:], ALU.add).then_inc(S["x2_ready"], 1)
                dve.wait_ge(S["x2_ready"], b + 1)
                norm_stats(b, x2[par], bn2, mv2, ve2, "ln2")

            def mask(b, tile):
                dve.wait_ge(S[f"sc{tile}"], b + 1)
                if tile == 0:
                    seen(dve, S["pv1"], b)
                else:
                    dve.wait_ge(S["pv0"], b + 1)
                v.tensor_tensor(scm[:].rearrange("p r j q t -> p (r j q t)"), ps_s[:].rearrange("p r n -> p (r n)"),
                                decay[:].rearrange("p r j q t -> p (r j q t)"), ALU.mult).then_inc(S[f"mk{tile}"], 1)

            def router_scores(b):
                dve.wait_ge(S["lg_exp"], b + 1)
                v.tensor_scalar(r_den[:], r_exp[:], 1.0, None, ALU.add).then_inc(S["r1"], 1)
                dve.wait_ge(S["r1"], b + 1)
                v.reciprocal(r_sig[:], r_den[:]).then_inc(S["route"], 1)
                dve.wait_ge(S["route"], ROUTE_STEPS * b + 1)
                v.tensor_tensor(r_sc[:], r_sig[:], spread(bias_row[:], 1, NT), ALU.add).then_inc(S["route"], 1)
                dve.wait_ge(S["route"], ROUTE_STEPS * b + 2)
                v.memset(g_sum[:, :, G:2 * G], OUT)
                for i in range(NT):
                    for g_ in range(G):
                        last = v.max(g_top[:, i * G + g_], r_sc[:, i, EG * g_:EG * g_ + EG])
                last.then_inc(S["route"], 1)

            def router_choice(b, par):
                dve.wait_ge(S["route"], ROUTE_STEPS * b + 3)
                v.tensor_tensor(g_sum[:, :, 0:G], g_top[:, :, 0].rearrange("p (i g) -> p i g", i=NT),
                                g_top[:, :, 1].rearrange("p (i g) -> p i g", i=NT), ALU.add).then_inc(S["route"], 1)
                dve.wait_ge(S["route"], ROUTE_STEPS * b + 4)
                settle()
                for i in range(NT):
                    last = v.max(g_best[:, i], g_sum[:, i])
                last.then_inc(S["route"], 1)
                dve.wait_ge(S["route"], ROUTE_STEPS * b + 5)
                v.memset(g_best[:, :, KG:8], OUT).then_inc(S["route"], 1)
                dve.wait_ge(S["route"], ROUTE_STEPS * b + 6)
                settle()
                for i in range(NT):
                    last = v.match_replace(g_rep[:, i], g_best[:, i], g_sum[:, i], PICK)
                last.then_inc(S["route"], 1)
                dve.wait_ge(S["route"], ROUTE_STEPS * b + 7)
                v.tensor_scalar(g_pick[:], g_rep[:, :, 0:G], 1.5 * OUT, None, ALU.is_lt).then_inc(S["route"], 1)
                dve.wait_ge(S["route"], ROUTE_STEPS * b + 8)
                v.tensor_scalar(g_pen[:], g_pick[:], -OUT, OUT, ALU.mult, ALU.add).then_inc(S["route"], 1)
                dve.wait_ge(S["route"], ROUTE_STEPS * b + 9)
                r4 = r_sc[:].rearrange("p i (g e) -> p i g e", g=G)
                v.tensor_tensor(e_val[:].rearrange("p i (g e) -> p i g e", g=G), r4, spread(g_pen[:], 3, EG),
                                ALU.add).then_inc(S["route"], 1)
                dve.wait_ge(S["route"], ROUTE_STEPS * b + 10)
                settle()
                for i in range(NT):
                    last = v.max(e_best[:, i], e_val[:, i])
                last.then_inc(S["route"], 1)
                dve.wait_ge(S["route"], ROUTE_STEPS * b + 11)
                v.memset(e_best[:, :, TOPK:8], OUT).then_inc(S["route"], 1)
                dve.wait_ge(S["route"], ROUTE_STEPS * b + 12)
                settle()
                for i in range(NT):
                    last = v.match_replace(e_rep[:, i], e_best[:, i], e_val[:, i], PICK)
                last.then_inc(S["route"], 1)
                dve.wait_ge(S["route"], ROUTE_STEPS * b + 13)
                v.scalar_tensor_tensor(out=sel[:].rearrange("p i (g e) -> p i g e", g=G),
                                       in0=e_rep[:].rearrange("p i (g e) -> p i g e", g=G), scalar=1.5 * OUT,
                                       in1=spread(g_pick[:], 3, EG), op0=ALU.is_lt, op1=ALU.mult
                                       ).then_inc(S["route"], 1)
                dve.wait_ge(S["route"], ROUTE_STEPS * b + 14)
                seen(dve, S["pos_done"], b)
                v.tensor_copy(sel_bf[:], sel[:]).then_inc(S["selbf_ready"], 1)
                v.tensor_tensor(w_raw[:], sel[:], r_sig[:], ALU.mult).then_inc(S["route"], 1)
                dve.wait_ge(S["selbf_ready"], b + 1)
                v.tensor_tensor(carry[:, 1], carry[:, 0], sel_bf[:, 0], ALU.add).then_inc(S["carry_ready"], 1)
                dve.wait_ge(S["route"], ROUTE_STEPS * b + 15)
                v.tensor_reduce(w_sum[:], w_raw[:], AX_X, ALU.add).then_inc(S["route"], 1)
                dve.wait_ge(S["route"], ROUTE_STEPS * b + 16)
                v.reciprocal(w_rec[:], w_sum[:]).then_inc(S["route"], 1)
                dve.wait_ge(S["route"], ROUTE_STEPS * b + 17)
                dve.wait_ge(S["h2_ready"], b + 1)
                for i in range(NT):
                    last = v.tensor_scalar(h2row[par][:, i, C:ROWW], w_raw[:, i], w_rec[:, i:i + 1], ROUTE_SCALE,
                                           ALU.mult, ALU.mult)
                last.then_inc(S["w_ready"], 1)

            def shared(b):
                dve.wait_ge(S["sg_exp"], b + 1)
                v.scalar_tensor_tensor(out=s_gu[:], in0=s_exp[:], scalar=1.0, in1=ps_c[0:F, 0:N], op0=ALU.add,
                                       op1=ALU.mult).then_inc(S["sg1"], 1)
                dve.wait_ge(S["sg1"], b + 1)
                v.scalar_tensor_tensor(out=s_h[:], in0=s_gu[:], scalar=0.5, in1=ps_c[0:F, N:2 * N], op0=ALU.mult,
                                       op1=ALU.mult).then_inc(S["sh_ready"], 1)

            def shared_out(b, par):
                dve.wait_ge(S["dn_done"], b + 1)
                dve.wait_ge(S["ld_gb"], 16)
                v.tensor_tensor(sh_g[:], ps_b[:].rearrange("p (i c) -> p i c", i=NT), spread(gb_all[:, b], 1, NT),
                                ALU.mult).then_inc(S["sh_gated"], 1)
                dve.wait_ge(S["sh_gated"], b + 1)
                v.tensor_tensor(pre[:, bass.ds(NT * b, NT)], sh_g[:], x2[par][:], ALU.add).then_inc(S["pre_ready"], 1)

            def slots(b, par):
                dve.wait_ge(S["pos_done"], b + 1)
                pos = ps_o[:, E:E + NT * E].rearrange("p (i e) -> p i e", i=NT)
                v.scalar_tensor_tensor(out=keep[:], in0=pos, scalar=float(CAP), in1=sel[:], op0=ALU.is_lt,
                                       op1=ALU.mult)
                v.tensor_tensor(row_key[:], spread(row_base[:], 1, NT), pos, ALU.subtract).then_inc(S["slot_step"], 1)
                v.tensor_tensor(carry[:, 0], carry[:, 1], sel_bf[:, 1], ALU.add)
                dve.wait_ge(S["slot_step"], 3 * b + 1)
                v.tensor_tensor(key[:], keep[:], row_key[:], ALU.mult).then_inc(S["slot_step"], 1)
                dve.wait_ge(S["slot_step"], 3 * b + 2)
                settle()
                for i in range(NT):
                    last = v.max(key_top[:, i], key[:, i])
                last.then_inc(S["slot_step"], 1)
                dve.wait_ge(S["slot_step"], 3 * b + 3)
                v.tensor_scalar(slot_all[:, bass.ds(NT * b, NT)], key_top[:], -1.0, float(ROWS), ALU.mult, ALU.add)
                v.tensor_scalar(slot_ix[par][:], key_top[:], -1.0, float(ROWS), ALU.mult,
                                ALU.add).then_inc(S["slots_ready"], 1)

            def step(s, par, h, hp):
                cur, nxt = not at_end(s, B), not at_end(s, B - 1)
                has_prev = not before(s, 1) and not at_end(s, B + 1)
                has_two = not before(s, 2)
                if has_two:
                    router_scores(s - 2)
                if nxt:
                    norm1_stats(s + 1)
                if has_two:
                    shared(s - 2)
                if has_prev:
                    out_norms(s - 1, 1 - par)
                if cur:
                    rms(s, par)
                if has_two:
                    router_choice(s - 2, par)
                if cur:
                    mask(s, 0)
                if has_two:
                    slots(s - 2, par)
                if has_prev:
                    residual(s - 1, 1 - par, hp)
                if nxt:
                    norm1_apply(s + 1, 1 - par)
                if cur:
                    state_block(s)
                if has_prev:
                    seen(dve, S["h2_mul"], s - 1)
                    norm_apply(s - 1, x2[1 - par], mv2, rstd2, z2, "ln2", "z2_ready")
                if cur:
                    mask(s, 1)
                if has_two:
                    shared_out(s - 2, par)

            norm1_stats(0)
            dve.wait_ge(S["m_cols"], 1)
            norm1_apply(0, 0)
            dve.wait_ge(S["c_lam"], 1)
            dve.wait_ge(S["c_shape"], 2)
            dve.wait_ge(S["c_decay"], 1)
            dve.wait_ge(S["st_zero"], 16)
            token_steps(dve, step)

            def pair_step(q, i, m):
                if not at_end(q, PAIRS - 1):
                    n = (m + 1) % NBUF
                    dve.wait_ge(S["xtp"], q + 2)
                    seen(dve, S["gup"], q)
                    v.tensor_copy(xt[n].rearrange("p k r -> p (k r)"), e_xt[n]).then_inc(S["xt_taken"], 1)
                if not before(q, 0) and not at_end(q, PAIRS):
                    n = m % NBUF
                    dve.wait_ge(S["ge_exp"], q + 1)
                    v.scalar_tensor_tensor(out=e_gu[n], in0=e_exp[n], scalar=1.0, in1=e_gups[n][0:F, 0:P],
                                           op0=ALU.add, op1=ALU.mult).then_inc(S["silu_step"], 1)
                    dve.wait_ge(S["silu_step"], q + 1)
                    v.scalar_tensor_tensor(out=e_h[n], in0=e_gu[n], scalar=0.5, in1=e_gups[n][0:F, P:2 * P],
                                           op0=ALU.mult, op1=ALU.mult).then_inc(S["gh_ready"], 1)
                if not at_end(q, PAIRS - 1):
                    n = (m + 1) % NBUF
                    seen(dve, S["e_evac"], q)
                    for half in range(2):
                        rows = slice(SLOTS * half, SLOTS * half + SLOTS)
                        e = 2 * q + (2 + half)
                        last = v.tensor_copy(wcol[n][rows], xr[n][rows, bass.ds(C + e, 1)])
                    last.then_inc(S["wcol_ready"], 1)

            pair_steps(dve, pair_step)

            def indices(t, i):
                v.tensor_copy(slot_ix[i][:, 0:1], slot_all[:, bass.ds(t, 1)]).then_inc(S["y_ix"], 1)

            def combine(b, i):
                t = NT * b + i
                dve.wait_ge(S[f"st_gath{i}"], 16 * TOPK * (b + 1))
                v.tensor_reduce(ysum[i], gath[i].rearrange("p j c -> p c j"), AX_X, ALU.add).then_inc(S["y_sum"], 1)
                dve.wait_ge(S["y_sum"], t + 1)
                v.tensor_tensor(ygb[i], ysum[i], gb_all[:, b], ALU.mult).then_inc(S["y_gb"], 1)
                dve.wait_ge(S["y_gb"], t + 1)
                dve.wait_ge(S[f"st_y{i}"], 16 * b + 16)
                v.tensor_tensor(yout[i], ygb[i], pre[:, t], ALU.add).then_inc(S["y_out"], 1)

            for i in range(NT):
                dve.sem_inc(S[f"st_y{i}"], 16)
                indices(i, i)
            with dve.Fori(0, B - 1) as b:
                for i in range(NT):
                    combine(b, i)
                    indices(NT * b + (NT + i), i)
            for i in range(NT):
                combine(B - 1, i)

        @block.tensor
        def _(pe):
            mm = nc.tensor

            pe.wait_ge(S["m_silu"], 1)
            pe.wait_ge(S["c_shape"], 2)
            for k in range(KC):
                last = mm.transpose(ps_o[:, B * k:B * k + B], c_sb[:, P * k:P * k + P], ident[0:B, 0:B])
            last.then_inc(S["m_tp"], 1)
            pe.wait_ge(S["m_ct"], 1)
            pe.wait_ge(S["ld_wmod"], 16)
            for i in range(4):
                for k in range(KC):
                    mm.matmul(ps_o[:, 64 + B * i:64 + B * i + B], wmod_sb[:, k, P * i:P * i + P], c_cols[:, k],
                             start=(k == 0), stop=(k == KC - 1))
            for i, ps in enumerate((ps_b, ps_c)):
                for k in range(KC):
                    last = mm.matmul(ps[0:B, :], c_cols[:, k], wmod_sb[:, k, 512 * (i + 1):512 * (i + 2)],
                                    start=(k == 0), stop=(k == KC - 1))
            last.then_inc(S["m_mm"], 1)

            def norm1_transpose(b):
                pe.wait_ge(S["z1_ready"], b + 1)
                seen(pe, S["h2T_ready"], b - 1)
                seen(pe, S["rr_a"], b)
                seen(pe, S["klam_ready"], b)
                for j in range(KC):
                    for i in range(NT):
                        last = mm.transpose(ps_a[:, N * j + T * i:N * j + T * i + T], z1[:, i, P * j:P * j + P], ident[:])
                last.then_inc(S["xt_done"], 1)

            pe.wait_ge(S["q_tern"], 1)
            for k in range(KC):
                for o in range(4):
                    mm.transpose(ps_s[:, k, P * o:P * o + P], qkv_raw[:, o, P * k:P * k + P], ident[:])
                for o in range(2):
                    mm.transpose(ps_s[:, 2, C * k + P * o:C * k + P * o + P], qkv_raw[:, 4 + o, P * k:P * k + P], ident[:])
                for o in range(2):
                    last = mm.transpose(ps_s[:, 3, C * k + P * o:C * k + P * o + P], proj_raw[:, o, P * k:P * k + P], ident[:])
            last.then_inc(S["q_tp"], 1)
            pe.wait_ge(S["q_w"], 1)
            pe.wait_ge(S["m_rows0"], 1)
            pe.wait_ge(S["m_cols"], 1)
            pe.wait_ge(S["c_misc"], 1)
            pe.wait_ge(S["ld_gate"], 16)
            pe.wait_ge(S["ld_shared"], 48)
            norm1_transpose(0)

            def project_qkv(b):
                pe.wait_ge(S["hT_ready"], b + 1)
                pe.wait_ge(S["hsq_ready"], b + 1)
                for j in range(KC):
                    for k in range(KC):
                        last = mm.matmul(ps_a[:, N * j:N * j + N], w_qkv[:, k, P * j:P * j + P], hT[:, k],
                                        start=(k == 0), stop=(k == KC - 1))
                last.then_inc(S["q_done"], 1)
                seen(pe, S["lg_exp"], b - 1)
                seen(pe, S["state_ready"], b)
                for j in range(KC):
                    for k in range(KC):
                        last = mm.matmul(ps_b[:, N * j:N * j + N], w_qkv[:, k, C + P * j:C + P * j + P], hT[:, k],
                                        start=(k == 0), stop=(k == KC - 1))
                last.then_inc(S["k_done"], 1)
                pe.wait_ge(S["q_taken"], b + 1)
                for i in range(NT):
                    for k in range(KC):
                        last = mm.matmul(ps_a[:, C + i:C + i + 1], hsq[:, k, T * i:T * i + T], stat_w[:, 0, 0:1],
                                        start=(k == 0), stop=(k == KC - 1))
                for k in range(KC):
                    last = mm.matmul(ps_a[:, 0:C], hT[:, k, 0:T], w_qkv[:, k, C:2 * C], start=(k == 0), stop=(k == KC - 1))
                last.then_inc(S["kt_done"], 1)
                seen(pe, S["sh_ready"], b - 1)
                seen(pe, S["v_taken"], b)
                for i in range(NT):
                    for k in range(KC):
                        last = mm.matmul(ps_c[:, C * i:C * i + C], hT[:, k, T * i:T * i + T], w_qkv[:, k, 2 * C:3 * C],
                                        start=(k == 0), stop=(k == KC - 1))
                last.then_inc(S["v_done"], 1)

            def first_state(b):
                pe.wait_ge(S["klam_ready"], b + 1)
                pe.wait_ge(S["v_taken"], b + 1)
                pe.wait_ge(S["k_taken"], b + 1)
                for j in range(KC):
                    last = mm.matmul(ps_b[:, P * j:P * j + P], k_lam[:, P * j:P * j + P], v_full[:, P * j:P * j + P],
                                    start=True, stop=True)
                last.then_inc(S["kv_done"], 1)

            def out_stats(b):
                pe.wait_ge(S["o_taken"], b + 1)
                for i in range(NT):
                    for k in range(KC):
                        last = mm.matmul(ps_o[:, i:i + 1], osq[:, i, k], stat_w[:, k, 1:2],
                                        start=(k == 0), stop=(k == KC - 1))
                last.then_inc(S["os_done"], 1)

            def project_out(b):
                seen(pe, S["sh_ready"], b)
                seen(pe, S["v_taken"], min(b + 2, B) if isinstance(b, int) else b + 2)
                for i in range(NT):
                    for k in range(KC):
                        last = mm.matmul(ps_c[:, C * i:C * i + C], oT[:, i, k], w_proj[:, k],
                                        start=(k == 0), stop=(k == KC - 1))
                last.then_inc(S["proj_done"], 1)

            def scores(b, tile):
                if tile == 0:
                    pe.wait_ge(S["k_taken"], b + 1)
                    pe.wait_ge(S["q_taken"], b + 1)
                    seen(pe, S["mk1"], b)
                else:
                    pe.wait_ge(S["mk0"], b + 1)
                ts = slice(T * tile, T * tile + T)
                for j in range(KC):
                    for q in range(2):
                        col = T * (2 * j + q)
                        for r in range(4):
                            last = mm.matmul(ps_s[:, r, col:col + T], k_eo[q][32 * r:32 * r + 32, j, ts],
                                             qT[32 * r:32 * r + 32, j, ts], start=True, stop=True)
                last.then_inc(S[f"sc{tile}"], 1)

            def values(b, tile):
                if tile == 0:
                    seen(pe, S["f1"], b)
                    seen(pe, S["slots_ready"], b - 1)
                    pe.wait_ge(S["v_taken"], b + 1)
                else:
                    pe.wait_ge(S["state_ready"], b + 1)
                    pe.wait_ge(S["qlam_ready"], b + 1)
                pe.wait_ge(S[f"mk{tile}"], b + 1)
                for j in range(KC):
                    dst = ps_o[:, 256 * tile + T * j:256 * tile + T * j + T]
                    if tile:
                        mm.matmul(dst, state[:, j], q_lam[:, j], start=True, stop=False, skip_group_check=True)
                    for q in range(2):
                        for r in range(4):
                            vq = v_eo[q][:, tile, 4 * j + r].rearrange("p q d -> p (q d)")
                            last = mm.matmul(dst[32 * r:32 * r + 32], vq, scm[:, r, j, q],
                                             start=(q == 0 and not tile), stop=(q == 1), skip_group_check=True)
                last.then_inc(S[f"pv{tile}"], 1)

            def norm2_transpose(b, par):
                pe.wait_ge(S["h2_ready"], b + 1)
                for j in range(KC):
                    for i in range(NT):
                        last = mm.transpose(ps_a[:, N * j + T * i:N * j + T * i + T], h2row[par][:, i, P * j:P * j + P],
                                           ident[:])
                last.then_inc(S["h2t_done"], 1)

            def logits(b):
                pe.wait_ge(S["h2T_ready"], b + 1)
                seen(pe, S["state_ready"], min(b + 2, B) if isinstance(b, int) else b + 2)
                seen(pe, S["sh_gated"], b)
                for i in range(NT):
                    for k in range(KC):
                        last = mm.matmul(ps_b[:, E * i:E * i + E], h2T[:, k, T * i:T * i + T], gate_sb[:, k],
                                        start=(k == 0), stop=(k == KC - 1))
                last.then_inc(S["lg_done"], 1)

            def gate_up(b):
                pe.wait_ge(S["attn_ready"], b + 1)
                for g_ in range(2):
                    for k in range(KC):
                        last = mm.matmul(ps_c[0:F, N * g_:N * g_ + N], ws_gu[:, k, g_], h2T[:, k],
                                        start=(k == 0), stop=(k == KC - 1))
                last.then_inc(S["gu_done"], 1)

            def shared_down(b):
                pe.wait_ge(S["sh_ready"], b + 1)
                pe.wait_ge(S["lg_exp"], b + 1)
                seen(pe, S["state_ready"], min(b + 3, B) if isinstance(b, int) else b + 3)
                for i in range(NT):
                    last = mm.matmul(ps_b[:, C * i:C * i + C], s_h[:, T * i:T * i + T], ws_d[:], start=True, stop=True)
                last.then_inc(S["dn_done"], 1)

            def positions(b):
                seen(pe, S["f1"], min(b + 2, B) if isinstance(b, int) else b + 2)
                pe.wait_ge(S["selbf_ready"], b + 1)
                pe.wait_ge(S["carry_ready"], b + 1)
                for i in range(NT):
                    mm.matmul(ps_o[:, E * (i + 1):E * (i + 2)], upper[:], sel_bf[:, i], start=True, stop=False)
                    last = mm.matmul(ps_o[:, E * (i + 1):E * (i + 2)], ones_bf[:], carry[:, i], start=False, stop=True)
                last.then_inc(S["pos_done"], 1)

            def step(s, par, h, hp):
                cur, nxt = not at_end(s, B), not at_end(s, B - 1)
                has_prev = not before(s, 1) and not at_end(s, B + 1)
                has_two = not before(s, 2)
                if has_prev:
                    out_stats(s - 1)
                if cur:
                    project_qkv(s)
                    scores(s, 0)
                if has_two:
                    positions(s - 2)
                if has_prev:
                    project_out(s - 1)
                if cur:
                    first_state(s)
                    scores(s, 1)
                if has_two:
                    shared_down(s - 2)
                if cur:
                    values(s, 0)
                if has_prev:
                    norm2_transpose(s - 1, 1 - par)
                if cur:
                    values(s, 1)
                if has_prev:
                    logits(s - 1)
                if nxt:
                    norm1_transpose(s + 1)
                if has_prev:
                    gate_up(s - 1)

            token_steps(pe, step)

            pe.wait_ge(S["pre_ready"], B)
            pe.wait_ge(S["slots_ready"], B)

            def pair_step(q, i, m):
                if not at_end(q, PAIRS - 1):
                    n = (m + 1) % NBUF
                    pe.wait_ge(S[f"ld_xr{n}"], 16 * (turn(i, m + 1, NBUF) + 1))
                    seen(pe, S["xt_taken"], q)
                    for k in range(KC):
                        last = mm.transpose(e_xt[n][:, P * k:P * k + P], xr[n][:, k:C:KC], ident[:])
                    last.then_inc(S["xtp"], 1)
                if not before(q, 0) and not at_end(q, PAIRS):
                    n, slot = m % NBUF, m % RING
                    pe.wait_ge(S["xt_taken"], q + 1)
                    pe.wait_ge(S["pairs_landed"], q + 1)
                    for g_, w in enumerate((eg, eu)):
                        for half in range(2):
                            for k in range(KC):
                                col = P * g_ + SLOTS * half
                                last = mm.matmul(e_gups[n][0:F, col:col + SLOTS], w[:, slot, half, k],
                                                 xt[n][:, k, SLOTS * half:SLOTS * half + SLOTS],
                                                 start=(k == 0), stop=(k == KC - 1))
                    last.then_inc(S["gup"], 1)
                if not before(q, 1):
                    n, slot = (m - 1) % NBUF, (m - 1) % RING
                    pe.wait_ge(S["gh_ready"], q)
                    for half in range(2):
                        last = mm.matmul(e_dn[n][SLOTS * half:SLOTS * half + SLOTS, :],
                                         e_h[n][:, SLOTS * half:SLOTS * half + SLOTS],
                                         ed[:, slot, half], start=True, stop=True)
                    last.then_inc(S["dnp"], 1)

            pair_steps(pe, pair_step)


_INS = ["L0_attn_x", "L0_attn_qkv_w", "L0_attn_qkv_norm_w", "L0_attn_proj_w", "L0_attn_proj_norm_w",
        "L0_attn_norm_w", "L0_attn_s", "L0_ffn_gate_w", "L0_ffn_bias", "L0_ffn_w_gate", "L0_ffn_w_up",
        "L0_ffn_w_down", "L0_ffn_ws_gate", "L0_ffn_ws_up", "L0_ffn_ws_down", "L0_c", "L0_wmod"]


def kernel(**inputs):
    import numpy as np
    import concourse.bacc as bacc
    from concourse.bass_utils import run_bass_kernel_spmd

    nc = bacc.Bacc("TRN2", target_bir_lowering=False, num_devices=1)
    arrays, args = {}, []
    for name in _INS:
        a = np.ascontiguousarray(inputs[name])
        arrays[f"in_{name}"] = a
        args.append(nc.dram_tensor(f"in_{name}", a.shape, mybir.dt.from_np(a.dtype), kind="ExternalInput").ap())
    args.append(nc.dram_tensor("out", (B, N, C), F32, kind="ExternalOutput").ap())
    adaln_attention_moe(nc, *args)
    r = run_bass_kernel_spmd(nc, [arrays], core_ids=[0])
    return r.results[0]["out"]
```

```python
from contextlib import ExitStack

import concourse.bass as bass
from concourse import mybir

ALU = mybir.AluOpType
ACT = mybir.ActivationFunctionType
F32 = mybir.dt.float32
BF16 = mybir.dt.bfloat16
U32 = mybir.dt.uint32
AX_X = mybir.AxisListType.X
RADD = bass.bass_isa.ReduceOp.add

P = 128
B, N, C = 8, 256, 256
HEADS, HD = 16, 16
T = 128
NT = N // T
KC = C // P
HPJ = HEADS // KC
E, TOPK, F = 64, 6, 96
G, KG = 8, 4
EG = E // G
CAP = 2 * (256 * TOPK // E)
SLOTS = 64
ROWS = E * SLOTS
KEYS = C + E
TKEY = KEYS + 8
ROWW = 336
YROWS = B * N * TOPK
PAIRS = E // 2
RING = 10
YBUF = 4
NBUF = 2
EPS_F = 1.1920928955078125e-07
EPS_LN = 1e-5
EPS_O = 1e-6
ROUTE_SCALE = 2.5
MAGIC = 12582912.0
ROUTE_STEPS = 17
OUT = -1.0e30
PICK = -2.0e30


def spread(ap, at, n):
    dims = [list(d) for d in ap.ap]
    dims.insert(at, [0, n])
    return bass.AP(ap.tensor, ap.offset, dims)


def seen(eng, sem, count):
    if isinstance(count, int) and count <= 0:
        return
    eng.wait_ge(sem, count)


def adaln_attention_moe(nc, x, qkv_w, qkv_norm_w, proj_w, proj_norm_w, norm_w, s, gate_w, bias,
                        w_gate, w_up, w_down, ws_gate, ws_up, ws_down, c, wmod, out):
    with ExitStack() as ctx:
        def sb(name, shape, dt=F32):
            return ctx.enter_context(nc.sbuf_tensor(name, shape, dt))

        def sem(name):
            return ctx.enter_context(nc.semaphore(name))

        rows_dram = nc.dram_tensor("rows_dram", [ROWS, ROWW], F32, kind="Internal").ap()
        y_dram = nc.dram_tensor("y_dram", [YROWS, C], F32, kind="Internal").ap()
        mod_dram = nc.dram_tensor("mod_dram", [B, 4 * C], F32, kind="Internal").ap()

        ident = sb("ident", [P, P])
        upper = sb("upper", [P, P], BF16)
        ones_bf = sb("ones_bf", [P, P], BF16)
        half_exp = sb("half_exp", [P, 2, 2])
        diff = sb("diff", [P, T])
        t_left = sb("t_left", [P, 1])
        part_ix = sb("part_ix", [P, 1], U32)
        part_bit = sb("part_bit", [P, 1], U32)
        y_zeros = sb("y_zeros", [P, 1024])
        slot_key = sb("slot_key", [P, PAIRS])
        token_key = sb("token_key", [P, B * NT])
        trow = sb("trow", [P, T])
        decay = sb("decay", [P, 4, KC, 2, T])
        s_row = sb("s_row", [P, HEADS])
        s_part = sb("s_part", [P, KC])
        neg_s = sb("neg_s", [P, HEADS])
        neg_s_part = sb("neg_s_part", [P, KC])
        lam_q = sb("lam_q", [P, KC, T])
        lam_rev = sb("lam_rev", [P, HEADS])
        even_odd = sb("even_odd", [P, 2])
        head_block = sb("head_block", [P, P])
        w_qkv = sb("w_qkv", [P, KC, 3 * C])
        w_proj = sb("w_proj", [P, KC, C])
        norm_cols = sb("norm_cols", [P, 3, KC])
        q_scale = sb("q_scale", [P, 2, KC])
        stat_w = sb("stat_w", [P, KC, 2])
        gate_sb = sb("gate_sb", [P, KC, E])
        ws_gu = sb("ws_gu", [P, KC, 2, F])
        ws_d = sb("ws_d", [F, C])
        bias_row = sb("bias_row", [P, E])
        row_base = sb("row_base", [P, E])
        mod_cols = sb("mod_cols", [P, 4, B])
        abs_sum = sb("abs_sum", [P, 2])
        abs_all = sb("abs_all", [P, 2])
        w_mean = sb("w_mean", [P, 2])
        w_inv = sb("w_inv", [P, 2])
        c_sb = sb("c_sb", [B, C])
        c_sig = sb("c_sig", [B, C])
        c_cols = sb("c_cols", [P, KC, B])
        mod_rows = sb("mod_rows", [B, 4 * C])
        sign_rows = sb("sign_rows", [B, 2, C])
        abs_rows = sb("abs_rows", [B, 2, C])

        xa = sb("xa", [P, NT, C])
        xres = sb("xres", [P, NT, C])
        mod_b = [sb(f"mod_b{i}", [P, 3, C]) for i in range(2)]
        gb_all = sb("gb_all", [P, B, C])
        mod_cur = [sb(f"mod_cur{i}", [P, 4]) for i in range(2)]
        bn1 = sb("bn1", [P, NT, 6])
        mv1 = sb("mv1", [P, NT, 2])
        ve1 = sb("ve1", [P, NT])
        rstd1 = sb("rstd1", [P, NT])
        z1 = sb("z1", [P, NT, C])
        hT = sb("hT", [P, KC, N])
        hsq = sb("hsq", [P, KC, N])
        rr_t = sb("rr_t", [P, NT])
        rr2 = sb("rr2", [P, NT])
        a16 = [sb(f"a16_{i}", [P, NT]) for i in range(2)]
        qT = sb("qT", [P, KC, N])
        k_eo = [sb(f"k_eo{i}", [P, KC, N]) for i in range(2)]
        v_eo = [sb(f"v_eo{i}", [P, NT, HEADS // 2, 2, HD]) for i in range(2)]
        v_full = sb("v_full", [P, C])
        k_lam = sb("k_lam", [P, C])
        q_lam = sb("q_lam", [P, KC, T])
        state = sb("state", [P, KC, P])
        scm = sb("scm", [P, 4, KC, 2, T])
        oT = sb("oT", [P, NT, KC, T])
        osq = sb("osq", [P, NT, KC, T])
        fin = sb("fin", [P, 5, NT])
        fac = sb("fac", [P, NT])
        attn = sb("attn", [P, NT, C])
        x2 = [sb(f"x2_{i}", [P, NT, C]) for i in range(2)]
        bn2 = sb("bn2", [P, NT, 6])
        mv2 = sb("mv2", [P, NT, 2])
        ve2 = sb("ve2", [P, NT])
        rstd2 = sb("rstd2", [P, NT])
        z2 = sb("z2", [P, NT, C])
        h2s = sb("h2s", [P, NT, C])
        h2row = [sb(f"h2row{i}", [P, NT, ROWW]) for i in range(2)]
        h2T = sb("h2T", [P, KC, N])
        pre = sb("pre", [P, B * NT, C])
        r_exp = sb("r_exp", [P, NT, E])
        r_den = sb("r_den", [P, NT, E])
        r_sig = sb("r_sig", [P, NT, E])
        r_sc = sb("r_sc", [P, NT, E])
        g_top = sb("g_top", [P, NT * G, 8])
        g_sum = sb("g_sum", [P, NT, 2 * G])
        g_best = sb("g_best", [P, NT, 8])
        g_rep = sb("g_rep", [P, NT, 2 * G])
        g_pick = sb("g_pick", [P, NT, G])
        g_pen = sb("g_pen", [P, NT, G])
        e_val = sb("e_val", [P, NT, E])
        e_best = sb("e_best", [P, NT, 8])
        e_rep = sb("e_rep", [P, NT, E])
        sel = sb("sel", [P, NT, E])
        sel_bf = sb("sel_bf", [P, NT, E], BF16)
        carry = sb("carry", [P, NT, E], BF16)
        w_raw = sb("w_raw", [P, NT, E])
        w_sum = sb("w_sum", [P, NT])
        w_rec = sb("w_rec", [P, NT])
        keep = sb("keep", [P, NT, E])
        row_key = sb("row_key", [P, NT, E])
        key = sb("key", [P, NT, E])
        slot_ix = [sb(f"slot_ix{i}", [P, NT, 8], U32) for i in range(2)]
        s_exp = sb("s_exp", [F, N])
        s_gu = sb("s_gu", [F, N])
        s_h = sb("s_h", [F, N])
        sh_g = sb("sh_g", [P, NT, C])

        eg = sb("eg", [P, RING, 2, KC, F])
        eu = sb("eu", [P, RING, 2, KC, F])
        ed = sb("ed", [F, RING, 2, C])
        pad = sb("pad", [P, 1])
        pool_pad = sb("pool_pad", [P, 5])
        wcol = [sb(f"wcol{i}", [P, 1]) for i in range(NBUF)]
        larger = sb("larger", [P, 8])
        rank = [sb(f"rank{i}", [P, 1]) for i in range(NBUF)]
        y_base = [sb(f"y_base{i}", [P, 1]) for i in range(NBUF)]
        y_pos = sb("y_pos", [P, 1])
        y_row = [sb(f"y_row{i}", [P, 1], U32) for i in range(NBUF)]
        xr = [h2row[0][:, 0], h2row[1][:, 0]]
        xt = [attn[:, i].rearrange("p (k r) -> p k r", k=KC) for i in range(NBUF)]
        e_exp = [s_exp[:, 0:P], s_exp[:, P:N]]
        e_gu = [s_gu[:, 0:P], s_gu[:, P:N]]
        e_h = [s_h[:, 0:P], s_h[:, P:N]]
        e_out = [oT[:, i].rearrange("p j t -> p (j t)") for i in range(NBUF)]
        qkv_raw = eg[:, 0:4].rearrange("p a b k f -> p (a b k f)")[:, 0:6 * C].rearrange("p (a c) -> p a c", a=6)
        proj_raw = eg[:, 4:6].rearrange("p a b k f -> p (a b k f)")[:, 0:2 * C].rearrange("p (a c) -> p a c", a=2)
        wmod_sb = eu[:, 0:8].rearrange("p a b k f -> p (a b k f)").rearrange("p (k n) -> p k n", k=2)
        zeros = scm[:].rearrange("p r j q t -> p (r j q t)")[:, 0:4 * ROWW]
        y_in = [w[:, 4 * i:4 * i + 4].rearrange("p a b k f -> p (a b k f)") for w in (eg, eu) for i in range(2)]
        ysum = [z1[:, i] for i in range(2)]
        ygb = [h2s[:, i] for i in range(2)]
        yout = [z2[:, i] for i in range(2)]

        ps_s = ctx.enter_context(nc.psum_tensor("ps_s", [P, 4, 512], F32))
        ps_o = ctx.enter_context(nc.psum_tensor("ps_o", [P, 512], F32))
        ps_a = ctx.enter_context(nc.psum_tensor("ps_a", [P, 512], F32))
        ps_b = ctx.enter_context(nc.psum_tensor("ps_b", [P, 512], F32))
        ps_c = ctx.enter_context(nc.psum_tensor("ps_c", [P, 512], F32))
        e_xt = [ps_a[:, 0:C], ps_b[:, 0:C]]
        e_gups = [ps_s[:, i, 0:2 * P] for i in range(NBUF)]
        e_dn = [ps_c[:, 0:C], ps_o[:, 0:C]]

        names = """
        prologue_step
        silu_step
        shared_step
        slot_step
        factor_step
        route
        ld_small ld_norms ld_c ld_wmod ld_qkvw ld_projw ld_gate ld_shared ld_xa ld_xres ld_modb0 ld_modb1 ld_gb
        e_free st_fill ld_y0 ld_y1 ld_y2 ld_y3 y_taken ld_xr0 ld_xr1 st_mod st_zero st_rows0 st_rows1 st_put0 st_put1
        st_y0 st_y1
        c_zero c_fill c_shape c_neg c_decay0 c_decay c_lam   c_misc
        q_abs q_all     q_tern q_tp q_sc q_w
        m_exp   m_silu m_tp m_ct m_mm m_cols m_rows0    m_rows
        ln1_step ln1_ve ln1_rstd z1_ready xt_done mod_cur_ready hT_ready hsq_ready
        q_done q_taken k_done k_taken v_done v_taken kt_done rr_a rr2_ready a16_ready
        klam_ready qlam_ready kv_done state_ready
        sc0 sc1 mk0 mk1 pv0 pv1 o_taken
        os_done f1   f5 f_ready proj_done attn_ready x2_ready
        ln2_step ln2_ve ln2_rstd z2_ready h2_mul h2_ready h2t_done h2T_ready
        lg_done lg_exp r1               selbf_ready
           w_ready carry_ready
        gu_done sg_exp sg1   sh_ready dn_done sh_gated pre_ready
        pos_done    slots_ready
        xtp xt_taken wcol_ready gup ge_exp    gh_ready dnp e_evac
        settled put_step put_pos put_row rank_step y_sum y_gb y_out
        """.split() + [f"ld_slot{i}" for i in range(RING)]
        S = {n: sem(n) for n in names}

        block = ctx.enter_context(nc.Block())

        x_t = x.rearrange("b (i p) c -> b p i c", p=P)
        out_t = out.rearrange("b (i p) c -> (b i) p c", p=P)
        wg_v = w_gate.rearrange("(r e) (p k) f -> r p e k f", e=2, k=KC)
        wu_v = w_up.rearrange("(r e) (p k) f -> r p e k f", e=2, k=KC)
        wd_v = w_down.rearrange("(r e) f c -> r f e c", e=2)
        rows_v = rows_dram.rearrange("(r p) c -> r p c", p=P)
        fill_v = y_dram.rearrange("(b p r) c -> b p (r c)", b=B, p=P).rearrange("b p (a n) -> b p a n", n=1024)
        y_v = y_dram.rearrange("(t p j) c -> t p (j c)", p=P, j=TOPK)

        def token_steps(eng, step):
            for s in range(3):
                step(s, s % 2, s // 2, max(s - 1, 0) // 2)
            with eng.Fori(0, (B - 4) // 2) as i:
                step(2 * i + 3, 1, i + 1, i + 1)
                step(2 * i + 4, 0, i + 2, i + 1)
            step(B - 1, 1, (B - 1) // 2, (B - 2) // 2)
            step(B, 0, B // 2, (B - 1) // 2)
            step(B + 1, 1, (B + 1) // 2, B // 2)

        def pair_steps(eng, step):
            step(-1, 0, -1)
            step(0, 0, 0)
            with eng.Fori(0, (PAIRS - 2) // RING) as i:
                for m in range(1, 1 + RING):
                    step(RING * i + m, i, m)
            step(PAIRS - 1, 0, PAIRS - 1)
            step(PAIRS, 0, PAIRS)

        def turn(i, m, n):
            return RING // n * i + m // n

        def before(v, start):
            return isinstance(v, int) and v < start

        def at_end(v, end):
            return isinstance(v, int) and v >= end

        @block.sync
        def _(sp):
            sp.dma_start(c_sb[:], c).then_inc(S["ld_c"], 16)
            sp.dma_start(s_row[:], spread(s, 0, P)).then_inc(S["ld_small"], 16)
            for j in range(KC):
                for a in range(HPJ):
                    sp.dma_start(s_part[HD * a:HD * a + HD, j:j + 1], spread(s[HPJ * j + a:HPJ * j + a + 1], 0, HD)
                                 ).then_inc(S["ld_small"], 16)
            sp.dma_start(xa[:], x_t[0]).then_inc(S["ld_xa"], 16)
            sp.dma_start(gate_sb[:], gate_w.rearrange("(k p) e -> p k e", p=P)).then_inc(S["ld_gate"], 16)
            sp.dma_start(ws_gu[:, :, 0], ws_gate.rearrange("(k p) f -> p k f", p=P)).then_inc(S["ld_shared"], 16)
            sp.dma_start(ws_gu[:, :, 1], ws_up.rearrange("(k p) f -> p k f", p=P)).then_inc(S["ld_shared"], 16)
            sp.dma_start(ws_d[:], ws_down).then_inc(S["ld_shared"], 16)
            sp.wait_ge(S["c_zero"], 1)
            sp.dma_start(rows_dram.rearrange("(p r) c -> p (r c)", p=P).rearrange("p (a n) -> p a n", n=4 * ROWW),
                         spread(zeros, 1, ROWS // P // 4)).then_inc(S["st_zero"], 16)
            sp.wait_ge(S["m_rows"], 1)
            sp.dma_start(mod_dram, mod_rows[:]).then_inc(S["st_mod"], 16)
            sp.wait_ge(S["st_mod"], 16)
            sp.dma_start(gb_all[:], spread(mod_dram[:, 3 * C:4 * C], 0, P)).then_inc(S["ld_gb"], 16)
            sp.wait_ge(S["q_tp"], 1)
            sp.wait_ge(S["m_mm"], 1)

            def load_pair(p, slot):
                sp.dma_start(eg[:, slot], wg_v[p]).then_inc(S[f"ld_slot{slot}"], 16)
                sp.dma_start(eu[:, slot], wu_v[p]).then_inc(S[f"ld_slot{slot}"], 16)
                sp.dma_start(ed[:, slot], wd_v[p]).then_inc(S[f"ld_slot{slot}"], 16)

            def step(s, par, h, hp):
                if at_end(s, B):
                    return
                if not at_end(s, B - 1):
                    sp.wait_ge(S["z1_ready"], s + 1)
                    sp.dma_start(xa[:], x_t[s + 1]).then_inc(S["ld_xa"], 16)
                seen(sp, S["h2_ready"], s - 1)
                sp.dma_start(mod_b[par][:].rearrange("p a c -> p (a c)"),
                             spread(mod_dram[s, 0:3 * C], 0, P)).then_inc(S[f"ld_modb{par}"], 16)
                if before(s, 3):
                    for p in range(RING * s // 3, RING * (s + 1) // 3):
                        load_pair(p, p)
                seen(sp, S["x2_ready"], s)
                sp.dma_start(xres[:], x_t[s]).then_inc(S["ld_xres"], 16)

            token_steps(sp, step)

            for par in range(2):
                sp.wait_ge(S[f"st_rows{par}"], 16 * B // 2 * NT * TOPK)
            for q in range(NBUF):
                sp.dma_start(xr[q], rows_v[q]).then_inc(S[f"ld_xr{q}"], 16)

            def load_rows(q, buf):
                sp.wait_ge(S["xtp"], q - NBUF + 1)
                sp.wait_ge(S["wcol_ready"], q - NBUF + 1)
                sp.dma_start(xr[buf], rows_v[q]).then_inc(S[f"ld_xr{buf}"], 16)

            def load_ahead(q, slot):
                sp.wait_ge(S["dnp"], q - LAG + 1)
                load_pair(q + (RING - LAG), slot)

            LAG = 4
            for q in range(NBUF, LAG):
                load_rows(q, q % NBUF)
            TURNS = (PAIRS - RING) // RING
            with sp.Fori(0, TURNS) as i:
                for m in range(LAG, LAG + RING):
                    load_rows(RING * i + m, m % NBUF)
                    load_ahead(RING * i + m, m - LAG)
            for q in range(RING * TURNS + LAG, PAIRS):
                load_rows(q, q % NBUF)
                if q + RING - LAG < PAIRS:
                    load_ahead(q, (q - LAG) % RING)

            for n in range(NBUF):
                sp.wait_ge(S[f"st_put{n}"], 16 * PAIRS // NBUF)

            def load_y(t, buf):
                sp.dma_start(y_in[buf], y_v[t]).then_inc(S[f"ld_y{buf}"], 16)

            def store_out(t, i):
                sp.wait_ge(S["y_out"], t + 1)
                sp.dma_start(out_t[t], yout[i]).then_inc(S[f"st_y{i}"], 16)

            for t in range(YBUF):
                load_y(t, t)
            with sp.Fori(0, B * NT // YBUF - 1) as i:
                for m in range(YBUF):
                    sp.wait_ge(S["y_sum"], YBUF * i + (m + 1))
                    load_y(YBUF * i + (m + YBUF), m)
                    store_out(YBUF * i + m, m % NT)
            for t in range(B * NT - YBUF, B * NT):
                store_out(t, t % NT)
            for i in range(NT):
                sp.wait_ge(S[f"st_y{i}"], 16 * B + 16)

        @block.gpsimd
        def _(pool):
            g = nc.gpsimd
            last_row = g.to_reg(ROWS - 1)
            g.memset(zeros, 0.0).then_inc(S["c_zero"], 1)
            g.memset(ident[:], 0.0)
            g.memset(upper[:], 1.0)
            g.memset(head_block[:], 1.0)
            g.memset(half_exp[:, 0], -0.5)
            g.memset(half_exp[:, 1], 0.5)
            g.memset(y_zeros[:], 0.0)
            for i in range(2):
                g.memset(v_eo[i][:], 0.0)
            g.memset(carry[:], 0.0)
            g.memset(stat_w[:], 1.0)
            g.iota(part_ix[:], pattern=[[0, 1]], base=0, channel_multiplier=1)
            g.iota(t_left[:], pattern=[[0, 1]], base=T, channel_multiplier=-1, allow_small_or_imprecise_dtypes=True)
            g.iota(trow[:], pattern=[[1, T]], base=0, channel_multiplier=0, allow_small_or_imprecise_dtypes=True)
            g.iota(slot_key[:], pattern=[[-P, PAIRS]], base=ROWS, channel_multiplier=-1,
                   allow_small_or_imprecise_dtypes=True)
            g.iota(token_key[:], pattern=[[-P * TOPK, B * NT]], base=YROWS, channel_multiplier=-TOPK,
                   allow_small_or_imprecise_dtypes=True)
            for i in range(2):
                g.memset(h2row[i][:, :, TKEY:ROWW], 0.0)
            g.iota(row_base[:], pattern=[[-SLOTS, E]], base=ROWS, channel_multiplier=0,
                   allow_small_or_imprecise_dtypes=True)
            g.iota(diff[:], pattern=[[1, T]], base=0, channel_multiplier=-1,
                   allow_small_or_imprecise_dtypes=True).then_inc(S["c_fill"], 1)
            pool.wait_ge(S["c_fill"], 1)
            g.affine_select(out=ident[:], in_=ident[:], pattern=[[-1, P]], compare_op=ALU.not_equal, fill=1.0,
                            base=0, channel_multiplier=1)
            g.affine_select(out=upper[:], in_=upper[:], pattern=[[1, P]], compare_op=ALU.is_ge, fill=0.0,
                            base=-1, channel_multiplier=-1)
            hb = head_block[:].rearrange("p (g e) -> p g e", e=HD)
            g.affine_select(out=hb, in_=hb, pattern=[[-HD, HPJ], [0, HD]], compare_op=ALU.is_ge, fill=0.0,
                            base=0, channel_multiplier=1).then_inc(S["c_shape"], 1)
            pool.wait_ge(S["c_shape"], 1)
            g.affine_select(out=hb, in_=hb, pattern=[[HD, HPJ], [0, HD]], compare_op=ALU.is_ge, fill=0.0,
                            base=HD - 1, channel_multiplier=-1).then_inc(S["c_shape"], 1)
            pool.wait_ge(S["q_abs"], 1)
            g.partition_all_reduce(abs_all[:], abs_sum[:], P, RADD).then_inc(S["q_all"], 1)
            pool.wait_ge(S["c_decay0"], 1)
            dv = decay[:].rearrange("p r j q t -> p (r j q) t")
            g.affine_select(out=dv, in_=dv, pattern=[[0, HEADS], [1, T]], compare_op=ALU.is_ge, fill=0.0,
                            base=0, channel_multiplier=-1).then_inc(S["c_decay"], 1)

            def power(out_, in_, which, ready, done, n):
                pool.wait_ge(S[ready], n)
                g.tensor_tensor(out_, in_, half_exp[:, which], ALU.pow).then_inc(S[done], 1)

            def settle(at):
                return g.tensor_tensor(pool_pad[:, at:at + 1], half_exp[:, 0, 0:1], half_exp[:, 0, 0:1], ALU.add)

            def dispatch(b, par, tile):
                if tile == 0:
                    pool.wait_ge(S["slots_ready"], b + 1)
                    pool.wait_ge(S["w_ready"], b + 1)
                    pool.wait_ge(S["h2_ready"], b + 1)
                    settle(par)
                for j in range(TOPK):
                    g.indirect_dma_start(
                        out=rows_dram, out_offset=bass.IndirectOffsetOnAxis(ap=slot_ix[par][:, tile, j:j + 1], axis=0),
                        in_=h2row[par][:, tile, :], in_offset=None, bounds_check=last_row,
                        oob_is_err=False).then_inc(S[f"st_rows{par}"], 16)

            def step(s, par, h, hp):
                if not at_end(s, B - 1):
                    power(rstd1[:], ve1[:], 0, "ln1_ve", "ln1_rstd", s + 2)
                if not before(s, 1) and not at_end(s, B + 1):
                    power(fac[:], fin[:, 4], 1, "f5", "f_ready", s)
                if not before(s, 3):
                    dispatch(s - 3, 1 - par, 0)
                    dispatch(s - 3, 1 - par, 1)
                if not before(s, 1) and not at_end(s, B + 1):
                    power(rstd2[:], ve2[:], 0, "ln2_ve", "ln2_rstd", s)
                if not at_end(s, B):
                    pool.wait_ge(S["q_taken"], s + 1)
                    seen(pool, S["pv1"], s)
                    g.tensor_tensor(q_lam[:], qT[:, :, T:2 * T], lam_q[:], ALU.mult).then_inc(S["qlam_ready"], 1)
                if not before(s, 1) and not at_end(s, B + 1):
                    pool.wait_ge(S["z2_ready"], s)
                    pool.wait_ge(S[f"ld_modb{1 - par}"], 16 * (hp + 1))
                    g.tensor_tensor(h2s[:], z2[:], spread(mod_b[1 - par][:, 2], 1, NT), ALU.mult).then_inc(S["h2_mul"], 1)
                    pool.wait_ge(S["h2_mul"], s)
                    seen(pool, S["h2t_done"], s - 2)
                    seen(pool, S[f"st_rows{1 - par}"], 16 * NT * TOPK * hp)
                    g.tensor_tensor(h2row[1 - par][:, :, 0:C], h2s[:], spread(mod_b[1 - par][:, 1], 1, NT),
                                    ALU.add).then_inc(S["h2_ready"], 1)

            pool.wait_ge(S["ln1_ve"], 1)
            g.tensor_tensor(rstd1[:], ve1[:], half_exp[:, 0], ALU.pow).then_inc(S["ln1_rstd"], 1)
            pool.wait_ge(S["st_zero"], 16)
            pool.wait_ge(S["c_lam"], 1)
            token_steps(pool, step)
            for tile in range(NT):
                dispatch(B - 1, 1, tile)

            last_y = g.to_reg(YROWS - 1)
            pool.wait_ge(S["st_fill"], 16 * B)

            def put(q, i, n, last_n):
                pool.wait_ge(S["put_row"], q + 1)
                g.tensor_tensor(y_pos[:], rank[n][:], y_base[n][:], ALU.add).then_inc(S["put_pos"], 1)
                pool.wait_ge(S["put_pos"], q + 1)
                settle(3)
                g.tensor_copy(y_row[n][:], y_pos[:]).then_inc(S["put_step"], 1)
                pool.wait_ge(S["e_evac"], q + 1)
                pool.wait_ge(S["put_step"], q + 1)
                settle(2)
                g.indirect_dma_start(out=y_dram, out_offset=bass.IndirectOffsetOnAxis(ap=y_row[n][:, 0:1], axis=0),
                                     in_=e_out[n], in_offset=None, bounds_check=last_y,
                                     oob_is_err=False).then_inc(S[f"st_put{n}"], 16)
                if last_n is not None:
                    pool.wait_ge(S[f"st_put{1 - n}"], last_n)
                    pool.sem_inc(S["e_free"], 1)

            put(0, 0, 0, None)
            with pool.Fori(0, (PAIRS - 2) // NBUF) as i:
                put(NBUF * i + 1, i, 1, 16 * i + 16)
                put(NBUF * i + 2, i, 0, 16 * i + 16)
            put(PAIRS - 1, 0, 1, None)

            def gate(t, b, i):
                pool.wait_ge(S["y_sum"], t + 1)
                pool.wait_ge(S["settled"], 2 * t + 1)
                settle(4).then_inc(S["settled"], 1)
                g.tensor_tensor(ygb[i], ysum[i], gb_all[:, b], ALU.mult).then_inc(S["y_gb"], 1)
                pool.wait_ge(S["y_gb"], t + (NT + 1))
                pool.wait_ge(S[f"st_y{i}"], 16 * b + 16)
                pool.wait_ge(S["settled"], 2 * t + 2)
                settle(4).then_inc(S["settled"], 1)
                g.tensor_tensor(yout[i], ygb[i], pre[:, t], ALU.add).then_inc(S["y_out"], 1)

            for i in range(NT):
                pool.sem_inc(S[f"st_y{i}"], 16)
            pool.sem_inc(S["settled"], 1)
            pool.sem_inc(S["y_gb"], NT)
            with pool.Fori(0, B) as b:
                for i in range(NT):
                    gate(NT * b + i, b, i)

        @block.scalar
        def _(act):
            a = nc.scalar
            a.dma_start(qkv_raw, qkv_w.rearrange("(a p) c -> p a c", p=P)).then_inc(S["ld_qkvw"], 16)
            a.dma_start(proj_raw, proj_w.rearrange("(a p) c -> p a c", p=P)).then_inc(S["ld_projw"], 16)
            a.dma_start(wmod_sb, wmod.rearrange("(k p) n -> p k n", p=P)).then_inc(S["ld_wmod"], 16)
            for i, w in enumerate((qkv_norm_w, norm_w, proj_norm_w)):
                a.dma_start(norm_cols[:, i], w.rearrange("(k p) -> p k", p=P),
                            allow_slow_non_contiguous=True).then_inc(S["ld_norms"], 16)
            a.dma_start(bias_row[:], spread(bias, 0, P)).then_inc(S["ld_norms"], 16)

            def copy(out_, in_, scale=1.0):
                return a.activation(out_, in_, ACT.Copy, scale=scale)

            act.wait_ge(S["ld_c"], 16)
            a.activation(c_sig[:], c_sb[:], ACT.Exp, scale=-1.0).then_inc(S["m_exp"], 1)
            act.wait_ge(S["c_neg"], 1)
            for h in range(HEADS):
                last = a.activation(decay[:, h % 8 // 2, h // 8, h % 2], diff[:], ACT.Exp, scale=neg_s[:, h:h + 1])
            last.then_inc(S["c_decay0"], 1)
            for j in range(KC):
                a.activation(lam_q[:, j], trow[:], ACT.Exp, scale=neg_s_part[:, j:j + 1])
            a.activation(lam_rev[:], neg_s[:], ACT.Exp, scale=t_left[:, 0:1]).then_inc(S["c_lam"], 1)

            def norm1_out(b, par):
                act.wait_ge(S["xt_done"], b + 1)
                act.wait_ge(S["mod_cur_ready"], b + 1)
                seen(act, S["v_done"], b)
                seen(act, S["kt_done"], b)
                for j in range(KC):
                    last = a.activation(hT[:, j], ps_a[:, N * j:N * j + N], ACT.Identity,
                                        scale=mod_cur[par][:, 2 + j:3 + j], bias=mod_cur[par][:, j:j + 1])
                last.then_inc(S["hT_ready"], 1)
                for j in range(KC):
                    last = a.activation(hsq[:, j], ps_a[:, N * j:N * j + N], ACT.Square,
                                        scale=mod_cur[par][:, 2 + j:3 + j], bias=mod_cur[par][:, j:j + 1])
                last.then_inc(S["hsq_ready"], 1)

            def step(s, par, h, hp):
                has_prev = not before(s, 1) and not at_end(s, B + 1)
                cur = not at_end(s, B)
                if cur:
                    a.dma_start(fill_v[s], spread(y_zeros[:], 1, N * TOPK * C // P // 1024)).then_inc(S["st_fill"], 16)
                if cur:
                    act.wait_ge(S["q_done"], s + 1)
                    seen(act, S["qlam_ready"], s)
                    copy(qT[:].rearrange("p j t -> p (j t)"), ps_a[:]).then_inc(S["q_taken"], 1)
                    act.wait_ge(S["k_done"], s + 1)
                    for i in range(2):
                        last = copy(k_eo[i][:].rearrange("p j t -> p (j t)"), ps_b[:], even_odd[:, i:i + 1])
                    last.then_inc(S["k_taken"], 1)
                    act.wait_ge(S["v_done"], s + 1)
                    act.wait_ge(S["rr2_ready"], s + 1)
                    copy(v_full[:], ps_c[:, 0:C], rr2[:, 0:1])
                    for tile in range(NT):
                        vv = ps_c[:, C * tile:C * tile + C].rearrange("p (a q d) -> p a q d", q=2, d=HD)
                        for i in range(2):
                            last = copy(v_eo[i][:, tile, :, i], vv[:, :, i], rr2[:, tile:tile + 1])
                    last.then_inc(S["v_taken"], 1)
                if has_prev:
                    act.wait_ge(S["h2t_done"], s)
                    copy(h2T[:].rearrange("p j t -> p (j t)"), ps_a[:]).then_inc(S["h2T_ready"], 1)
                if cur:
                    act.wait_ge(S["pv1"], s + 1)
                    copy(oT[:].rearrange("p i j t -> p (i j t)"), ps_o[:])
                    a.activation(osq[:].rearrange("p i j t -> p (i j t)"), ps_o[:], ACT.Square).then_inc(S["o_taken"], 1)
                if has_prev:
                    act.wait_ge(S["lg_done"], s)
                    seen(act, S["r1"], s - 1)
                    a.activation(r_exp[:].rearrange("p i e -> p (i e)"), ps_b[:, 0:NT * E], ACT.Exp,
                                 scale=-1.0).then_inc(S["lg_exp"], 1)
                if not at_end(s, B - 1):
                    norm1_out(s + 1, 1 - par)
                if has_prev:
                    act.wait_ge(S["gu_done"], s)
                    seen(act, S["sg1"], s - 1)
                    a.activation(s_exp[:], ps_c[0:F, 0:N], ACT.Tanh, scale=0.5).then_inc(S["sg_exp"], 1)

            norm1_out(0, 0)
            act.wait_ge(S["c_misc"], 1)
            act.wait_ge(S["c_fill"], 1)
            token_steps(act, step)

            def pair_step(q, i, m):
                if not before(q, 0) and not at_end(q, PAIRS):
                    act.wait_ge(S["gup"], q + 1)
                    a.activation(e_exp[m % NBUF], e_gups[m % NBUF][0:F, 0:P], ACT.Tanh,
                                 scale=0.5).then_inc(S["ge_exp"], 1)
                if not before(q, 1):
                    n = (m - 1) % NBUF
                    act.wait_ge(S["dnp"], q)
                    act.wait_ge(S["wcol_ready"], q)
                    act.wait_ge(S["e_free"], q)
                    copy(e_out[n], e_dn[n], wcol[n][:, 0:1]).then_inc(S["e_evac"], 1)

            act.sem_inc(S["e_free"], NBUF)
            pair_steps(act, pair_step)

        @block.vector
        def _(dve):
            v = nc.vector
            dve.wait_ge(S["m_exp"], 1)
            v.tensor_scalar(c_sig[:], c_sig[:], 1.0, None, ALU.add).then_inc(S["prologue_step"], 1)
            dve.wait_ge(S["prologue_step"], 1)
            v.reciprocal(c_sig[:], c_sig[:]).then_inc(S["prologue_step"], 1)
            dve.wait_ge(S["prologue_step"], 2)
            v.tensor_tensor(c_sb[:], c_sb[:], c_sig[:], ALU.mult).then_inc(S["m_silu"], 1)
            dve.wait_ge(S["ld_qkvw"], 16)
            v.tensor_reduce(abs_sum[:, 0:1], qkv_raw, mybir.AxisListType.XY, ALU.add, apply_absolute_value=True)
            dve.wait_ge(S["ld_projw"], 16)
            v.tensor_reduce(abs_sum[:, 1:2], proj_raw, mybir.AxisListType.XY, ALU.add,
                            apply_absolute_value=True).then_inc(S["q_abs"], 1)
            dve.wait_ge(S["ld_small"], 16 * (1 + HEADS))
            dve.wait_ge(S["ld_norms"], 16 * 4)
            dve.wait_ge(S["c_fill"], 1)
            v.tensor_scalar(neg_s[:], s_row[:], -1.0, None, ALU.mult)
            v.tensor_scalar(neg_s_part[:], s_part[:], -1.0, None, ALU.mult)
            v.tensor_scalar(diff[:], diff[:], 0.0, None, ALU.max).then_inc(S["c_neg"], 1)
            v.memset(ones_bf[:], 1.0)
            v.tensor_scalar(part_bit[:], part_ix[:], HD, None, ALU.bitwise_and).then_inc(S["prologue_step"], 1)
            dve.wait_ge(S["prologue_step"], 3)
            v.tensor_scalar(even_odd[:, 1:2], part_bit[:], 1.0 / HD, None, ALU.mult)
            v.tensor_scalar(even_odd[:, 0:1], part_bit[:], -1.0 / HD, 1.0, ALU.mult, ALU.add)
            v.tensor_tensor(q_scale[:, 0], norm_cols[:, 1], norm_cols[:, 1], ALU.mult).then_inc(S["prologue_step"], 1)
            dve.wait_ge(S["prologue_step"], 4)
            v.tensor_scalar(stat_w[:, :, 1], q_scale[:, 0], EPS_F, None, ALU.add)
            v.tensor_tensor(q_scale[:, 1], norm_cols[:, 1], norm_cols[:, 2], ALU.mult).then_inc(S["c_misc"], 1)
            dve.wait_ge(S["q_all"], 1)
            v.tensor_scalar(w_mean[:, 0:1], abs_all[:, 0:1], 1.0 / (3 * C * C), 1e-5, ALU.mult, ALU.max)
            v.tensor_scalar(w_mean[:, 1:2], abs_all[:, 1:2], 1.0 / (C * C), 1e-5, ALU.mult,
                            ALU.max).then_inc(S["prologue_step"], 1)
            dve.wait_ge(S["prologue_step"], 5)
            v.reciprocal(w_inv[:], w_mean[:]).then_inc(S["prologue_step"], 1)
            dve.wait_ge(S["c_misc"], 1)
            v.tensor_scalar(q_scale[:, 0], norm_cols[:, 0], w_mean[:, 0:1], None, ALU.mult)
            v.tensor_scalar(q_scale[:, 1], q_scale[:, 1], w_mean[:, 1:2], None, ALU.mult).then_inc(S["q_sc"], 1)
            dve.wait_ge(S["prologue_step"], 6)
            v.tensor_scalar(qkv_raw, qkv_raw, w_inv[:, 0:1], MAGIC, ALU.mult, ALU.add)
            v.tensor_scalar(proj_raw, proj_raw, w_inv[:, 1:2], MAGIC, ALU.mult, ALU.add).then_inc(S["prologue_step"], 1)
            dve.wait_ge(S["prologue_step"], 7)
            v.tensor_scalar(qkv_raw, qkv_raw, MAGIC, 1.0, ALU.subtract, ALU.min)
            v.tensor_scalar(proj_raw, proj_raw, MAGIC, 1.0, ALU.subtract, ALU.min).then_inc(S["prologue_step"], 1)
            dve.wait_ge(S["prologue_step"], 8)
            v.tensor_scalar(qkv_raw, qkv_raw, -1.0, None, ALU.max)
            v.tensor_scalar(proj_raw, proj_raw, -1.0, None, ALU.max).then_inc(S["q_tern"], 1)
            dve.wait_ge(S["m_tp"], 1)
            v.tensor_copy(c_cols[:].rearrange("p k b -> p (k b)"), ps_o[:, 0:KC * B]).then_inc(S["m_ct"], 1)
            dve.wait_ge(S["m_mm"], 1)
            mc = mod_cols[:].rearrange("p m b -> p (m b)")
            v.tensor_copy(mc[:, 0:2 * B], ps_o[:, 64:64 + 2 * B])
            v.tensor_scalar(mc[:, 2 * B:4 * B], ps_o[:, 64 + 2 * B:64 + 4 * B], 1.0, None, ALU.add).then_inc(S["m_cols"], 1)
            v.tensor_copy(mod_rows[:, 0:2 * C], ps_b[0:B, :])
            v.tensor_copy(mod_rows[:, 2 * C:4 * C], ps_c[0:B, :]).then_inc(S["m_rows0"], 1)
            dve.wait_ge(S["m_rows0"], 1)
            gates = mod_rows[:].rearrange("p (m c) -> p m c", m=4)[:, 0:4:3]
            v.tensor_scalar(mod_rows[:, 2 * C:3 * C], mod_rows[:, 2 * C:3 * C], 1.0, None, ALU.add)
            v.tensor_scalar(sign_rows[:], gates, 0.0, 2.0, ALU.is_ge, ALU.mult).then_inc(S["prologue_step"], 1)
            v.scalar_tensor_tensor(out=abs_rows[:], in0=gates, scalar=-1.0, in1=gates, op0=ALU.mult,
                                   op1=ALU.max).then_inc(S["prologue_step"], 1)
            dve.wait_ge(S["prologue_step"], 9)
            v.tensor_scalar(sign_rows[:], sign_rows[:], 1.0, None, ALU.subtract).then_inc(S["prologue_step"], 1)
            dve.wait_ge(S["prologue_step"], 10)
            dve.wait_ge(S["prologue_step"], 11)
            v.scalar_tensor_tensor(out=gates, in0=abs_rows[:], scalar=0.25, in1=sign_rows[:], op0=ALU.max,
                                   op1=ALU.mult).then_inc(S["m_rows"], 1)
            dve.wait_ge(S["q_tp"], 1)
            dve.wait_ge(S["q_sc"], 1)
            for k in range(KC):
                v.tensor_scalar(w_qkv[:, k, 0:512], ps_s[:, k], q_scale[:, 0, k:k + 1], None, ALU.mult)
                v.tensor_scalar(w_qkv[:, k, 512:768], ps_s[:, 2, C * k:C * k + C], q_scale[:, 0, k:k + 1], None, ALU.mult)
                last = v.tensor_scalar(w_proj[:, k], ps_s[:, 3, C * k:C * k + C], q_scale[:, 1, k:k + 1], None, ALU.mult)
            last.then_inc(S["q_w"], 1)

            def settle():
                v.memset(pad[:], 0.0)

            def norm_stats(b, x_, bn, mv, ve, pre_):
                for i in range(NT):
                    last = v.bn_stats(bn[:, i], x_[:, i])
                last.then_inc(S[pre_ + "_step"], 1)
                dve.wait_ge(S[pre_ + "_step"], 2 * b + 1)
                settle()
                for i in range(NT):
                    last = v.bn_aggr(mv[:, i], bn[:, i])
                last.then_inc(S[pre_ + "_step"], 1)
                dve.wait_ge(S[pre_ + "_step"], 2 * b + 2)
                v.tensor_scalar(ve[:], mv[:, :, 1], EPS_LN, None, ALU.add).then_inc(S[pre_ + "_ve"], 1)

            def norm_apply(b, x_, mv, rstd, z, pre_, z_sem):
                dve.wait_ge(S[pre_ + "_rstd"], b + 1)
                for i in range(NT):
                    last = v.tensor_scalar(z[:, i], x_[:, i], mv[:, i, 0:1], rstd[:, i:i + 1], ALU.subtract, ALU.mult)
                last.then_inc(S[z_sem], 1)

            def norm1_stats(b):
                dve.wait_ge(S["ld_xa"], 16 * (b + 1))
                norm_stats(b, xa, bn1, mv1, ve1, "ln1")

            def norm1_apply(b, par):
                seen(dve, S["xt_done"], b)
                norm_apply(b, xa, mv1, rstd1, z1, "ln1", "z1_ready")
                seen(dve, S["hsq_ready"], b - 1)
                v.tensor_copy(mod_cur[par][:], mod_cols[:, :, b]).then_inc(S["mod_cur_ready"], 1)

            def rms(b, par):
                dve.wait_ge(S["kt_done"], b + 1)
                v.tensor_scalar(rr_t[:], ps_a[:, C:C + NT], 1.0 / C, EPS_F, ALU.mult, ALU.add).then_inc(S["rr_a"], 1)
                dve.wait_ge(S["rr_a"], b + 1)
                seen(dve, S["v_taken"], b)
                v.reciprocal(rr2[:], rr_t[:]).then_inc(S["rr2_ready"], 1)
                dve.wait_ge(S["kt_done"], b + 1)
                seen(dve, S["kv_done"], b)
                v.tensor_tensor(k_lam[:].rearrange("p (h d) -> p h d", d=HD),
                                ps_a[:, 0:C].rearrange("p (h d) -> p h d", d=HD), spread(lam_rev[:], 2, HD),
                                ALU.mult).then_inc(S["klam_ready"], 1)
                dve.wait_ge(S["rr2_ready"], b + 1)
                v.tensor_scalar(a16[par][:], rr2[:], 1.0 / HD, None, ALU.mult).then_inc(S["a16_ready"], 1)
            def state_block(b):
                dve.wait_ge(S["kv_done"], b + 1)
                seen(dve, S["pv1"], b)
                v.tensor_tensor(state[:], ps_b[:, 0:KC * P].rearrange("p (j m) -> p j m", j=KC),
                                spread(head_block[:], 1, KC), ALU.mult).then_inc(S["state_ready"], 1)

            def out_norms(b, par):
                dve.wait_ge(S["os_done"], b + 1)
                dve.wait_ge(S["a16_ready"], b + 1)
                v.scalar_tensor_tensor(out=fin[:, 1], in0=ps_o[:, 0:NT], scalar=1.0 / C, in1=a16[par][:],
                                       op0=ALU.mult, op1=ALU.mult).then_inc(S["f1"], 1)
                dve.wait_ge(S["f1"], b + 1)
                v.tensor_scalar(fin[:, 2], fin[:, 1], EPS_F * EPS_O, None, ALU.add).then_inc(S["factor_step"], 1)
                dve.wait_ge(S["factor_step"], 2 * b + 1)
                v.reciprocal(fin[:, 3], fin[:, 2]).then_inc(S["factor_step"], 1)
                dve.wait_ge(S["factor_step"], 2 * b + 2)
                v.tensor_tensor(fin[:, 4], fin[:, 3], a16[par][:], ALU.mult).then_inc(S["f5"], 1)

            def residual(b, par, hb):
                dve.wait_ge(S["f_ready"], b + 1)
                dve.wait_ge(S["proj_done"], b + 1)
                dve.wait_ge(S[f"ld_modb{par}"], 16 * (hb + 1))
                for i in range(NT):
                    last = v.scalar_tensor_tensor(out=attn[:, i], in0=ps_c[:, C * i:C * i + C], scalar=fac[:, i:i + 1],
                                                  in1=mod_b[par][:, 0], op0=ALU.mult, op1=ALU.mult)
                last.then_inc(S["attn_ready"], 1)
                dve.wait_ge(S["attn_ready"], b + 1)
                dve.wait_ge(S["ld_xres"], 16 * (b + 1))
                v.tensor_tensor(x2[par][:], attn[:], xres[:], ALU.add).then_inc(S["x2_ready"], 1)
                dve.wait_ge(S["x2_ready"], b + 1)
                norm_stats(b, x2[par], bn2, mv2, ve2, "ln2")

            def mask(b, tile):
                dve.wait_ge(S[f"sc{tile}"], b + 1)
                if tile == 0:
                    seen(dve, S["pv1"], b)
                else:
                    dve.wait_ge(S["pv0"], b + 1)
                v.tensor_tensor(scm[:].rearrange("p r j q t -> p (r j q t)"), ps_s[:].rearrange("p r n -> p (r n)"),
                                decay[:].rearrange("p r j q t -> p (r j q t)"), ALU.mult).then_inc(S[f"mk{tile}"], 1)

            def router_scores(b):
                dve.wait_ge(S["lg_exp"], b + 1)
                v.tensor_scalar(r_den[:], r_exp[:], 1.0, None, ALU.add).then_inc(S["r1"], 1)
                dve.wait_ge(S["r1"], b + 1)
                v.reciprocal(r_sig[:], r_den[:]).then_inc(S["route"], 1)
                dve.wait_ge(S["route"], ROUTE_STEPS * b + 1)
                v.tensor_tensor(r_sc[:], r_sig[:], spread(bias_row[:], 1, NT), ALU.add).then_inc(S["route"], 1)
                dve.wait_ge(S["route"], ROUTE_STEPS * b + 2)
                v.memset(g_sum[:, :, G:2 * G], OUT)
                for i in range(NT):
                    for g_ in range(G):
                        last = v.max(g_top[:, i * G + g_], r_sc[:, i, EG * g_:EG * g_ + EG])
                last.then_inc(S["route"], 1)

            def router_choice(b, par):
                dve.wait_ge(S["route"], ROUTE_STEPS * b + 3)
                v.tensor_tensor(g_sum[:, :, 0:G], g_top[:, :, 0].rearrange("p (i g) -> p i g", i=NT),
                                g_top[:, :, 1].rearrange("p (i g) -> p i g", i=NT), ALU.add).then_inc(S["route"], 1)
                dve.wait_ge(S["route"], ROUTE_STEPS * b + 4)
                settle()
                for i in range(NT):
                    last = v.max(g_best[:, i], g_sum[:, i])
                last.then_inc(S["route"], 1)
                dve.wait_ge(S["route"], ROUTE_STEPS * b + 5)
                v.memset(g_best[:, :, KG:8], OUT).then_inc(S["route"], 1)
                dve.wait_ge(S["route"], ROUTE_STEPS * b + 6)
                settle()
                for i in range(NT):
                    last = v.match_replace(g_rep[:, i], g_best[:, i], g_sum[:, i], PICK)
                last.then_inc(S["route"], 1)
                dve.wait_ge(S["route"], ROUTE_STEPS * b + 7)
                v.tensor_scalar(g_pick[:], g_rep[:, :, 0:G], 1.5 * OUT, None, ALU.is_lt).then_inc(S["route"], 1)
                dve.wait_ge(S["route"], ROUTE_STEPS * b + 8)
                v.tensor_scalar(g_pen[:], g_pick[:], -OUT, OUT, ALU.mult, ALU.add).then_inc(S["route"], 1)
                dve.wait_ge(S["route"], ROUTE_STEPS * b + 9)
                r4 = r_sc[:].rearrange("p i (g e) -> p i g e", g=G)
                v.tensor_tensor(e_val[:].rearrange("p i (g e) -> p i g e", g=G), r4, spread(g_pen[:], 3, EG),
                                ALU.add).then_inc(S["route"], 1)
                dve.wait_ge(S["route"], ROUTE_STEPS * b + 10)
                settle()
                for i in range(NT):
                    last = v.max(e_best[:, i], e_val[:, i])
                last.then_inc(S["route"], 1)
                dve.wait_ge(S["route"], ROUTE_STEPS * b + 11)
                v.memset(e_best[:, :, TOPK:8], OUT).then_inc(S["route"], 1)
                dve.wait_ge(S["route"], ROUTE_STEPS * b + 12)
                settle()
                for i in range(NT):
                    last = v.match_replace(e_rep[:, i], e_best[:, i], e_val[:, i], PICK)
                last.then_inc(S["route"], 1)
                dve.wait_ge(S["route"], ROUTE_STEPS * b + 13)
                v.scalar_tensor_tensor(out=sel[:].rearrange("p i (g e) -> p i g e", g=G),
                                       in0=e_rep[:].rearrange("p i (g e) -> p i g e", g=G), scalar=1.5 * OUT,
                                       in1=spread(g_pick[:], 3, EG), op0=ALU.is_lt, op1=ALU.mult
                                       ).then_inc(S["route"], 1)
                dve.wait_ge(S["route"], ROUTE_STEPS * b + 14)
                seen(dve, S["pos_done"], b)
                v.tensor_copy(sel_bf[:], sel[:]).then_inc(S["selbf_ready"], 1)
                v.tensor_tensor(w_raw[:], sel[:], r_sig[:], ALU.mult).then_inc(S["route"], 1)
                dve.wait_ge(S["selbf_ready"], b + 1)
                v.tensor_tensor(carry[:, 1], carry[:, 0], sel_bf[:, 0], ALU.add).then_inc(S["carry_ready"], 1)
                dve.wait_ge(S["route"], ROUTE_STEPS * b + 15)
                v.tensor_reduce(w_sum[:], w_raw[:], AX_X, ALU.add).then_inc(S["route"], 1)
                dve.wait_ge(S["route"], ROUTE_STEPS * b + 16)
                v.reciprocal(w_rec[:], w_sum[:]).then_inc(S["route"], 1)
                dve.wait_ge(S["route"], ROUTE_STEPS * b + 17)
                dve.wait_ge(S["h2_ready"], b + 1)
                for i in range(NT):
                    last = v.tensor_scalar(h2row[par][:, i, C:KEYS], w_raw[:, i], w_rec[:, i:i + 1], ROUTE_SCALE,
                                           ALU.mult, ALU.mult)
                last.then_inc(S["w_ready"], 1)

            def shared(b):
                dve.wait_ge(S["sg_exp"], b + 1)
                v.scalar_tensor_tensor(out=s_gu[:], in0=s_exp[:], scalar=1.0, in1=ps_c[0:F, 0:N], op0=ALU.add,
                                       op1=ALU.mult).then_inc(S["sg1"], 1)
                dve.wait_ge(S["sg1"], b + 1)
                v.scalar_tensor_tensor(out=s_h[:], in0=s_gu[:], scalar=0.5, in1=ps_c[0:F, N:2 * N], op0=ALU.mult,
                                       op1=ALU.mult).then_inc(S["sh_ready"], 1)

            def shared_out(b, par):
                dve.wait_ge(S["dn_done"], b + 1)
                dve.wait_ge(S["ld_gb"], 16)
                v.tensor_tensor(sh_g[:], ps_b[:].rearrange("p (i c) -> p i c", i=NT), spread(gb_all[:, b], 1, NT),
                                ALU.mult).then_inc(S["sh_gated"], 1)
                dve.wait_ge(S["sh_gated"], b + 1)
                v.tensor_tensor(pre[:, bass.ds(NT * b, NT)], sh_g[:], x2[par][:], ALU.add).then_inc(S["pre_ready"], 1)

            def slots(b, par):
                dve.wait_ge(S["pos_done"], b + 1)
                pos = ps_o[:, E:E + NT * E].rearrange("p (i e) -> p i e", i=NT)
                v.scalar_tensor_tensor(out=keep[:], in0=pos, scalar=float(CAP), in1=sel[:], op0=ALU.is_lt,
                                       op1=ALU.mult)
                v.tensor_tensor(row_key[:], spread(row_base[:], 1, NT), pos, ALU.subtract).then_inc(S["slot_step"], 1)
                v.tensor_tensor(carry[:, 0], carry[:, 1], sel_bf[:, 1], ALU.add)
                dve.wait_ge(S["slot_step"], 3 * b + 1)
                v.tensor_tensor(key[:], keep[:], row_key[:], ALU.mult).then_inc(S["slot_step"], 1)
                dve.wait_ge(S["slot_step"], 3 * b + 2)
                settle()
                for i in range(NT):
                    last = v.max(h2row[par][:, i, KEYS:TKEY], key[:, i])
                last.then_inc(S["slot_step"], 1)
                dve.wait_ge(S["slot_step"], 3 * b + 3)
                v.tensor_copy(h2row[par][:, :, TKEY], token_key[:, bass.ds(NT * b, NT)])
                v.tensor_scalar(slot_ix[par][:], h2row[par][:, :, KEYS:TKEY], -1.0, float(ROWS), ALU.mult,
                                ALU.add).then_inc(S["slots_ready"], 1)

            def step(s, par, h, hp):
                cur, nxt = not at_end(s, B), not at_end(s, B - 1)
                has_prev = not before(s, 1) and not at_end(s, B + 1)
                has_two = not before(s, 2)
                if has_two:
                    router_scores(s - 2)
                if nxt:
                    norm1_stats(s + 1)
                if has_two:
                    shared(s - 2)
                if not before(s, 3):
                    slots(s - 3, 1 - par)
                if has_prev:
                    out_norms(s - 1, 1 - par)
                if cur:
                    rms(s, par)
                if has_two:
                    router_choice(s - 2, par)
                if cur:
                    mask(s, 0)
                if cur:
                    state_block(s)
                if has_prev:
                    residual(s - 1, 1 - par, hp)
                if nxt:
                    norm1_apply(s + 1, 1 - par)
                if has_prev:
                    seen(dve, S["h2_mul"], s - 1)
                    norm_apply(s - 1, x2[1 - par], mv2, rstd2, z2, "ln2", "z2_ready")
                if cur:
                    mask(s, 1)
                if has_two:
                    shared_out(s - 2, par)

            norm1_stats(0)
            dve.wait_ge(S["m_cols"], 1)
            norm1_apply(0, 0)
            dve.wait_ge(S["c_lam"], 1)
            dve.wait_ge(S["c_shape"], 2)
            dve.wait_ge(S["c_decay"], 1)
            dve.wait_ge(S["st_zero"], 16)
            token_steps(dve, step)
            slots(B - 1, 1)

            def pair_step(q, i, m):
                if not at_end(q, PAIRS - 1):
                    n = (m + 1) % NBUF
                    dve.wait_ge(S["xtp"], q + 2)
                    seen(dve, S["gup"], q)
                    v.tensor_copy(xt[n].rearrange("p k r -> p (k r)"), e_xt[n]).then_inc(S["xt_taken"], 1)
                if not before(q, 0) and not at_end(q, PAIRS):
                    n = m % NBUF
                    dve.wait_ge(S["ge_exp"], q + 1)
                    v.scalar_tensor_tensor(out=e_gu[n], in0=e_exp[n], scalar=1.0, in1=e_gups[n][0:F, 0:P],
                                           op0=ALU.add, op1=ALU.mult).then_inc(S["silu_step"], 1)
                    dve.wait_ge(S["silu_step"], q + 1)
                    v.scalar_tensor_tensor(out=e_h[n], in0=e_gu[n], scalar=0.5, in1=e_gups[n][0:F, P:2 * P],
                                           op0=ALU.mult, op1=ALU.mult).then_inc(S["gh_ready"], 1)
                if not at_end(q, PAIRS - 1):
                    n = (m + 1) % NBUF
                    seen(dve, S["e_evac"], q)
                    for half in range(2):
                        rows = slice(SLOTS * half, SLOTS * half + SLOTS)
                        e = 2 * q + (2 + half)
                        v.tensor_copy(wcol[n][rows], xr[n][rows, bass.ds(C + e, 1)])
                    seen(dve, S["put_pos"], q)
                    v.tensor_tensor(larger[:], xr[n][:, KEYS:TKEY], spread(slot_key[:, q + 1], 1, 8), ALU.is_gt)
                    v.tensor_scalar(y_base[n][:], xr[n][:, TKEY:TKEY + 1], -1.0, float(YROWS), ALU.mult,
                                    ALU.add).then_inc(S["wcol_ready"], 1)
                    dve.wait_ge(S["wcol_ready"], q + 2)
                    v.tensor_reduce(rank[n][:], larger[:], AX_X, ALU.add).then_inc(S["put_row"], 1)

            pair_steps(dve, pair_step)

            with dve.Fori(0, B * NT // YBUF) as i:
                for m in range(YBUF):
                    dve.wait_ge(S[f"ld_y{m}"], 16 * i + 16)
                    dve.wait_ge(S["y_gb"], YBUF * i + (m + 1))
                    v.tensor_reduce(ysum[m % NT], y_in[m].rearrange("p (j c) -> p c j", c=C), AX_X,
                                    ALU.add).then_inc(S["y_sum"], 1)

        @block.tensor
        def _(pe):
            mm = nc.tensor

            pe.wait_ge(S["m_silu"], 1)
            pe.wait_ge(S["c_shape"], 2)
            for k in range(KC):
                last = mm.transpose(ps_o[:, B * k:B * k + B], c_sb[:, P * k:P * k + P], ident[0:B, 0:B])
            last.then_inc(S["m_tp"], 1)
            pe.wait_ge(S["m_ct"], 1)
            pe.wait_ge(S["ld_wmod"], 16)
            for i in range(4):
                for k in range(KC):
                    mm.matmul(ps_o[:, 64 + B * i:64 + B * i + B], wmod_sb[:, k, P * i:P * i + P], c_cols[:, k],
                             start=(k == 0), stop=(k == KC - 1))
            for i, ps in enumerate((ps_b, ps_c)):
                for k in range(KC):
                    last = mm.matmul(ps[0:B, :], c_cols[:, k], wmod_sb[:, k, 512 * (i + 1):512 * (i + 2)],
                                    start=(k == 0), stop=(k == KC - 1))
            last.then_inc(S["m_mm"], 1)

            def norm1_transpose(b):
                pe.wait_ge(S["z1_ready"], b + 1)
                seen(pe, S["h2T_ready"], b - 1)
                seen(pe, S["rr_a"], b)
                seen(pe, S["klam_ready"], b)
                for j in range(KC):
                    for i in range(NT):
                        last = mm.transpose(ps_a[:, N * j + T * i:N * j + T * i + T], z1[:, i, P * j:P * j + P], ident[:])
                last.then_inc(S["xt_done"], 1)

            pe.wait_ge(S["q_tern"], 1)
            for k in range(KC):
                for o in range(4):
                    mm.transpose(ps_s[:, k, P * o:P * o + P], qkv_raw[:, o, P * k:P * k + P], ident[:])
                for o in range(2):
                    mm.transpose(ps_s[:, 2, C * k + P * o:C * k + P * o + P], qkv_raw[:, 4 + o, P * k:P * k + P], ident[:])
                for o in range(2):
                    last = mm.transpose(ps_s[:, 3, C * k + P * o:C * k + P * o + P], proj_raw[:, o, P * k:P * k + P], ident[:])
            last.then_inc(S["q_tp"], 1)
            pe.wait_ge(S["q_w"], 1)
            pe.wait_ge(S["m_rows0"], 1)
            pe.wait_ge(S["m_cols"], 1)
            pe.wait_ge(S["c_misc"], 1)
            pe.wait_ge(S["ld_gate"], 16)
            pe.wait_ge(S["ld_shared"], 48)
            norm1_transpose(0)

            def project_qkv(b):
                pe.wait_ge(S["hT_ready"], b + 1)
                pe.wait_ge(S["hsq_ready"], b + 1)
                for j in range(KC):
                    for k in range(KC):
                        last = mm.matmul(ps_a[:, N * j:N * j + N], w_qkv[:, k, P * j:P * j + P], hT[:, k],
                                        start=(k == 0), stop=(k == KC - 1))
                last.then_inc(S["q_done"], 1)
                seen(pe, S["lg_exp"], b - 1)
                seen(pe, S["state_ready"], b)
                for j in range(KC):
                    for k in range(KC):
                        last = mm.matmul(ps_b[:, N * j:N * j + N], w_qkv[:, k, C + P * j:C + P * j + P], hT[:, k],
                                        start=(k == 0), stop=(k == KC - 1))
                last.then_inc(S["k_done"], 1)
                pe.wait_ge(S["q_taken"], b + 1)
                for i in range(NT):
                    for k in range(KC):
                        last = mm.matmul(ps_a[:, C + i:C + i + 1], hsq[:, k, T * i:T * i + T], stat_w[:, 0, 0:1],
                                        start=(k == 0), stop=(k == KC - 1))
                for k in range(KC):
                    last = mm.matmul(ps_a[:, 0:C], hT[:, k, 0:T], w_qkv[:, k, C:2 * C], start=(k == 0), stop=(k == KC - 1))
                last.then_inc(S["kt_done"], 1)
                seen(pe, S["sh_ready"], b - 1)
                seen(pe, S["v_taken"], b)
                for i in range(NT):
                    for k in range(KC):
                        last = mm.matmul(ps_c[:, C * i:C * i + C], hT[:, k, T * i:T * i + T], w_qkv[:, k, 2 * C:3 * C],
                                        start=(k == 0), stop=(k == KC - 1))
                last.then_inc(S["v_done"], 1)

            def first_state(b):
                pe.wait_ge(S["klam_ready"], b + 1)
                pe.wait_ge(S["v_taken"], b + 1)
                pe.wait_ge(S["k_taken"], b + 1)
                for j in range(KC):
                    last = mm.matmul(ps_b[:, P * j:P * j + P], k_lam[:, P * j:P * j + P], v_full[:, P * j:P * j + P],
                                    start=True, stop=True)
                last.then_inc(S["kv_done"], 1)

            def out_stats(b):
                pe.wait_ge(S["o_taken"], b + 1)
                for i in range(NT):
                    for k in range(KC):
                        last = mm.matmul(ps_o[:, i:i + 1], osq[:, i, k], stat_w[:, k, 1:2],
                                        start=(k == 0), stop=(k == KC - 1))
                last.then_inc(S["os_done"], 1)

            def project_out(b):
                seen(pe, S["sh_ready"], b)
                seen(pe, S["v_taken"], min(b + 2, B) if isinstance(b, int) else b + 2)
                for i in range(NT):
                    for k in range(KC):
                        last = mm.matmul(ps_c[:, C * i:C * i + C], oT[:, i, k], w_proj[:, k],
                                        start=(k == 0), stop=(k == KC - 1))
                last.then_inc(S["proj_done"], 1)

            def scores(b, tile):
                if tile == 0:
                    pe.wait_ge(S["k_taken"], b + 1)
                    pe.wait_ge(S["q_taken"], b + 1)
                    seen(pe, S["mk1"], b)
                else:
                    pe.wait_ge(S["mk0"], b + 1)
                ts = slice(T * tile, T * tile + T)
                for j in range(KC):
                    for q in range(2):
                        col = T * (2 * j + q)
                        for r in range(4):
                            last = mm.matmul(ps_s[:, r, col:col + T], k_eo[q][32 * r:32 * r + 32, j, ts],
                                             qT[32 * r:32 * r + 32, j, ts], start=True, stop=True)
                last.then_inc(S[f"sc{tile}"], 1)

            def values(b, tile):
                if tile == 0:
                    seen(pe, S["f1"], b)
                    seen(pe, S["slots_ready"], b - 2)
                    pe.wait_ge(S["v_taken"], b + 1)
                else:
                    pe.wait_ge(S["state_ready"], b + 1)
                    pe.wait_ge(S["qlam_ready"], b + 1)
                pe.wait_ge(S[f"mk{tile}"], b + 1)
                for j in range(KC):
                    dst = ps_o[:, 256 * tile + T * j:256 * tile + T * j + T]
                    if tile:
                        mm.matmul(dst, state[:, j], q_lam[:, j], start=True, stop=False, skip_group_check=True)
                    for q in range(2):
                        for r in range(4):
                            vq = v_eo[q][:, tile, 4 * j + r].rearrange("p q d -> p (q d)")
                            last = mm.matmul(dst[32 * r:32 * r + 32], vq, scm[:, r, j, q],
                                             start=(q == 0 and not tile), stop=(q == 1), skip_group_check=True)
                last.then_inc(S[f"pv{tile}"], 1)

            def norm2_transpose(b, par):
                pe.wait_ge(S["h2_ready"], b + 1)
                for j in range(KC):
                    for i in range(NT):
                        last = mm.transpose(ps_a[:, N * j + T * i:N * j + T * i + T], h2row[par][:, i, P * j:P * j + P],
                                           ident[:])
                last.then_inc(S["h2t_done"], 1)

            def logits(b):
                pe.wait_ge(S["h2T_ready"], b + 1)
                seen(pe, S["state_ready"], min(b + 2, B) if isinstance(b, int) else b + 2)
                seen(pe, S["sh_gated"], b)
                for i in range(NT):
                    for k in range(KC):
                        last = mm.matmul(ps_b[:, E * i:E * i + E], h2T[:, k, T * i:T * i + T], gate_sb[:, k],
                                        start=(k == 0), stop=(k == KC - 1))
                last.then_inc(S["lg_done"], 1)

            def gate_up(b):
                pe.wait_ge(S["attn_ready"], b + 1)
                for g_ in range(2):
                    for k in range(KC):
                        last = mm.matmul(ps_c[0:F, N * g_:N * g_ + N], ws_gu[:, k, g_], h2T[:, k],
                                        start=(k == 0), stop=(k == KC - 1))
                last.then_inc(S["gu_done"], 1)

            def shared_down(b):
                pe.wait_ge(S["sh_ready"], b + 1)
                pe.wait_ge(S["lg_exp"], b + 1)
                seen(pe, S["state_ready"], min(b + 3, B) if isinstance(b, int) else b + 3)
                for i in range(NT):
                    last = mm.matmul(ps_b[:, C * i:C * i + C], s_h[:, T * i:T * i + T], ws_d[:], start=True, stop=True)
                last.then_inc(S["dn_done"], 1)

            def positions(b):
                seen(pe, S["o_taken"], min(b + 3, B) if isinstance(b, int) else b + 3)
                pe.wait_ge(S["selbf_ready"], b + 1)
                pe.wait_ge(S["carry_ready"], b + 1)
                for i in range(NT):
                    mm.matmul(ps_o[:, E * (i + 1):E * (i + 2)], upper[:], sel_bf[:, i], start=True, stop=False)
                    last = mm.matmul(ps_o[:, E * (i + 1):E * (i + 2)], ones_bf[:], carry[:, i], start=False, stop=True)
                last.then_inc(S["pos_done"], 1)

            def step(s, par, h, hp):
                cur, nxt = not at_end(s, B), not at_end(s, B - 1)
                has_prev = not before(s, 1) and not at_end(s, B + 1)
                has_two = not before(s, 2)
                if has_prev:
                    out_stats(s - 1)
                if not before(s, 3):
                    positions(s - 3)
                if cur:
                    project_qkv(s)
                    scores(s, 0)
                if has_prev:
                    project_out(s - 1)
                if cur:
                    first_state(s)
                    scores(s, 1)
                if has_two:
                    shared_down(s - 2)
                if cur:
                    values(s, 0)
                if has_prev:
                    norm2_transpose(s - 1, 1 - par)
                if cur:
                    values(s, 1)
                if has_prev:
                    logits(s - 1)
                if nxt:
                    norm1_transpose(s + 1)
                if has_prev:
                    gate_up(s - 1)

            token_steps(pe, step)
            positions(B - 1)

            pe.wait_ge(S["pre_ready"], B)
            pe.wait_ge(S["slots_ready"], B)

            def pair_step(q, i, m):
                if not at_end(q, PAIRS - 1):
                    n = (m + 1) % NBUF
                    pe.wait_ge(S[f"ld_xr{n}"], 16 * (turn(i, m + 1, NBUF) + 1))
                    seen(pe, S["xt_taken"], q)
                    for k in range(KC):
                        last = mm.transpose(e_xt[n][:, P * k:P * k + P], xr[n][:, k:C:KC], ident[:])
                    last.then_inc(S["xtp"], 1)
                if not before(q, 0) and not at_end(q, PAIRS):
                    n, slot = m % NBUF, m % RING
                    pe.wait_ge(S["xt_taken"], q + 1)
                    pe.wait_ge(S[f"ld_slot{slot}"], 48 * (turn(i, m, RING) + 1))
                    for g_, w in enumerate((eg, eu)):
                        for half in range(2):
                            for k in range(KC):
                                col = P * g_ + SLOTS * half
                                last = mm.matmul(e_gups[n][0:F, col:col + SLOTS], w[:, slot, half, k],
                                                 xt[n][:, k, SLOTS * half:SLOTS * half + SLOTS],
                                                 start=(k == 0), stop=(k == KC - 1))
                    last.then_inc(S["gup"], 1)
                if not before(q, 1):
                    n, slot = (m - 1) % NBUF, (m - 1) % RING
                    pe.wait_ge(S["gh_ready"], q)
                    for half in range(2):
                        last = mm.matmul(e_dn[n][SLOTS * half:SLOTS * half + SLOTS, :],
                                         e_h[n][:, SLOTS * half:SLOTS * half + SLOTS],
                                         ed[:, slot, half], start=True, stop=True)
                    last.then_inc(S["dnp"], 1)

            pair_steps(pe, pair_step)


_INS = ["L0_attn_x", "L0_attn_qkv_w", "L0_attn_qkv_norm_w", "L0_attn_proj_w", "L0_attn_proj_norm_w",
        "L0_attn_norm_w", "L0_attn_s", "L0_ffn_gate_w", "L0_ffn_bias", "L0_ffn_w_gate", "L0_ffn_w_up",
        "L0_ffn_w_down", "L0_ffn_ws_gate", "L0_ffn_ws_up", "L0_ffn_ws_down", "L0_c", "L0_wmod"]


def kernel(**inputs):
    import numpy as np
    import concourse.bacc as bacc
    from concourse.bass_utils import run_bass_kernel_spmd

    nc = bacc.Bacc("TRN2", target_bir_lowering=False, num_devices=1)
    arrays, args = {}, []
    for name in _INS:
        a = np.ascontiguousarray(inputs[name])
        arrays[f"in_{name}"] = a
        args.append(nc.dram_tensor(f"in_{name}", a.shape, mybir.dt.from_np(a.dtype), kind="ExternalInput").ap())
    args.append(nc.dram_tensor("out", (B, N, C), F32, kind="ExternalOutput").ap())
    adaln_attention_moe(nc, *args)
    r = run_bass_kernel_spmd(nc, [arrays], core_ids=[0])
    return r.results[0]["out"]
```

```python
from contextlib import ExitStack

import concourse.bass as bass
from concourse import mybir

ALU = mybir.AluOpType
ACT = mybir.ActivationFunctionType
F32 = mybir.dt.float32
BF16 = mybir.dt.bfloat16
U32 = mybir.dt.uint32
AX_X = mybir.AxisListType.X
RADD = bass.bass_isa.ReduceOp.add

P = 128
B, N, C = 8, 256, 256
HEADS, HD = 16, 16
T = 128
NT = N // T
KC = C // P
HPJ = HEADS // KC
E, TOPK, F = 64, 6, 96
G, KG = 8, 4
EG = E // G
CAP = 2 * (256 * TOPK // E)
SLOTS = 64
ROWS = E * SLOTS
KEYS = C + E
TKEY = KEYS + 8
ROWW = 336
YROWS = B * N * TOPK
PAIRS = E // 2
RING = 16
YBUF = 4
WBUF = 8
OBUF = 4
XBUF = 8
QUADS = RING // 2
NBUF = 2
EPS_F = 1.1920928955078125e-07
EPS_LN = 1e-5
EPS_O = 1e-6
ROUTE_SCALE = 2.5
MAGIC = 12582912.0
ROUTE_STEPS = 17
OUT = -1.0e30
PICK = -2.0e30


def spread(ap, at, n):
    dims = [list(d) for d in ap.ap]
    dims.insert(at, [0, n])
    return bass.AP(ap.tensor, ap.offset, dims)


def seen(eng, sem, count):
    if isinstance(count, int) and count <= 0:
        return
    eng.wait_ge(sem, count)


def adaln_attention_moe(nc, x, qkv_w, qkv_norm_w, proj_w, proj_norm_w, norm_w, s, gate_w, bias,
                        w_gate, w_up, w_down, ws_gate, ws_up, ws_down, c, wmod, out):
    with ExitStack() as ctx:
        def sb(name, shape, dt=F32):
            return ctx.enter_context(nc.sbuf_tensor(name, shape, dt))

        def sem(name):
            return ctx.enter_context(nc.semaphore(name))

        rows_dram = nc.dram_tensor("rows_dram", [ROWS, ROWW], F32, kind="Internal").ap()
        y_dram = nc.dram_tensor("y_dram", [YROWS, C], F32, kind="Internal").ap()
        mod_dram = nc.dram_tensor("mod_dram", [B, 4 * C], F32, kind="Internal").ap()

        ident = sb("ident", [P, P])
        upper = sb("upper", [P, P], BF16)
        ones_bf = sb("ones_bf", [P, P], BF16)
        half_exp = sb("half_exp", [P, 2, 2])
        diff = sb("diff", [P, T])
        t_left = sb("t_left", [P, 1])
        part_ix = sb("part_ix", [P, 1], U32)
        part_bit = sb("part_bit", [P, 1], U32)
        y_zeros = sb("y_zeros", [P, C])
        slot_key = sb("slot_key", [P, PAIRS])
        token_key = sb("token_key", [P, B * NT])
        trow = sb("trow", [P, T])
        decay = sb("decay", [P, 4, KC, 2, T])
        s_row = sb("s_row", [P, HEADS])
        s_part = sb("s_part", [P, KC])
        neg_s = sb("neg_s", [P, HEADS])
        neg_s_part = sb("neg_s_part", [P, KC])
        lam_q = sb("lam_q", [P, KC, T])
        lam_rev = sb("lam_rev", [P, HEADS])
        even_odd = sb("even_odd", [P, 2])
        head_block = sb("head_block", [P, P])
        w_qkv = sb("w_qkv", [P, KC, 3 * C])
        w_proj = sb("w_proj", [P, KC, C])
        norm_cols = sb("norm_cols", [P, 3, KC])
        q_scale = sb("q_scale", [P, 2, KC])
        stat_w = sb("stat_w", [P, KC, 2])
        gate_sb = sb("gate_sb", [P, KC, E])
        ws_gu = sb("ws_gu", [P, KC, 2, F])
        ws_d = sb("ws_d", [F, C])
        bias_row = sb("bias_row", [P, E])
        row_base = sb("row_base", [P, E])
        mod_cols = sb("mod_cols", [P, 4, B])
        abs_sum = sb("abs_sum", [P, 2])
        abs_all = sb("abs_all", [P, 2])
        w_mean = sb("w_mean", [P, 2])
        w_inv = sb("w_inv", [P, 2])
        c_sb = sb("c_sb", [B, C])
        c_sig = sb("c_sig", [B, C])
        c_cols = sb("c_cols", [P, KC, B])
        mod_rows = sb("mod_rows", [B, 4 * C])

        xa = sb("xa", [P, NT, C])
        xres = sb("xres", [P, NT, C])
        mod_b = [sb(f"mod_b{i}", [P, 3, C]) for i in range(2)]
        gb_all = sb("gb_all", [P, B, C])
        mod_cur = [sb(f"mod_cur{i}", [P, 4]) for i in range(2)]
        bn1 = sb("bn1", [P, NT, 6])
        mv1 = sb("mv1", [P, NT, 2])
        ve1 = sb("ve1", [P, NT])
        rstd1 = sb("rstd1", [P, NT])
        z1 = sb("z1", [P, NT, C])
        hT = sb("hT", [P, KC, N])
        hsq = sb("hsq", [P, KC, N])
        rr_t = sb("rr_t", [P, NT])
        rr2 = sb("rr2", [P, NT])
        a16 = [sb(f"a16_{i}", [P, NT]) for i in range(2)]
        qT = sb("qT", [P, KC, N])
        k_eo = [sb(f"k_eo{i}", [P, KC, N]) for i in range(2)]
        v_eo = [sb(f"v_eo{i}", [P, NT, HEADS // 2, 2, HD]) for i in range(2)]
        v_full = sb("v_full", [P, C])
        k_lam = sb("k_lam", [P, C])
        q_lam = sb("q_lam", [P, KC, T])
        state = sb("state", [P, KC, P])
        scm = sb("scm", [P, 4, KC, 2, T])
        oT = sb("oT", [P, NT, KC, T])
        osq = sb("osq", [P, NT, KC, T])
        fin = sb("fin", [P, 5, NT])
        fac = sb("fac", [P, NT])
        attn = sb("attn", [P, NT, C])
        x2 = [sb(f"x2_{i}", [P, NT, C]) for i in range(2)]
        bn2 = sb("bn2", [P, NT, 6])
        mv2 = sb("mv2", [P, NT, 2])
        ve2 = sb("ve2", [P, NT])
        rstd2 = sb("rstd2", [P, NT])
        z2 = sb("z2", [P, NT, C])
        h2s = sb("h2s", [P, NT, C])
        h2row = [sb(f"h2row{i}", [P, NT, ROWW]) for i in range(2)]
        h2T = sb("h2T", [P, KC, N])
        pre = sb("pre", [P, B * NT, C])
        r_exp = sb("r_exp", [P, NT, E])
        r_den = sb("r_den", [P, NT, E])
        r_sig = sb("r_sig", [P, NT, E])
        r_sc = sb("r_sc", [P, NT, E])
        g_top = sb("g_top", [P, NT * G, 8])
        g_sum = sb("g_sum", [P, NT, 2 * G])
        g_best = sb("g_best", [P, NT, 8])
        g_rep = sb("g_rep", [P, NT, 2 * G])
        g_pick = sb("g_pick", [P, NT, G])
        g_pen = sb("g_pen", [P, NT, G])
        e_val = sb("e_val", [P, NT, E])
        e_best = sb("e_best", [P, NT, 8])
        e_rep = sb("e_rep", [P, NT, E])
        sel = sb("sel", [P, NT, E])
        sel_bf = sb("sel_bf", [P, NT, E], BF16)
        carry = sb("carry", [P, NT, E], BF16)
        w_raw = sb("w_raw", [P, NT, E])
        w_sum = sb("w_sum", [P, NT])
        w_rec = sb("w_rec", [P, NT])
        keep = sb("keep", [P, NT, E])
        row_key = sb("row_key", [P, NT, E])
        key = sb("key", [P, NT, E])
        slot_ix = [sb(f"slot_ix{i}", [P, NT, 8], U32) for i in range(2)]
        s_exp = sb("s_exp", [F, N])
        s_gu = sb("s_gu", [F, N])
        s_h = sb("s_h", [F, N])
        sh_g = sb("sh_g", [P, NT, C])

        egu = sb("egu", [P, QUADS, 2, 4, KC, F])
        ed = sb("ed", [F, QUADS, 4, C])
        pad = sb("pad", [P, 1])
        pool_pad = sb("pool_pad", [P, 5])
        wcol = [sb(f"wcol{i}", [P, 1]) for i in range(WBUF)]
        larger = sb("larger", [P, 8])
        rank = sb("rank", [P, 1])
        y_row = [sb(f"y_row{i}", [P, 1], U32) for i in range(WBUF)]
        spare = scm[:].rearrange("p r j q t -> p (r j q t)")
        row_bufs = [h[:] for h in h2row] + [spare[:, NT * ROWW * i:NT * ROWW * (i + 1)].rearrange("p (n c) -> p n c", n=NT)
                            for i in range(XBUF // 2 - 2)]
        xr = [row_bufs[i // 2][:, i % 2] for i in range(XBUF)]
        xt = [attn[:, i].rearrange("p (k r) -> p k r", k=KC) for i in range(NBUF)]
        e_exp = [z1[:, i, 0:F] for i in range(NBUF)]
        e_gu = [z2[:, i, 0:F] for i in range(NBUF)]
        e_h = [h2s[:, i, 0:F] for i in range(NBUF)]
        e_ht = [s_h[:, 0:P], s_h[:, P:N]]
        e_out = ([oT[:, i].rearrange("p j t -> p (j t)") for i in range(NT)]
                 + [osq[:, i].rearrange("p j t -> p (j t)") for i in range(OBUF - NT)])
        flat = egu[:].rearrange("p a g e k f -> p (a g e k f)")
        qkv_raw = flat[:, 0:6 * C].rearrange("p (a c) -> p a c", a=6)
        proj_raw = flat[:, 6 * C:8 * C].rearrange("p (a c) -> p a c", a=2)
        wmod_sb = flat[:, 8 * C:20 * C].rearrange("p (k n) -> p k n", k=2)
        abs_rows, sign_rows = h2s[0:B], z2[0:B]
        zeros = scm[:].rearrange("p r j q t -> p (r j q t)")[:, 0:4 * ROWW]
        y_in = [flat[:, TOPK * C * i:TOPK * C * (i + 1)] for i in range(YBUF)]
        ysum = [z1[:, i] for i in range(2)]
        ygb = [h2s[:, i] for i in range(2)]
        yout = [z2[:, i] for i in range(2)]

        ps_s = ctx.enter_context(nc.psum_tensor("ps_s", [P, 4, 512], F32))
        ps_o = ctx.enter_context(nc.psum_tensor("ps_o", [P, 512], F32))
        ps_a = ctx.enter_context(nc.psum_tensor("ps_a", [P, 512], F32))
        ps_b = ctx.enter_context(nc.psum_tensor("ps_b", [P, 512], F32))
        ps_c = ctx.enter_context(nc.psum_tensor("ps_c", [P, 512], F32))
        e_xt = [ps_a[:, 0:C], ps_b[:, 0:C]]
        e_gups = [ps_s[:, i, 0:2 * F] for i in range(NBUF)]
        e_hts = [ps_s[0:F, NBUF + i, 0:P] for i in range(NBUF)]
        e_dn = [ps_c[:, 0:C], ps_o[:, 0:C]]

        names = """
        prologue_step ln1_step ln2_step silu_step slot_step factor_step route ld_small ld_norms ld_c ld_wmod ld_qkvw
        ld_projw ld_gate ld_shared ld_xa ld_xres ld_modb0 ld_modb1 ld_gb e_free st_fill ld_y0 ld_y1
        ld_y2 ld_y3 ld_xr0 ld_xr1 ld_xr2 ld_xr3 st_mod st_zero st_rows0 st_rows1 st_put0 st_put1
        st_put2 st_put3 st_y0 st_y1 c_zero c_fill c_shape c_neg c_decay0 c_decay c_lam c_misc q_abs
        q_all q_tern q_tp q_sc q_w m_exp m_silu m_tp m_ct m_mm m_cols m_rows0 m_rows ln1_ve ln1_rstd
        z1_ready xt_done mod_cur_ready hT_ready hsq_ready q_done q_taken k_done k_taken v_done
        v_taken kt_done rr_a rr2_ready a16_ready klam_ready qlam_ready kv_done state_ready sc0 sc1
        mk0 mk1 pv0 pv1 o_taken os_done f1 f5 f_ready proj_done attn_ready x2_ready ln2_ve ln2_rstd
        z2_ready h2_mul h2_ready h2t_done h2T_ready lg_done lg_exp r1 selbf_ready w_ready
        carry_ready gu_done sg_exp sg1 sh_ready dn_done sh_gated pre_ready pos_done slots_ready xtp
        xt_taken wcol_ready gup ge_exp gh_ready htp ht_taken dnp e_evac settled put_step put_row
        rank_step y_sum y_gb y_out
        """.split() + [f"ld_quad{i}" for i in range(QUADS)]
        S = {n: sem(n) for n in names}

        block = ctx.enter_context(nc.Block())

        x_t = x.rearrange("b (i p) c -> b p i c", p=P)
        out_t = out.rearrange("b (i p) c -> (b i) p c", p=P)
        wg_v = w_gate.rearrange("(r e) (p k) f -> r p e k f", e=4, k=KC)
        wu_v = w_up.rearrange("(r e) (p k) f -> r p e k f", e=4, k=KC)
        wd_v = w_down.rearrange("(r e) f c -> r f e c", e=4)
        rows_v = rows_dram.rearrange("(r n p) c -> r p n c", p=P, n=2)
        fill_v = y_dram.rearrange("(b p r) c -> b p (r c)", b=B, p=P).rearrange("b p (a n) -> b p a n", n=C)
        y_v = y_dram.rearrange("(t p j) c -> t p (j c)", p=P, j=TOPK)

        def token_steps(eng, step):
            for s in range(3):
                step(s, s % 2, s // 2, max(s - 1, 0) // 2)
            with eng.Fori(0, (B - 4) // 2) as i:
                step(2 * i + 3, 1, i + 1, i + 1)
                step(2 * i + 4, 0, i + 2, i + 1)
            step(B - 1, 1, (B - 1) // 2, (B - 2) // 2)
            step(B, 0, B // 2, (B - 1) // 2)
            step(B + 1, 1, (B + 1) // 2, B // 2)

        def pair_steps(eng, step):
            for q in range(-1, 2):
                step(q, 0, q)
            turns = (PAIRS - 3) // RING
            with eng.Fori(0, turns) as i:
                for m in range(2, 2 + RING):
                    step(RING * i + m, i, m)
            for q in range(RING * turns + 2, PAIRS + 2):
                step(q, 0, q)

        def turn(i, m, n):
            return RING // n * i + m // n

        def before(v, start):
            return isinstance(v, int) and v < start

        def at_end(v, end):
            return isinstance(v, int) and v >= end

        @block.sync
        def _(sp):
            sp.dma_start(c_sb[:], c).then_inc(S["ld_c"], 16)
            sp.dma_start(s_row[:], spread(s, 0, P)).then_inc(S["ld_small"], 16)
            for j in range(KC):
                for a in range(HPJ):
                    sp.dma_start(s_part[HD * a:HD * a + HD, j:j + 1], spread(s[HPJ * j + a:HPJ * j + a + 1], 0, HD)
                                 ).then_inc(S["ld_small"], 16)
            sp.dma_start(xa[:], x_t[0]).then_inc(S["ld_xa"], 16)
            sp.dma_start(gate_sb[:], gate_w.rearrange("(k p) e -> p k e", p=P)).then_inc(S["ld_gate"], 16)
            sp.dma_start(ws_gu[:, :, 0], ws_gate.rearrange("(k p) f -> p k f", p=P)).then_inc(S["ld_shared"], 16)
            sp.dma_start(ws_gu[:, :, 1], ws_up.rearrange("(k p) f -> p k f", p=P)).then_inc(S["ld_shared"], 16)
            sp.dma_start(ws_d[:], ws_down).then_inc(S["ld_shared"], 16)
            sp.wait_ge(S["c_zero"], 1)
            sp.dma_start(rows_dram.rearrange("(p r) c -> p (r c)", p=P).rearrange("p (a n) -> p a n", n=4 * ROWW),
                         spread(zeros, 1, ROWS // P // 4)).then_inc(S["st_zero"], 16)
            sp.wait_ge(S["m_rows"], 1)
            sp.dma_start(mod_dram, mod_rows[:]).then_inc(S["st_mod"], 16)
            sp.wait_ge(S["st_mod"], 16)
            sp.dma_start(gb_all[:], spread(mod_dram[:, 3 * C:4 * C], 0, P)).then_inc(S["ld_gb"], 16)
            sp.wait_ge(S["q_tp"], 1)
            sp.wait_ge(S["m_mm"], 1)

            def load_quad(r, slot):
                sp.dma_start(egu[:, slot, 0], wg_v[r]).then_inc(S[f"ld_quad{slot}"], 16)
                sp.dma_start(egu[:, slot, 1], wu_v[r]).then_inc(S[f"ld_quad{slot}"], 16)
                sp.dma_start(ed[:, slot], wd_v[r]).then_inc(S[f"ld_quad{slot}"], 16)

            def step(s, par, h, hp):
                if at_end(s, B):
                    return
                if not at_end(s, B - 1):
                    sp.wait_ge(S["z1_ready"], s + 1)
                    sp.dma_start(xa[:], x_t[s + 1]).then_inc(S["ld_xa"], 16)
                seen(sp, S["h2_ready"], s - 1)
                sp.dma_start(mod_b[par][:].rearrange("p a c -> p (a c)"),
                             spread(mod_dram[s, 0:3 * C], 0, P)).then_inc(S[f"ld_modb{par}"], 16)
                if before(s, 3):
                    for r in range(QUADS * s // 3, QUADS * (s + 1) // 3):
                        load_quad(r, r)
                seen(sp, S["x2_ready"], s)
                sp.dma_start(xres[:], x_t[s]).then_inc(S["ld_xres"], 16)

            token_steps(sp, step)

            for par in range(2):
                sp.wait_ge(S[f"st_rows{par}"], 16 * B // 2 * NT * TOPK)
            def load_rows(d, buf):
                sp.dma_start(row_bufs[buf], rows_v[d]).then_inc(S[f"ld_xr{buf}"], 16)

            for d in range(XBUF // 2):
                load_rows(d, d)
            for d in range(XBUF // 2, PAIRS // 2):
                first = 2 * d - XBUF
                sp.wait_ge(S["xtp"], first + 2)
                sp.wait_ge(S["put_row"], first + 2)
                load_rows(d, d % (XBUF // 2))
                if first // 2 + QUADS < PAIRS // 2:
                    sp.wait_ge(S["dnp"], first + 2)
                    load_quad(first // 2 + QUADS, first // 2 % QUADS)

            for n in range(OBUF):
                sp.wait_ge(S[f"st_put{n}"], 16 * PAIRS // OBUF)

            def load_y(t, buf):
                sp.dma_start(y_in[buf], y_v[t]).then_inc(S[f"ld_y{buf}"], 16)

            def store_out(t, i):
                sp.wait_ge(S["y_out"], t + 1)
                sp.dma_start(out_t[t], yout[i]).then_inc(S[f"st_y{i}"], 16)

            for t in range(YBUF):
                load_y(t, t)
            with sp.Fori(0, B * NT // YBUF - 1) as i:
                for m in range(YBUF):
                    sp.wait_ge(S["y_sum"], YBUF * i + (m + 1))
                    load_y(YBUF * i + (m + YBUF), m)
                    store_out(YBUF * i + m, m % NT)
            for t in range(B * NT - YBUF, B * NT):
                store_out(t, t % NT)
            for i in range(NT):
                sp.wait_ge(S[f"st_y{i}"], 16 * B + 16)

        @block.gpsimd
        def _(pool):
            g = nc.gpsimd
            last_row = g.to_reg(ROWS - 1)
            g.memset(zeros, 0.0).then_inc(S["c_zero"], 1)
            g.memset(ident[:], 0.0)
            g.memset(upper[:], 1.0)
            g.memset(head_block[:], 1.0)
            g.memset(half_exp[:, 0], -0.5)
            g.memset(half_exp[:, 1], 0.5)
            g.memset(y_zeros[:], 0.0)
            for i in range(2):
                g.memset(v_eo[i][:], 0.0)
            g.memset(carry[:], 0.0)
            g.memset(stat_w[:], 1.0)
            g.iota(part_ix[:], pattern=[[0, 1]], base=0, channel_multiplier=1)
            g.iota(t_left[:], pattern=[[0, 1]], base=T, channel_multiplier=-1, allow_small_or_imprecise_dtypes=True)
            g.iota(trow[:], pattern=[[1, T]], base=0, channel_multiplier=0, allow_small_or_imprecise_dtypes=True)
            g.iota(slot_key[:], pattern=[[-P, PAIRS]], base=ROWS, channel_multiplier=-1,
                   allow_small_or_imprecise_dtypes=True)
            g.iota(token_key[:], pattern=[[-P * TOPK, B * NT]], base=YROWS, channel_multiplier=-TOPK,
                   allow_small_or_imprecise_dtypes=True)
            for i in range(2):
                g.memset(h2row[i][:, :, TKEY:ROWW], 0.0)
            g.iota(row_base[:], pattern=[[-SLOTS, E]], base=ROWS, channel_multiplier=0,
                   allow_small_or_imprecise_dtypes=True)
            g.iota(diff[:], pattern=[[1, T]], base=0, channel_multiplier=-1,
                   allow_small_or_imprecise_dtypes=True).then_inc(S["c_fill"], 1)
            pool.wait_ge(S["c_fill"], 1)
            g.affine_select(out=ident[:], in_=ident[:], pattern=[[-1, P]], compare_op=ALU.not_equal, fill=1.0,
                            base=0, channel_multiplier=1)
            g.affine_select(out=upper[:], in_=upper[:], pattern=[[1, P]], compare_op=ALU.is_ge, fill=0.0,
                            base=-1, channel_multiplier=-1)
            hb = head_block[:].rearrange("p (g e) -> p g e", e=HD)
            g.affine_select(out=hb, in_=hb, pattern=[[-HD, HPJ], [0, HD]], compare_op=ALU.is_ge, fill=0.0,
                            base=0, channel_multiplier=1).then_inc(S["c_shape"], 1)
            pool.wait_ge(S["c_shape"], 1)
            g.affine_select(out=hb, in_=hb, pattern=[[HD, HPJ], [0, HD]], compare_op=ALU.is_ge, fill=0.0,
                            base=HD - 1, channel_multiplier=-1).then_inc(S["c_shape"], 1)
            pool.wait_ge(S["q_abs"], 1)
            g.partition_all_reduce(abs_all[:], abs_sum[:], P, RADD).then_inc(S["q_all"], 1)
            pool.wait_ge(S["c_decay0"], 1)
            dv = decay[:].rearrange("p r j q t -> p (r j q) t")
            g.affine_select(out=dv, in_=dv, pattern=[[0, HEADS], [1, T]], compare_op=ALU.is_ge, fill=0.0,
                            base=0, channel_multiplier=-1).then_inc(S["c_decay"], 1)

            def power(out_, in_, which, ready, done, n):
                pool.wait_ge(S[ready], n)
                g.tensor_tensor(out_, in_, half_exp[:, which], ALU.pow).then_inc(S[done], 1)

            def settle(at):
                return g.tensor_tensor(pool_pad[:, at:at + 1], half_exp[:, 0, 0:1], half_exp[:, 0, 0:1], ALU.add)

            def dispatch(b, par, tile):
                if tile == 0:
                    pool.wait_ge(S["slots_ready"], b + 1)
                    pool.wait_ge(S["w_ready"], b + 1)
                    pool.wait_ge(S["h2_ready"], b + 1)
                    settle(par)
                for j in range(TOPK):
                    g.indirect_dma_start(
                        out=rows_dram, out_offset=bass.IndirectOffsetOnAxis(ap=slot_ix[par][:, tile, j:j + 1], axis=0),
                        in_=h2row[par][:, tile, :], in_offset=None, bounds_check=last_row,
                        oob_is_err=False).then_inc(S[f"st_rows{par}"], 16)

            def step(s, par, h, hp):
                if not at_end(s, B - 1):
                    power(rstd1[:], ve1[:], 0, "ln1_ve", "ln1_rstd", s + 2)
                if not before(s, 1) and not at_end(s, B + 1):
                    power(fac[:], fin[:, 4], 1, "f5", "f_ready", s)
                if not at_end(s, B):
                    pool.wait_ge(S["q_taken"], s + 1)
                    seen(pool, S["pv1"], s)
                    g.tensor_tensor(q_lam[:], qT[:, :, T:2 * T], lam_q[:], ALU.mult).then_inc(S["qlam_ready"], 1)
                if not before(s, 1) and not at_end(s, B + 1):
                    power(rstd2[:], ve2[:], 0, "ln2_ve", "ln2_rstd", s)
                    pool.wait_ge(S["z2_ready"], s)
                    pool.wait_ge(S[f"ld_modb{1 - par}"], 16 * (hp + 1))
                    g.tensor_tensor(h2s[:], z2[:], spread(mod_b[1 - par][:, 2], 1, NT), ALU.mult).then_inc(S["h2_mul"], 1)
                    pool.wait_ge(S["h2_mul"], s)
                    seen(pool, S["h2t_done"], s - 2)
                    seen(pool, S[f"st_rows{1 - par}"], 16 * NT * TOPK * hp)
                    g.tensor_tensor(h2row[1 - par][:, :, 0:C], h2s[:], spread(mod_b[1 - par][:, 1], 1, NT),
                                    ALU.add).then_inc(S["h2_ready"], 1)
                if not before(s, 2):
                    for tile in range(NT):
                        dispatch(s - 2, par, tile)

            pool.wait_ge(S["ln1_ve"], 1)
            g.tensor_tensor(rstd1[:], ve1[:], half_exp[:, 0], ALU.pow).then_inc(S["ln1_rstd"], 1)
            pool.wait_ge(S["st_zero"], 16)
            pool.wait_ge(S["c_lam"], 1)
            token_steps(pool, step)

            last_y = g.to_reg(YROWS - 1)
            pool.wait_ge(S["st_fill"], 16 * B)

            def put(q, n, w, last_n):
                pool.wait_ge(S["put_row"], q + 1)
                pool.wait_ge(S["e_evac"], q + 1)
                seen(pool, S["put_step"], q)
                settle(2).then_inc(S["put_step"], 1)
                g.indirect_dma_start(out=y_dram, out_offset=bass.IndirectOffsetOnAxis(ap=y_row[w][:, 0:1], axis=0),
                                     in_=e_out[n], in_offset=None, bounds_check=last_y,
                                     oob_is_err=False).then_inc(S[f"st_put{n}"], 16)
                if last_n is not None:
                    pool.wait_ge(S[f"st_put{(n + 1) % OBUF}"], last_n)
                    pool.sem_inc(S["e_free"], 1)

            for q in range(OBUF - 1):
                put(q, q, q, None)
            turns = (PAIRS - OBUF) // WBUF
            with pool.Fori(0, turns) as i:
                for m in range(OBUF - 1, OBUF - 1 + WBUF):
                    put(WBUF * i + m, m % OBUF, m % WBUF, 16 * (WBUF // OBUF * i + (m + 1) // OBUF))
            for q in range(WBUF * turns + OBUF - 1, PAIRS):
                put(q, q % OBUF, q % WBUF, 16 * ((q + 1) // OBUF))

            def gate(t, b, i):
                pool.wait_ge(S["y_sum"], t + 1)
                pool.wait_ge(S["settled"], 2 * t + 1)
                settle(4).then_inc(S["settled"], 1)
                g.tensor_tensor(ygb[i], ysum[i], gb_all[:, b], ALU.mult).then_inc(S["y_gb"], 1)
                pool.wait_ge(S["y_gb"], t + (NT + 1))
                pool.wait_ge(S[f"st_y{i}"], 16 * b + 16)
                pool.wait_ge(S["settled"], 2 * t + 2)
                settle(4).then_inc(S["settled"], 1)
                g.tensor_tensor(yout[i], ygb[i], pre[:, t], ALU.add).then_inc(S["y_out"], 1)

            for i in range(NT):
                pool.sem_inc(S[f"st_y{i}"], 16)
            pool.sem_inc(S["settled"], 1)
            pool.sem_inc(S["y_gb"], NT)
            with pool.Fori(0, B) as b:
                for i in range(NT):
                    gate(NT * b + i, b, i)

        @block.scalar
        def _(act):
            a = nc.scalar
            a.dma_start(qkv_raw, qkv_w.rearrange("(a p) c -> p a c", p=P)).then_inc(S["ld_qkvw"], 16)
            a.dma_start(proj_raw, proj_w.rearrange("(a p) c -> p a c", p=P)).then_inc(S["ld_projw"], 16)
            a.dma_start(wmod_sb, wmod.rearrange("(k p) n -> p k n", p=P)).then_inc(S["ld_wmod"], 16)
            for i, w in enumerate((qkv_norm_w, norm_w, proj_norm_w)):
                a.dma_start(norm_cols[:, i], w.rearrange("(k p) -> p k", p=P),
                            allow_slow_non_contiguous=True).then_inc(S["ld_norms"], 16)
            a.dma_start(bias_row[:], spread(bias, 0, P)).then_inc(S["ld_norms"], 16)

            def copy(out_, in_, scale=1.0):
                return a.activation(out_, in_, ACT.Copy, scale=scale)

            act.wait_ge(S["ld_c"], 16)
            a.activation(c_sig[:], c_sb[:], ACT.Exp, scale=-1.0).then_inc(S["m_exp"], 1)
            act.wait_ge(S["c_neg"], 1)
            for h in range(HEADS):
                last = a.activation(decay[:, h % 8 // 2, h // 8, h % 2], diff[:], ACT.Exp, scale=neg_s[:, h:h + 1])
            last.then_inc(S["c_decay0"], 1)
            for j in range(KC):
                a.activation(lam_q[:, j], trow[:], ACT.Exp, scale=neg_s_part[:, j:j + 1])
            a.activation(lam_rev[:], neg_s[:], ACT.Exp, scale=t_left[:, 0:1]).then_inc(S["c_lam"], 1)

            def norm1_out(b, par):
                act.wait_ge(S["xt_done"], b + 1)
                act.wait_ge(S["mod_cur_ready"], b + 1)
                seen(act, S["v_done"], b)
                seen(act, S["kt_done"], b)
                for j in range(KC):
                    last = a.activation(hT[:, j], ps_a[:, N * j:N * j + N], ACT.Identity,
                                        scale=mod_cur[par][:, 2 + j:3 + j], bias=mod_cur[par][:, j:j + 1])
                last.then_inc(S["hT_ready"], 1)
                for j in range(KC):
                    last = a.activation(hsq[:, j], ps_a[:, N * j:N * j + N], ACT.Square,
                                        scale=mod_cur[par][:, 2 + j:3 + j], bias=mod_cur[par][:, j:j + 1])
                last.then_inc(S["hsq_ready"], 1)

            def step(s, par, h, hp):
                has_prev = not before(s, 1) and not at_end(s, B + 1)
                cur = not at_end(s, B)
                if cur:
                    a.dma_start(fill_v[s], spread(y_zeros[:], 1, N * TOPK // P)).then_inc(S["st_fill"], 16)
                if cur:
                    act.wait_ge(S["q_done"], s + 1)
                    seen(act, S["qlam_ready"], s)
                    copy(qT[:].rearrange("p j t -> p (j t)"), ps_a[:]).then_inc(S["q_taken"], 1)
                    act.wait_ge(S["k_done"], s + 1)
                    for i in range(2):
                        last = copy(k_eo[i][:].rearrange("p j t -> p (j t)"), ps_b[:], even_odd[:, i:i + 1])
                    last.then_inc(S["k_taken"], 1)
                    act.wait_ge(S["v_done"], s + 1)
                    act.wait_ge(S["rr2_ready"], s + 1)
                    copy(v_full[:], ps_c[:, 0:C], rr2[:, 0:1])
                    for tile in range(NT):
                        vv = ps_c[:, C * tile:C * tile + C].rearrange("p (a q d) -> p a q d", q=2, d=HD)
                        for i in range(2):
                            last = copy(v_eo[i][:, tile, :, i], vv[:, :, i], rr2[:, tile:tile + 1])
                    last.then_inc(S["v_taken"], 1)
                if has_prev:
                    act.wait_ge(S["h2t_done"], s)
                    copy(h2T[:].rearrange("p j t -> p (j t)"), ps_a[:]).then_inc(S["h2T_ready"], 1)
                if cur:
                    act.wait_ge(S["pv1"], s + 1)
                    copy(oT[:].rearrange("p i j t -> p (i j t)"), ps_o[:])
                    a.activation(osq[:].rearrange("p i j t -> p (i j t)"), ps_o[:], ACT.Square).then_inc(S["o_taken"], 1)
                if has_prev:
                    act.wait_ge(S["lg_done"], s)
                    seen(act, S["r1"], s - 1)
                    a.activation(r_exp[:].rearrange("p i e -> p (i e)"), ps_b[:, 0:NT * E], ACT.Exp,
                                 scale=-1.0).then_inc(S["lg_exp"], 1)
                if not at_end(s, B - 1):
                    norm1_out(s + 1, 1 - par)
                if has_prev:
                    act.wait_ge(S["gu_done"], s)
                    seen(act, S["sg1"], s - 1)
                    a.activation(s_exp[:], ps_c[0:F, 0:N], ACT.Tanh, scale=0.5).then_inc(S["sg_exp"], 1)

            norm1_out(0, 0)
            act.wait_ge(S["c_misc"], 1)
            act.wait_ge(S["c_fill"], 1)
            token_steps(act, step)

            def pair_step(q, i, m):
                if not before(q, 0) and not at_end(q, PAIRS):
                    act.wait_ge(S["gup"], q + 1)
                    a.activation(e_exp[m % NBUF], e_gups[m % NBUF][:, 0:F], ACT.Tanh,
                                 scale=0.5).then_inc(S["ge_exp"], 1)
                if not before(q, 1) and not at_end(q, PAIRS + 1):
                    act.wait_ge(S["htp"], q)
                    copy(e_ht[(m - 1) % NBUF], e_hts[(m - 1) % NBUF]).then_inc(S["ht_taken"], 1)
                if not before(q, 2):
                    n = m % NBUF
                    act.wait_ge(S["dnp"], q - 1)
                    act.wait_ge(S["wcol_ready"], q - 1)
                    act.wait_ge(S["e_free"], q - 1 + (WBUF - OBUF))
                    copy(e_out[(m - 2) % OBUF], e_dn[n], wcol[(m - 2) % WBUF][:, 0:1]).then_inc(S["e_evac"], 1)

            act.sem_inc(S["e_free"], WBUF)
            pair_steps(act, pair_step)

        @block.vector
        def _(dve):
            v = nc.vector

            def settle():
                v.memset(pad[:], 0.0)

            def norm_stats(b, x_, bn, mv, ve, pre_):
                for i in range(NT):
                    last = v.bn_stats(bn[:, i], x_[:, i])
                last.then_inc(S[pre_ + "_step"], 1)
                dve.wait_ge(S[pre_ + "_step"], 2 * b + 1)
                settle()
                for i in range(NT):
                    last = v.bn_aggr(mv[:, i], bn[:, i])
                last.then_inc(S[pre_ + "_step"], 1)
                dve.wait_ge(S[pre_ + "_step"], 2 * b + 2)
                v.tensor_scalar(ve[:], mv[:, :, 1], EPS_LN, None, ALU.add).then_inc(S[pre_ + "_ve"], 1)

            def norm_apply(b, x_, mv, rstd, z, pre_, z_sem):
                dve.wait_ge(S[pre_ + "_rstd"], b + 1)
                for i in range(NT):
                    last = v.tensor_scalar(z[:, i], x_[:, i], mv[:, i, 0:1], rstd[:, i:i + 1], ALU.subtract, ALU.mult)
                last.then_inc(S[z_sem], 1)

            def norm1_stats(b):
                dve.wait_ge(S["ld_xa"], 16 * (b + 1))
                norm_stats(b, xa, bn1, mv1, ve1, "ln1")

            def norm1_apply(b, par):
                seen(dve, S["xt_done"], b)
                norm_apply(b, xa, mv1, rstd1, z1, "ln1", "z1_ready")
                seen(dve, S["hsq_ready"], b - 1)
                v.tensor_copy(mod_cur[par][:], mod_cols[:, :, b]).then_inc(S["mod_cur_ready"], 1)

            dve.wait_ge(S["m_exp"], 1)
            v.tensor_scalar(c_sig[:], c_sig[:], 1.0, None, ALU.add).then_inc(S["prologue_step"], 1)
            dve.wait_ge(S["prologue_step"], 1)
            v.reciprocal(c_sig[:], c_sig[:]).then_inc(S["prologue_step"], 1)
            dve.wait_ge(S["prologue_step"], 2)
            v.tensor_tensor(c_sb[:], c_sb[:], c_sig[:], ALU.mult).then_inc(S["m_silu"], 1)
            dve.wait_ge(S["ld_qkvw"], 16)
            v.tensor_reduce(abs_sum[:, 0:1], qkv_raw, mybir.AxisListType.XY, ALU.add, apply_absolute_value=True)
            dve.wait_ge(S["ld_projw"], 16)
            v.tensor_reduce(abs_sum[:, 1:2], proj_raw, mybir.AxisListType.XY, ALU.add,
                            apply_absolute_value=True).then_inc(S["q_abs"], 1)
            dve.wait_ge(S["m_tp"], 1)
            v.tensor_copy(c_cols[:].rearrange("p k b -> p (k b)"), ps_o[:, 0:KC * B]).then_inc(S["m_ct"], 1)
            dve.wait_ge(S["ld_small"], 16 * (1 + HEADS))
            dve.wait_ge(S["ld_norms"], 16 * 4)
            dve.wait_ge(S["c_fill"], 1)
            v.tensor_scalar(neg_s[:], s_row[:], -1.0, None, ALU.mult)
            v.tensor_scalar(neg_s_part[:], s_part[:], -1.0, None, ALU.mult)
            v.tensor_scalar(diff[:], diff[:], 0.0, None, ALU.max).then_inc(S["c_neg"], 1)
            v.memset(ones_bf[:], 1.0)
            v.tensor_scalar(part_bit[:], part_ix[:], HD, None, ALU.bitwise_and).then_inc(S["prologue_step"], 1)
            dve.wait_ge(S["prologue_step"], 3)
            v.tensor_scalar(even_odd[:, 1:2], part_bit[:], 1.0 / HD, None, ALU.mult)
            v.tensor_scalar(even_odd[:, 0:1], part_bit[:], -1.0 / HD, 1.0, ALU.mult, ALU.add)
            v.tensor_tensor(q_scale[:, 0], norm_cols[:, 1], norm_cols[:, 1], ALU.mult).then_inc(S["prologue_step"], 1)
            dve.wait_ge(S["prologue_step"], 4)
            v.tensor_scalar(stat_w[:, :, 1], q_scale[:, 0], EPS_F, None, ALU.add)
            v.tensor_tensor(q_scale[:, 1], norm_cols[:, 1], norm_cols[:, 2], ALU.mult).then_inc(S["c_misc"], 1)
            dve.wait_ge(S["q_all"], 1)
            v.tensor_scalar(w_mean[:, 0:1], abs_all[:, 0:1], 1.0 / (3 * C * C), 1e-5, ALU.mult, ALU.max)
            v.tensor_scalar(w_mean[:, 1:2], abs_all[:, 1:2], 1.0 / (C * C), 1e-5, ALU.mult,
                            ALU.max).then_inc(S["prologue_step"], 1)
            dve.wait_ge(S["prologue_step"], 5)
            v.reciprocal(w_inv[:], w_mean[:]).then_inc(S["prologue_step"], 1)
            dve.wait_ge(S["c_misc"], 1)
            v.tensor_scalar(q_scale[:, 0], norm_cols[:, 0], w_mean[:, 0:1], None, ALU.mult)
            v.tensor_scalar(q_scale[:, 1], q_scale[:, 1], w_mean[:, 1:2], None, ALU.mult).then_inc(S["q_sc"], 1)
            dve.wait_ge(S["prologue_step"], 6)
            v.tensor_scalar(qkv_raw, qkv_raw, w_inv[:, 0:1], MAGIC, ALU.mult, ALU.add)
            v.tensor_scalar(proj_raw, proj_raw, w_inv[:, 1:2], MAGIC, ALU.mult, ALU.add).then_inc(S["prologue_step"], 1)
            dve.wait_ge(S["prologue_step"], 7)
            v.tensor_scalar(qkv_raw, qkv_raw, MAGIC, 1.0, ALU.subtract, ALU.min)
            v.tensor_scalar(proj_raw, proj_raw, MAGIC, 1.0, ALU.subtract, ALU.min).then_inc(S["prologue_step"], 1)
            dve.wait_ge(S["prologue_step"], 8)
            v.tensor_scalar(qkv_raw, qkv_raw, -1.0, None, ALU.max)
            v.tensor_scalar(proj_raw, proj_raw, -1.0, None, ALU.max).then_inc(S["q_tern"], 1)
            norm1_stats(0)
            dve.wait_ge(S["m_mm"], 1)
            mc = mod_cols[:].rearrange("p m b -> p (m b)")
            v.tensor_copy(mc[:, 0:2 * B], ps_o[:, 64:64 + 2 * B])
            v.tensor_scalar(mc[:, 2 * B:4 * B], ps_o[:, 64 + 2 * B:64 + 4 * B], 1.0, None, ALU.add).then_inc(S["m_cols"], 1)
            dve.wait_ge(S["m_cols"], 1)
            norm1_apply(0, 0)
            dve.wait_ge(S["q_tp"], 1)
            dve.wait_ge(S["q_sc"], 1)
            for k in range(KC):
                v.tensor_scalar(w_qkv[:, k, 0:512], ps_s[:, k], q_scale[:, 0, k:k + 1], None, ALU.mult)
                v.tensor_scalar(w_qkv[:, k, 512:768], ps_s[:, 2, C * k:C * k + C], q_scale[:, 0, k:k + 1], None, ALU.mult)
                last = v.tensor_scalar(w_proj[:, k], ps_s[:, 3, C * k:C * k + C], q_scale[:, 1, k:k + 1], None, ALU.mult)
            last.then_inc(S["q_w"], 1)
            v.tensor_copy(mod_rows[:, 0:2 * C], ps_b[0:B, :])
            v.tensor_copy(mod_rows[:, 2 * C:4 * C], ps_c[0:B, :]).then_inc(S["m_rows0"], 1)
            dve.wait_ge(S["m_rows0"], 1)
            gates = mod_rows[:].rearrange("p (m c) -> p m c", m=4)[:, 0:4:3]
            v.tensor_scalar(mod_rows[:, 2 * C:3 * C], mod_rows[:, 2 * C:3 * C], 1.0, None, ALU.add)
            v.tensor_scalar(sign_rows[:], gates, 0.0, 2.0, ALU.is_ge, ALU.mult).then_inc(S["prologue_step"], 1)
            v.scalar_tensor_tensor(out=abs_rows[:], in0=gates, scalar=-1.0, in1=gates, op0=ALU.mult,
                                   op1=ALU.max).then_inc(S["prologue_step"], 1)
            dve.wait_ge(S["prologue_step"], 9)
            v.tensor_scalar(sign_rows[:], sign_rows[:], 1.0, None, ALU.subtract).then_inc(S["prologue_step"], 1)
            dve.wait_ge(S["prologue_step"], 10)
            dve.wait_ge(S["prologue_step"], 11)
            v.scalar_tensor_tensor(out=gates, in0=abs_rows[:], scalar=0.25, in1=sign_rows[:], op0=ALU.max,
                                   op1=ALU.mult).then_inc(S["m_rows"], 1)
            def rms(b, par):
                dve.wait_ge(S["kt_done"], b + 1)
                v.tensor_scalar(rr_t[:], ps_a[:, C:C + NT], 1.0 / C, EPS_F, ALU.mult, ALU.add).then_inc(S["rr_a"], 1)
                dve.wait_ge(S["rr_a"], b + 1)
                seen(dve, S["v_taken"], b)
                v.reciprocal(rr2[:], rr_t[:]).then_inc(S["rr2_ready"], 1)
                dve.wait_ge(S["kt_done"], b + 1)
                seen(dve, S["kv_done"], b)
                v.tensor_tensor(k_lam[:].rearrange("p (h d) -> p h d", d=HD),
                                ps_a[:, 0:C].rearrange("p (h d) -> p h d", d=HD), spread(lam_rev[:], 2, HD),
                                ALU.mult).then_inc(S["klam_ready"], 1)
                dve.wait_ge(S["rr2_ready"], b + 1)
                v.tensor_scalar(a16[par][:], rr2[:], 1.0 / HD, None, ALU.mult).then_inc(S["a16_ready"], 1)
            def state_block(b):
                dve.wait_ge(S["kv_done"], b + 1)
                seen(dve, S["pv1"], b)
                v.tensor_tensor(state[:], ps_b[:, 0:KC * P].rearrange("p (j m) -> p j m", j=KC),
                                spread(head_block[:], 1, KC), ALU.mult).then_inc(S["state_ready"], 1)

            def out_norms(b, par):
                dve.wait_ge(S["os_done"], b + 1)
                dve.wait_ge(S["a16_ready"], b + 1)
                v.scalar_tensor_tensor(out=fin[:, 1], in0=ps_o[:, 0:NT], scalar=1.0 / C, in1=a16[par][:],
                                       op0=ALU.mult, op1=ALU.mult).then_inc(S["f1"], 1)
                dve.wait_ge(S["f1"], b + 1)
                v.tensor_scalar(fin[:, 2], fin[:, 1], EPS_F * EPS_O, None, ALU.add).then_inc(S["factor_step"], 1)
                dve.wait_ge(S["factor_step"], 2 * b + 1)
                v.reciprocal(fin[:, 3], fin[:, 2]).then_inc(S["factor_step"], 1)
                dve.wait_ge(S["factor_step"], 2 * b + 2)
                v.tensor_tensor(fin[:, 4], fin[:, 3], a16[par][:], ALU.mult).then_inc(S["f5"], 1)

            def residual(b, par, hb):
                dve.wait_ge(S["f_ready"], b + 1)
                dve.wait_ge(S["proj_done"], b + 1)
                dve.wait_ge(S[f"ld_modb{par}"], 16 * (hb + 1))
                for i in range(NT):
                    last = v.scalar_tensor_tensor(out=attn[:, i], in0=ps_c[:, C * i:C * i + C], scalar=fac[:, i:i + 1],
                                                  in1=mod_b[par][:, 0], op0=ALU.mult, op1=ALU.mult)
                last.then_inc(S["attn_ready"], 1)
                dve.wait_ge(S["attn_ready"], b + 1)
                dve.wait_ge(S["ld_xres"], 16 * (b + 1))
                v.tensor_tensor(x2[par][:], attn[:], xres[:], ALU.add).then_inc(S["x2_ready"], 1)
                dve.wait_ge(S["x2_ready"], b + 1)
                norm_stats(b, x2[par], bn2, mv2, ve2, "ln2")

            def mask(b, tile):
                dve.wait_ge(S[f"sc{tile}"], b + 1)
                if tile == 0:
                    seen(dve, S["pv1"], b)
                else:
                    dve.wait_ge(S["pv0"], b + 1)
                v.tensor_tensor(scm[:].rearrange("p r j q t -> p (r j q t)"), ps_s[:].rearrange("p r n -> p (r n)"),
                                decay[:].rearrange("p r j q t -> p (r j q t)"), ALU.mult).then_inc(S[f"mk{tile}"], 1)

            def router_scores(b):
                dve.wait_ge(S["lg_exp"], b + 1)
                v.tensor_scalar(r_den[:], r_exp[:], 1.0, None, ALU.add).then_inc(S["r1"], 1)
                dve.wait_ge(S["r1"], b + 1)
                v.reciprocal(r_sig[:], r_den[:]).then_inc(S["route"], 1)
                dve.wait_ge(S["route"], ROUTE_STEPS * b + 1)
                v.tensor_tensor(r_sc[:], r_sig[:], spread(bias_row[:], 1, NT), ALU.add).then_inc(S["route"], 1)
                dve.wait_ge(S["route"], ROUTE_STEPS * b + 2)
                v.memset(g_sum[:, :, G:2 * G], OUT)
                for i in range(NT):
                    for g_ in range(G):
                        last = v.max(g_top[:, i * G + g_], r_sc[:, i, EG * g_:EG * g_ + EG])
                last.then_inc(S["route"], 1)

            def router_choice(b, par):
                dve.wait_ge(S["route"], ROUTE_STEPS * b + 3)
                v.tensor_tensor(g_sum[:, :, 0:G], g_top[:, :, 0].rearrange("p (i g) -> p i g", i=NT),
                                g_top[:, :, 1].rearrange("p (i g) -> p i g", i=NT), ALU.add).then_inc(S["route"], 1)
                dve.wait_ge(S["route"], ROUTE_STEPS * b + 4)
                settle()
                for i in range(NT):
                    last = v.max(g_best[:, i], g_sum[:, i])
                last.then_inc(S["route"], 1)
                dve.wait_ge(S["route"], ROUTE_STEPS * b + 5)
                v.memset(g_best[:, :, KG:8], OUT).then_inc(S["route"], 1)
                dve.wait_ge(S["route"], ROUTE_STEPS * b + 6)
                settle()
                for i in range(NT):
                    last = v.match_replace(g_rep[:, i], g_best[:, i], g_sum[:, i], PICK)
                last.then_inc(S["route"], 1)
                dve.wait_ge(S["route"], ROUTE_STEPS * b + 7)
                v.tensor_scalar(g_pick[:], g_rep[:, :, 0:G], 1.5 * OUT, None, ALU.is_lt).then_inc(S["route"], 1)
                dve.wait_ge(S["route"], ROUTE_STEPS * b + 8)
                v.tensor_scalar(g_pen[:], g_pick[:], -OUT, OUT, ALU.mult, ALU.add).then_inc(S["route"], 1)
                dve.wait_ge(S["route"], ROUTE_STEPS * b + 9)
                r4 = r_sc[:].rearrange("p i (g e) -> p i g e", g=G)
                v.tensor_tensor(e_val[:].rearrange("p i (g e) -> p i g e", g=G), r4, spread(g_pen[:], 3, EG),
                                ALU.add).then_inc(S["route"], 1)
                dve.wait_ge(S["route"], ROUTE_STEPS * b + 10)
                settle()
                for i in range(NT):
                    last = v.max(e_best[:, i], e_val[:, i])
                last.then_inc(S["route"], 1)
                dve.wait_ge(S["route"], ROUTE_STEPS * b + 11)
                v.memset(e_best[:, :, TOPK:8], OUT).then_inc(S["route"], 1)
                dve.wait_ge(S["route"], ROUTE_STEPS * b + 12)
                settle()
                for i in range(NT):
                    last = v.match_replace(e_rep[:, i], e_best[:, i], e_val[:, i], PICK)
                last.then_inc(S["route"], 1)
                dve.wait_ge(S["route"], ROUTE_STEPS * b + 13)
                v.scalar_tensor_tensor(out=sel[:].rearrange("p i (g e) -> p i g e", g=G),
                                       in0=e_rep[:].rearrange("p i (g e) -> p i g e", g=G), scalar=1.5 * OUT,
                                       in1=spread(g_pick[:], 3, EG), op0=ALU.is_lt, op1=ALU.mult
                                       ).then_inc(S["route"], 1)
                dve.wait_ge(S["route"], ROUTE_STEPS * b + 14)
                seen(dve, S["pos_done"], b)
                v.tensor_copy(sel_bf[:], sel[:]).then_inc(S["selbf_ready"], 1)
                v.tensor_tensor(w_raw[:], sel[:], r_sig[:], ALU.mult).then_inc(S["route"], 1)
                dve.wait_ge(S["selbf_ready"], b + 1)
                v.tensor_tensor(carry[:, 1], carry[:, 0], sel_bf[:, 0], ALU.add).then_inc(S["carry_ready"], 1)
                dve.wait_ge(S["route"], ROUTE_STEPS * b + 15)
                v.tensor_reduce(w_sum[:], w_raw[:], AX_X, ALU.add).then_inc(S["route"], 1)
                dve.wait_ge(S["route"], ROUTE_STEPS * b + 16)
                v.reciprocal(w_rec[:], w_sum[:]).then_inc(S["route"], 1)
                dve.wait_ge(S["route"], ROUTE_STEPS * b + 17)
                dve.wait_ge(S["h2_ready"], b + 1)
                for i in range(NT):
                    last = v.tensor_scalar(h2row[par][:, i, C:KEYS], w_raw[:, i], w_rec[:, i:i + 1], ROUTE_SCALE,
                                           ALU.mult, ALU.mult)
                last.then_inc(S["w_ready"], 1)

            def shared(b):
                dve.wait_ge(S["sg_exp"], b + 1)
                v.scalar_tensor_tensor(out=s_gu[:], in0=s_exp[:], scalar=1.0, in1=ps_c[0:F, 0:N], op0=ALU.add,
                                       op1=ALU.mult).then_inc(S["sg1"], 1)
                dve.wait_ge(S["sg1"], b + 1)
                v.scalar_tensor_tensor(out=s_h[:], in0=s_gu[:], scalar=0.5, in1=ps_c[0:F, N:2 * N], op0=ALU.mult,
                                       op1=ALU.mult).then_inc(S["sh_ready"], 1)

            def shared_out(b, par):
                dve.wait_ge(S["dn_done"], b + 1)
                dve.wait_ge(S["ld_gb"], 16)
                v.tensor_tensor(sh_g[:], ps_b[:].rearrange("p (i c) -> p i c", i=NT), spread(gb_all[:, b], 1, NT),
                                ALU.mult).then_inc(S["sh_gated"], 1)
                dve.wait_ge(S["sh_gated"], b + 1)
                v.tensor_tensor(pre[:, bass.ds(NT * b, NT)], sh_g[:], x2[par][:], ALU.add).then_inc(S["pre_ready"], 1)

            def slots(b, par):
                dve.wait_ge(S["pos_done"], b + 1)
                pos = ps_c[:, 0:NT * E].rearrange("p (i e) -> p i e", i=NT)
                v.scalar_tensor_tensor(out=keep[:], in0=pos, scalar=float(CAP), in1=sel[:], op0=ALU.is_lt,
                                       op1=ALU.mult)
                v.tensor_tensor(row_key[:], spread(row_base[:], 1, NT), pos, ALU.subtract).then_inc(S["slot_step"], 1)
                v.tensor_tensor(carry[:, 0], carry[:, 1], sel_bf[:, 1], ALU.add)
                dve.wait_ge(S["slot_step"], 3 * b + 1)
                v.tensor_tensor(key[:], keep[:], row_key[:], ALU.mult).then_inc(S["slot_step"], 1)
                dve.wait_ge(S["slot_step"], 3 * b + 2)
                settle()
                for i in range(NT):
                    last = v.max(h2row[par][:, i, KEYS:TKEY], key[:, i])
                last.then_inc(S["slot_step"], 1)
                dve.wait_ge(S["slot_step"], 3 * b + 3)
                v.tensor_copy(h2row[par][:, :, TKEY], token_key[:, bass.ds(NT * b, NT)])
                v.tensor_scalar(slot_ix[par][:], h2row[par][:, :, KEYS:TKEY], -1.0, float(ROWS), ALU.mult,
                                ALU.add).then_inc(S["slots_ready"], 1)

            def step(s, par, h, hp):
                cur, nxt = not at_end(s, B), not at_end(s, B - 1)
                has_prev = not before(s, 1) and not at_end(s, B + 1)
                has_two = not before(s, 2)
                if has_two:
                    router_scores(s - 2)
                if nxt:
                    norm1_stats(s + 1)
                if has_two:
                    shared(s - 2)
                if has_prev:
                    out_norms(s - 1, 1 - par)
                if cur:
                    rms(s, par)
                if has_two:
                    router_choice(s - 2, par)
                if cur:
                    mask(s, 0)
                if cur:
                    state_block(s)
                if has_prev:
                    residual(s - 1, 1 - par, hp)
                if nxt:
                    norm1_apply(s + 1, 1 - par)
                if has_prev:
                    seen(dve, S["h2_mul"], s - 1)
                    norm_apply(s - 1, x2[1 - par], mv2, rstd2, z2, "ln2", "z2_ready")
                if cur:
                    mask(s, 1)
                if has_two:
                    slots(s - 2, par)
                    shared_out(s - 2, par)

            dve.wait_ge(S["c_lam"], 1)
            dve.wait_ge(S["c_shape"], 2)
            dve.wait_ge(S["c_decay"], 1)
            dve.wait_ge(S["st_zero"], 16)
            token_steps(dve, step)

            def pair_step(q, i, m):
                if not at_end(q, PAIRS - 1):
                    n = (m + 1) % NBUF
                    dve.wait_ge(S["xtp"], q + 2)
                    seen(dve, S["gup"], q)
                    v.tensor_copy(xt[n].rearrange("p k r -> p (k r)"), e_xt[n]).then_inc(S["xt_taken"], 1)
                if not before(q, 0) and not at_end(q, PAIRS):
                    n = m % NBUF
                    dve.wait_ge(S["ge_exp"], q + 1)
                    v.scalar_tensor_tensor(out=e_gu[n], in0=e_exp[n], scalar=1.0, in1=e_gups[n][:, 0:F],
                                           op0=ALU.add, op1=ALU.mult).then_inc(S["silu_step"], 1)
                    dve.wait_ge(S["silu_step"], q + 1)
                    v.scalar_tensor_tensor(out=e_h[n], in0=e_gu[n], scalar=0.5, in1=e_gups[n][:, F:2 * F],
                                           op0=ALU.mult, op1=ALU.mult).then_inc(S["gh_ready"], 1)
                if not at_end(q, PAIRS - 1):
                    x, w = (m + 1) % XBUF, (m + 1) % WBUF
                    dve.wait_ge(S["e_free"], q + 2)
                    for half in range(2):
                        rows = slice(SLOTS * half, SLOTS * half + SLOTS)
                        e = 2 * q + (2 + half)
                        v.tensor_copy(wcol[w][rows], xr[x][rows, bass.ds(C + e, 1)])
                    v.tensor_tensor(larger[:], xr[x][:, KEYS:TKEY], spread(slot_key[:, q + 1], 1, 8),
                                    ALU.is_gt).then_inc(S["wcol_ready"], 1)
                    dve.wait_ge(S["wcol_ready"], q + 2)
                    v.tensor_reduce(rank[:], larger[:], AX_X, ALU.add).then_inc(S["rank_step"], 1)
                    dve.wait_ge(S["rank_step"], q + 2)
                    v.scalar_tensor_tensor(out=y_row[w][:], in0=rank[:], scalar=float(YROWS),
                                           in1=xr[x][:, TKEY:TKEY + 1], op0=ALU.add,
                                           op1=ALU.subtract).then_inc(S["put_row"], 1)

            pair_steps(dve, pair_step)

            with dve.Fori(0, B * NT // YBUF) as i:
                for m in range(YBUF):
                    dve.wait_ge(S[f"ld_y{m}"], 16 * i + 16)
                    dve.wait_ge(S["y_gb"], YBUF * i + (m + 1))
                    v.tensor_reduce(ysum[m % NT], y_in[m].rearrange("p (j c) -> p c j", c=C), AX_X,
                                    ALU.add).then_inc(S["y_sum"], 1)

        @block.tensor
        def _(pe):
            mm = nc.tensor

            pe.wait_ge(S["m_silu"], 1)
            pe.wait_ge(S["c_shape"], 2)
            for k in range(KC):
                last = mm.transpose(ps_o[:, B * k:B * k + B], c_sb[:, P * k:P * k + P], ident[0:B, 0:B])
            last.then_inc(S["m_tp"], 1)
            pe.wait_ge(S["m_ct"], 1)
            pe.wait_ge(S["ld_wmod"], 16)
            for i in range(4):
                for k in range(KC):
                    mm.matmul(ps_o[:, 64 + B * i:64 + B * i + B], wmod_sb[:, k, P * i:P * i + P], c_cols[:, k],
                             start=(k == 0), stop=(k == KC - 1))
            for i, ps in enumerate((ps_b, ps_c)):
                for k in range(KC):
                    last = mm.matmul(ps[0:B, :], c_cols[:, k], wmod_sb[:, k, 512 * (i + 1):512 * (i + 2)],
                                    start=(k == 0), stop=(k == KC - 1))
            last.then_inc(S["m_mm"], 1)

            def norm1_transpose(b):
                pe.wait_ge(S["z1_ready"], b + 1)
                seen(pe, S["h2T_ready"], b - 1)
                seen(pe, S["rr_a"], b)
                seen(pe, S["klam_ready"], b)
                for j in range(KC):
                    for i in range(NT):
                        last = mm.transpose(ps_a[:, N * j + T * i:N * j + T * i + T], z1[:, i, P * j:P * j + P], ident[:])
                last.then_inc(S["xt_done"], 1)

            pe.wait_ge(S["q_tern"], 1)
            for k in range(KC):
                for o in range(4):
                    mm.transpose(ps_s[:, k, P * o:P * o + P], qkv_raw[:, o, P * k:P * k + P], ident[:])
                for o in range(2):
                    mm.transpose(ps_s[:, 2, C * k + P * o:C * k + P * o + P], qkv_raw[:, 4 + o, P * k:P * k + P], ident[:])
                for o in range(2):
                    last = mm.transpose(ps_s[:, 3, C * k + P * o:C * k + P * o + P], proj_raw[:, o, P * k:P * k + P], ident[:])
            last.then_inc(S["q_tp"], 1)
            norm1_transpose(0)
            pe.wait_ge(S["q_w"], 1)
            pe.wait_ge(S["m_rows0"], 1)
            pe.wait_ge(S["m_cols"], 1)
            pe.wait_ge(S["c_misc"], 1)
            pe.wait_ge(S["ld_gate"], 16)
            pe.wait_ge(S["ld_shared"], 48)

            def project_qkv(b):
                pe.wait_ge(S["hT_ready"], b + 1)
                pe.wait_ge(S["hsq_ready"], b + 1)
                for j in range(KC):
                    for k in range(KC):
                        last = mm.matmul(ps_a[:, N * j:N * j + N], w_qkv[:, k, P * j:P * j + P], hT[:, k],
                                        start=(k == 0), stop=(k == KC - 1))
                last.then_inc(S["q_done"], 1)
                seen(pe, S["lg_exp"], b - 1)
                seen(pe, S["state_ready"], b)
                for j in range(KC):
                    for k in range(KC):
                        last = mm.matmul(ps_b[:, N * j:N * j + N], w_qkv[:, k, C + P * j:C + P * j + P], hT[:, k],
                                        start=(k == 0), stop=(k == KC - 1))
                last.then_inc(S["k_done"], 1)
                pe.wait_ge(S["q_taken"], b + 1)
                for i in range(NT):
                    for k in range(KC):
                        last = mm.matmul(ps_a[:, C + i:C + i + 1], hsq[:, k, T * i:T * i + T], stat_w[:, 0, 0:1],
                                        start=(k == 0), stop=(k == KC - 1))
                for k in range(KC):
                    last = mm.matmul(ps_a[:, 0:C], hT[:, k, 0:T], w_qkv[:, k, C:2 * C], start=(k == 0), stop=(k == KC - 1))
                last.then_inc(S["kt_done"], 1)
                seen(pe, S["sh_ready"], b - 1)
                seen(pe, S["v_taken"], b)
                for i in range(NT):
                    for k in range(KC):
                        last = mm.matmul(ps_c[:, C * i:C * i + C], hT[:, k, T * i:T * i + T], w_qkv[:, k, 2 * C:3 * C],
                                        start=(k == 0), stop=(k == KC - 1))
                last.then_inc(S["v_done"], 1)

            def first_state(b):
                pe.wait_ge(S["klam_ready"], b + 1)
                pe.wait_ge(S["v_taken"], b + 1)
                pe.wait_ge(S["k_taken"], b + 1)
                for j in range(KC):
                    last = mm.matmul(ps_b[:, P * j:P * j + P], k_lam[:, P * j:P * j + P], v_full[:, P * j:P * j + P],
                                    start=True, stop=True)
                last.then_inc(S["kv_done"], 1)

            def out_stats(b):
                pe.wait_ge(S["o_taken"], b + 1)
                for i in range(NT):
                    for k in range(KC):
                        last = mm.matmul(ps_o[:, i:i + 1], osq[:, i, k], stat_w[:, k, 1:2],
                                        start=(k == 0), stop=(k == KC - 1))
                last.then_inc(S["os_done"], 1)

            def project_out(b):
                seen(pe, S["sh_ready"], b)
                seen(pe, S["v_taken"], min(b + 2, B) if isinstance(b, int) else b + 2)
                for i in range(NT):
                    for k in range(KC):
                        last = mm.matmul(ps_c[:, C * i:C * i + C], oT[:, i, k], w_proj[:, k],
                                        start=(k == 0), stop=(k == KC - 1))
                last.then_inc(S["proj_done"], 1)

            def scores(b, tile):
                if tile == 0:
                    pe.wait_ge(S["k_taken"], b + 1)
                    pe.wait_ge(S["q_taken"], b + 1)
                    seen(pe, S["mk1"], b)
                else:
                    pe.wait_ge(S["mk0"], b + 1)
                ts = slice(T * tile, T * tile + T)
                for j in range(KC):
                    for q in range(2):
                        col = T * (2 * j + q)
                        for r in range(4):
                            last = mm.matmul(ps_s[:, r, col:col + T], k_eo[q][32 * r:32 * r + 32, j, ts],
                                             qT[32 * r:32 * r + 32, j, ts], start=True, stop=True)
                last.then_inc(S[f"sc{tile}"], 1)

            def values(b, tile):
                if tile == 0:
                    seen(pe, S["f1"], b)
                    pe.wait_ge(S["v_taken"], b + 1)
                else:
                    pe.wait_ge(S["state_ready"], b + 1)
                    pe.wait_ge(S["qlam_ready"], b + 1)
                pe.wait_ge(S[f"mk{tile}"], b + 1)
                for j in range(KC):
                    dst = ps_o[:, 256 * tile + T * j:256 * tile + T * j + T]
                    if tile:
                        mm.matmul(dst, state[:, j], q_lam[:, j], start=True, stop=False, skip_group_check=True)
                    for q in range(2):
                        for r in range(4):
                            vq = v_eo[q][:, tile, 4 * j + r].rearrange("p q d -> p (q d)")
                            last = mm.matmul(dst[32 * r:32 * r + 32], vq, scm[:, r, j, q],
                                             start=(q == 0 and not tile), stop=(q == 1), skip_group_check=True)
                last.then_inc(S[f"pv{tile}"], 1)

            def norm2_transpose(b, par):
                pe.wait_ge(S["h2_ready"], b + 1)
                for j in range(KC):
                    for i in range(NT):
                        last = mm.transpose(ps_a[:, N * j + T * i:N * j + T * i + T], h2row[par][:, i, P * j:P * j + P],
                                           ident[:])
                last.then_inc(S["h2t_done"], 1)

            def logits(b):
                pe.wait_ge(S["h2T_ready"], b + 1)
                seen(pe, S["state_ready"], min(b + 2, B) if isinstance(b, int) else b + 2)
                seen(pe, S["sh_gated"], b)
                for i in range(NT):
                    for k in range(KC):
                        last = mm.matmul(ps_b[:, E * i:E * i + E], h2T[:, k, T * i:T * i + T], gate_sb[:, k],
                                        start=(k == 0), stop=(k == KC - 1))
                last.then_inc(S["lg_done"], 1)

            def gate_up(b):
                pe.wait_ge(S["attn_ready"], b + 1)
                seen(pe, S["slots_ready"], b)
                for g_ in range(2):
                    for k in range(KC):
                        last = mm.matmul(ps_c[0:F, N * g_:N * g_ + N], ws_gu[:, k, g_], h2T[:, k],
                                        start=(k == 0), stop=(k == KC - 1))
                last.then_inc(S["gu_done"], 1)

            def shared_down(b):
                pe.wait_ge(S["sh_ready"], b + 1)
                pe.wait_ge(S["lg_exp"], b + 1)
                seen(pe, S["state_ready"], min(b + 3, B) if isinstance(b, int) else b + 3)
                for i in range(NT):
                    last = mm.matmul(ps_b[:, C * i:C * i + C], s_h[:, T * i:T * i + T], ws_d[:], start=True, stop=True)
                last.then_inc(S["dn_done"], 1)

            def positions(b):
                seen(pe, S["attn_ready"], min(b + 2, B) if isinstance(b, int) else b + 2)
                pe.wait_ge(S["selbf_ready"], b + 1)
                pe.wait_ge(S["carry_ready"], b + 1)
                for i in range(NT):
                    mm.matmul(ps_c[:, E * i:E * i + E], upper[:], sel_bf[:, i], start=True, stop=False)
                    last = mm.matmul(ps_c[:, E * i:E * i + E], ones_bf[:], carry[:, i], start=False, stop=True)
                last.then_inc(S["pos_done"], 1)

            def step(s, par, h, hp):
                cur, nxt = not at_end(s, B), not at_end(s, B - 1)
                has_prev = not before(s, 1) and not at_end(s, B + 1)
                has_two = not before(s, 2)
                if has_prev:
                    out_stats(s - 1)
                if cur:
                    project_qkv(s)
                    scores(s, 0)
                if has_prev:
                    project_out(s - 1)
                if cur:
                    first_state(s)
                    values(s, 0)
                    scores(s, 1)
                if has_two:
                    shared_down(s - 2)
                    positions(s - 2)
                if has_prev:
                    norm2_transpose(s - 1, 1 - par)
                if cur:
                    values(s, 1)
                if has_prev:
                    logits(s - 1)
                if nxt:
                    norm1_transpose(s + 1)
                if has_prev:
                    gate_up(s - 1)

            token_steps(pe, step)

            pe.wait_ge(S["pre_ready"], B)
            pe.wait_ge(S["slots_ready"], B)

            def pair_step(q, i, m):
                if not at_end(q, PAIRS - 1):
                    n = (m + 1) % NBUF
                    n, x = (m + 1) % NBUF, (m + 1) % XBUF
                    if x % 2 == 0:
                        pe.wait_ge(S[f"ld_xr{x // 2}"], 16 * (turn(i, m + 1, XBUF) + 1))
                    seen(pe, S["xt_taken"], q)
                    for k in range(KC):
                        last = mm.transpose(e_xt[n][:, P * k:P * k + P], xr[x][:, k:C:KC], ident[:])
                    last.then_inc(S["xtp"], 1)
                if not before(q, 0) and not at_end(q, PAIRS):
                    n, slot = m % NBUF, m % RING
                    pe.wait_ge(S["xt_taken"], q + 1)
                    if slot % 2 == 0:
                        pe.wait_ge(S[f"ld_quad{slot // 2}"], 48 * (turn(i, m, RING) + 1))
                    for half in range(2):
                        rows = slice(SLOTS * half, SLOTS * half + SLOTS)
                        for k in range(KC):
                            last = mm.matmul(e_gups[n][rows].rearrange("p (g f) -> p g f", f=F), xt[n][:, k, rows],
                                             egu[:, slot // 2, :, 2 * (slot % 2) + half, k],
                                             start=(k == 0), stop=(k == KC - 1))
                    last.then_inc(S["gup"], 1)
                if not before(q, 1) and not at_end(q, PAIRS + 1):
                    n = (m - 1) % NBUF
                    pe.wait_ge(S["gh_ready"], q)
                    mm.transpose(e_hts[n], e_h[n], ident[:]).then_inc(S["htp"], 1)
                if not before(q, 2):
                    n, slot = m % NBUF, (m - 2) % RING
                    pe.wait_ge(S["ht_taken"], q - 1)
                    for half in range(2):
                        rows = slice(SLOTS * half, SLOTS * half + SLOTS)
                        last = mm.matmul(e_dn[n][rows, :], e_ht[n][:, rows], ed[:, slot // 2, 2 * (slot % 2) + half], start=True, stop=True)
                    last.then_inc(S["dnp"], 1)

            pair_steps(pe, pair_step)


_INS = ["L0_attn_x", "L0_attn_qkv_w", "L0_attn_qkv_norm_w", "L0_attn_proj_w", "L0_attn_proj_norm_w",
        "L0_attn_norm_w", "L0_attn_s", "L0_ffn_gate_w", "L0_ffn_bias", "L0_ffn_w_gate", "L0_ffn_w_up",
        "L0_ffn_w_down", "L0_ffn_ws_gate", "L0_ffn_ws_up", "L0_ffn_ws_down", "L0_c", "L0_wmod"]


def kernel(**inputs):
    import numpy as np
    import concourse.bacc as bacc
    from concourse.bass_utils import run_bass_kernel_spmd

    nc = bacc.Bacc("TRN2", target_bir_lowering=False, num_devices=1)
    arrays, args = {}, []
    for name in _INS:
        a = np.ascontiguousarray(inputs[name])
        arrays[f"in_{name}"] = a
        args.append(nc.dram_tensor(f"in_{name}", a.shape, mybir.dt.from_np(a.dtype), kind="ExternalInput").ap())
    args.append(nc.dram_tensor("out", (B, N, C), F32, kind="ExternalOutput").ap())
    adaln_attention_moe(nc, *args)
    r = run_bass_kernel_spmd(nc, [arrays], core_ids=[0])
    return r.results[0]["out"]
```
